# Optimizing a Trainium2 kernel written in Bass

```python
import numpy as np
import jax
import jax.numpy as jnp

def _softmax(x, axis=-1):
    return jax.nn.softmax(x, axis=axis)

def _gelu(x):
    return jax.nn.gelu(x, approximate=True)

def _silu(x):
    return jax.nn.silu(x)

def _sigmoid(x):
    return jax.nn.sigmoid(x)

def _layernorm(x, axis=-1, eps=1e-05):
    m = jnp.mean(x, axis=axis, keepdims=True)
    v = jnp.var(x, axis=axis, keepdims=True)
    return (x - m) / jnp.sqrt(v + eps)

def _scatter_add(tgt, idx, src, axis=0):
    return tgt.at[idx].add(src)

def _segment_sum(src, seg, n):
    return jax.ops.segment_sum(src, seg, n)
kernel_name = 'mk_flamingo_gated_d1_seqx_r4_858551'

def setup_inputs(seed: int=0):
    np.random.seed(seed)
    _w = jnp.asarray

    def _rec_inputs():
        import jax
        import jax.numpy as jnp
        _rk = jax.random.key(seed)
        x = 0.0002417 + 0.9998 * jax.random.normal(jax.random.fold_in(_rk, 1), (4, 512, 256), jnp.float32)
        _lenS = 512 - jax.random.randint(jax.random.fold_in(_rk, 7), (4,), 0, max(1, 512 // 4) + 1, jnp.int32)
        _lenS2 = 512 - jax.random.randint(jax.random.fold_in(_rk, 8), (4,), 0, max(1, 512 // 4) + 1, jnp.int32)
        _ctx_1024P = jax.random.normal(jax.random.fold_in(_rk, 11), (4, 16, 256), jnp.float32)
        _ctx_1024c = jax.random.dirichlet(jax.random.fold_in(_rk, 511), 0.3 * jnp.ones((16,), jnp.float32), (4, 512))
        _ctx_1024t = jnp.einsum('bsk,bkd->bsd', _ctx_1024c, _ctx_1024P)
        _ctx_1024t = _ctx_1024t * jax.lax.rsqrt(jnp.mean(jnp.square(_ctx_1024t)) + 1e-12) * 0.953939
        ctx_1024 = 7.22013e-05 + 1.00017 * (_ctx_1024t + 0.3 * jax.random.normal(jax.random.fold_in(_rk, 611), (4, 512, 256), jnp.float32))
        _validS = jnp.arange(512)[None, :] < _lenS[:, None]
        _validS2 = jnp.arange(512)[None, :] < _lenS2[:, None]
        _causal = jnp.tril(jnp.ones((512, 512), dtype=bool))
        mask_Bx1x1xS2_if0 = jnp.where(jnp.ones((4, 1, 1, 512), dtype=bool), 0, 1).astype(jnp.int32)
        _g = jax.random.normal(jax.random.fold_in(_rk, 9001), (2, 1), jnp.float32)
        _g = jnp.sign(_g) * jnp.maximum(jnp.abs(_g), 1.0) + (_g == 0) * 1.0
        g_xattn = _g[0]
        g_ffn = _g[1]
        return (x, ctx_1024, mask_Bx1x1xS2_if0, g_xattn, g_ffn)
    x, ctx_1024, mask_Bx1x1xS2_if0, g_xattn, g_ffn = _rec_inputs()

    def _L0_xattn_setup():
        import jax, jax.numpy as jnp
        import numpy as np
        B, S, D_MODEL, H = (4, 512, 256, 16)
        DEPTH = D_MODEL // H

        def _split_heads(x):
            Bc = x.shape[0]
            return x.reshape(Bc, -1, H, DEPTH).transpose(0, 2, 1, 3)
        key = jax.random.key(seed)
        ks = jax.random.split(key, 12)
        inp = {'v': jax.random.normal(ks[0], (B, S, D_MODEL), jnp.float32), 'k': jax.random.normal(ks[1], (B, S, D_MODEL), jnp.float32), 'q': jax.random.normal(ks[2], (B, S, D_MODEL), jnp.float32), 'mask': jnp.zeros((B, 1, 1, S), jnp.int32), 'wq': jax.random.normal(ks[3], (D_MODEL, D_MODEL), jnp.float32) / np.sqrt(D_MODEL), 'bq': jnp.zeros((D_MODEL,), jnp.float32), 'wk': jax.random.normal(ks[4], (D_MODEL, D_MODEL), jnp.float32) / np.sqrt(D_MODEL), 'bk': jnp.zeros((D_MODEL,), jnp.float32), 'wv': jax.random.normal(ks[5], (D_MODEL, D_MODEL), jnp.float32) / np.sqrt(D_MODEL), 'bv': jnp.zeros((D_MODEL,), jnp.float32), 'gqw': 0.1 * jax.random.normal(ks[6], (S, 1), jnp.float32), 'gkw': 0.1 * jax.random.normal(ks[7], (S, 1), jnp.float32), 'wo': jax.random.normal(ks[8], (D_MODEL, D_MODEL), jnp.float32) / np.sqrt(D_MODEL), 'bo': jnp.zeros((D_MODEL,), jnp.float32)}
        return inp
    _L0_xattn_all = _L0_xattn_setup()
    _L0_xattn_in = {k: v for k, v in _L0_xattn_all.items() if k in ('wq', 'bq', 'wk', 'bk', 'wv', 'bv', 'gqw', 'gkw', 'wo', 'bo')}
    del _L0_xattn_all

    def _L0_ffn_setup():
        import jax, jax.numpy as jnp
        import numpy as np
        D_MODEL = 256
        N_HEAD = 16
        HEAD_DIM = D_MODEL // N_HEAD
        D_FF = 1024
        N_EXPERTS = 4
        EPS = 1e-05

        def _layer_norm(x, gamma, beta):
            mu = jnp.mean(x, axis=-1, keepdims=True)
            var = jnp.mean((x - mu) ** 2, axis=-1, keepdims=True)
            return (x - mu) / jnp.sqrt(var + EPS) * gamma + beta
        key = jax.random.key(seed)
        ks = jax.random.split(key, 20)
        f32 = jnp.float32
        sc = 1.0 / np.sqrt(D_MODEL)
        scf = 1.0 / np.sqrt(D_FF)
        return {'src': jax.random.normal(ks[0], (4, 128, D_MODEL), f32), 'Wq': jax.random.normal(ks[1], (D_MODEL, D_MODEL), f32) * sc, 'bq': jnp.zeros((D_MODEL,), f32), 'Wk': jax.random.normal(ks[2], (D_MODEL, D_MODEL), f32) * sc, 'bk': jnp.zeros((D_MODEL,), f32), 'Wv': jax.random.normal(ks[3], (D_MODEL, D_MODEL), f32) * sc, 'bv': jnp.zeros((D_MODEL,), f32), 'Wo': jax.random.normal(ks[4], (D_MODEL, D_MODEL), f32) * sc, 'bo': jnp.zeros((D_MODEL,), f32), 'router_w': jax.random.normal(ks[5], (D_MODEL, 1), f32) * 0.05, 'router_b': jnp.zeros((1,), f32), 'W1': jax.random.normal(ks[6], (N_EXPERTS, D_MODEL, D_FF), f32) * sc, 'b1': jnp.zeros((N_EXPERTS, D_FF), f32), 'W2': jax.random.normal(ks[7], (N_EXPERTS, D_FF, D_MODEL), f32) * scf, 'b2': jnp.zeros((N_EXPERTS, D_MODEL), f32), 'ln1_g': jnp.ones((D_MODEL,), f32), 'ln1_b': jnp.zeros((D_MODEL,), f32), 'ln2_g': jnp.ones((D_MODEL,), f32), 'ln2_b': jnp.zeros((D_MODEL,), f32)}
    _L0_ffn_all = _L0_ffn_setup()
    _L0_ffn_in = {k: v for k, v in _L0_ffn_all.items() if k in ('Wq', 'bq', 'Wk', 'bk', 'Wv', 'bv', 'Wo', 'bo', 'router_w', 'router_b', 'W1', 'b1', 'W2', 'b2', 'ln1_g', 'ln1_b', 'ln2_g', 'ln2_b')}
    del _L0_ffn_all
    return {'x': x, 'ctx_1024': ctx_1024, 'mask_Bx1x1xS2_if0': mask_Bx1x1xS2_if0, 'g_xattn': g_xattn, 'g_ffn': g_ffn, 'L0_xattn_wq': _L0_xattn_in['wq'], 'L0_xattn_bq': _L0_xattn_in['bq'], 'L0_xattn_wk': _L0_xattn_in['wk'], 'L0_xattn_bk': _L0_xattn_in['bk'], 'L0_xattn_wv': _L0_xattn_in['wv'], 'L0_xattn_bv': _L0_xattn_in['bv'], 'L0_xattn_gqw': _L0_xattn_in['gqw'], 'L0_xattn_gkw': _L0_xattn_in['gkw'], 'L0_xattn_wo': _L0_xattn_in['wo'], 'L0_xattn_bo': _L0_xattn_in['bo'], 'L0_ffn_Wq': _L0_ffn_in['Wq'], 'L0_ffn_bq': _L0_ffn_in['bq'], 'L0_ffn_Wk': _L0_ffn_in['Wk'], 'L0_ffn_bk': _L0_ffn_in['bk'], 'L0_ffn_Wv': _L0_ffn_in['Wv'], 'L0_ffn_bv': _L0_ffn_in['bv'], 'L0_ffn_Wo': _L0_ffn_in['Wo'], 'L0_ffn_bo': _L0_ffn_in['bo'], 'L0_ffn_router_w': _L0_ffn_in['router_w'], 'L0_ffn_router_b': _L0_ffn_in['router_b'], 'L0_ffn_W1': _L0_ffn_in['W1'], 'L0_ffn_b1': _L0_ffn_in['b1'], 'L0_ffn_W2': _L0_ffn_in['W2'], 'L0_ffn_b2': _L0_ffn_in['b2'], 'L0_ffn_ln1_g': _L0_ffn_in['ln1_g'], 'L0_ffn_ln1_b': _L0_ffn_in['ln1_b'], 'L0_ffn_ln2_g': _L0_ffn_in['ln2_g'], 'L0_ffn_ln2_b': _L0_ffn_in['ln2_b']}

def reference(x, ctx_1024, mask_Bx1x1xS2_if0, g_xattn, g_ffn, L0_xattn_wq, L0_xattn_bq, L0_xattn_wk, L0_xattn_bk, L0_xattn_wv, L0_xattn_bv, L0_xattn_gqw, L0_xattn_gkw, L0_xattn_wo, L0_xattn_bo, L0_ffn_Wq, L0_ffn_bq, L0_ffn_Wk, L0_ffn_bk, L0_ffn_Wv, L0_ffn_bv, L0_ffn_Wo, L0_ffn_bo, L0_ffn_router_w, L0_ffn_router_b, L0_ffn_W1, L0_ffn_b1, L0_ffn_W2, L0_ffn_b2, L0_ffn_ln1_g, L0_ffn_ln1_b, L0_ffn_ln2_g, L0_ffn_ln2_b):
    import jax
    import jax.numpy as jnp

    def _L0_xattn_ref(v, k, q, mask, wq, bq, wk, bk, wv, bv, gqw, gkw, wo, bo):
        import jax, jax.numpy as jnp
        import numpy as np
        B, S, D_MODEL, H = (4, 512, 256, 16)
        DEPTH = D_MODEL // H

        def _split_heads(x):
            Bc = x.shape[0]
            return x.reshape(Bc, -1, H, DEPTH).transpose(0, 2, 1, 3)
        qh = _split_heads(q @ wq + bq)
        kh = _split_heads(k @ wk + bk)
        vh = _split_heads(v @ wv + bv)
        qh = qh * gqw
        gq = jnp.sum(qh, axis=2, keepdims=True)
        kh = kh * gq * gkw
        gk = jnp.sum(kh, axis=2, keepdims=True)
        out = vh * gk + qh
        out = out.transpose(0, 2, 1, 3).reshape(out.shape[0], -1, D_MODEL)
        return out @ wo + bo

    def _L0_ffn_ref(src, Wq, bq, Wk, bk, Wv, bv, Wo, bo, router_w, router_b, W1, b1, W2, b2, ln1_g, ln1_b, ln2_g, ln2_b):
        import jax, jax.numpy as jnp
        import numpy as np
        D_MODEL = 256
        N_HEAD = 16
        HEAD_DIM = D_MODEL // N_HEAD
        D_FF = 1024
        N_EXPERTS = 4
        EPS = 1e-05

        def _layer_norm(x, gamma, beta):
            mu = jnp.mean(x, axis=-1, keepdims=True)
            var = jnp.mean((x - mu) ** 2, axis=-1, keepdims=True)
            return (x - mu) / jnp.sqrt(var + EPS) * gamma + beta
        B, T, _ = src.shape
        q = (src @ Wq + bq).reshape(B, T, N_HEAD, HEAD_DIM)
        k = (src @ Wk + bk).reshape(B, T, N_HEAD, HEAD_DIM)
        v = (src @ Wv + bv).reshape(B, T, N_HEAD, HEAD_DIM)
        scale = HEAD_DIM ** (-0.5)
        scores = jnp.einsum('bqhd,bkhd->bhqk', q, k) * scale
        probs = jax.nn.softmax(scores, axis=-1)
        attn = jnp.einsum('bhqk,bkhd->bqhd', probs, v).reshape(B, T, D_MODEL)
        attn = attn @ Wo + bo
        x = _layer_norm(src + attn, ln1_g, ln1_b)
        keys = (x @ router_w + router_b)[..., 0]
        expert_idx = jnp.remainder(jnp.floor(keys).astype(jnp.int32), N_EXPERTS)
        ff_out = jnp.zeros_like(x)
        for e in range(N_EXPERTS):
            h = jax.nn.relu(x @ W1[e] + b1[e])
            y = h @ W2[e] + b2[e]
            ff_out = ff_out + jnp.where((expert_idx == e)[..., None], y, 0.0)
        return _layer_norm(x + ff_out, ln2_g, ln2_b)
    x = x + jnp.tanh(g_xattn[0]) * _L0_xattn_ref(ctx_1024, ctx_1024, _layernorm(x, axis=-1), mask_Bx1x1xS2_if0, L0_xattn_wq, L0_xattn_bq, L0_xattn_wk, L0_xattn_bk, L0_xattn_wv, L0_xattn_bv, L0_xattn_gqw, L0_xattn_gkw, L0_xattn_wo, L0_xattn_bo)
    x = x + jnp.tanh(g_ffn[0]) * _L0_ffn_ref(_layernorm(x, axis=-1), L0_ffn_Wq, L0_ffn_bq, L0_ffn_Wk, L0_ffn_bk, L0_ffn_Wv, L0_ffn_bv, L0_ffn_Wo, L0_ffn_bo, L0_ffn_router_w, L0_ffn_router_b, L0_ffn_W1, L0_ffn_b1, L0_ffn_W2, L0_ffn_b2, L0_ffn_ln1_g, L0_ffn_ln1_b, L0_ffn_ln2_g, L0_ffn_ln2_b)
    return x

_drawn_inputs = setup_inputs


def setup_inputs(seed=0):
    import zlib

    import numpy as np

    out = dict(_drawn_inputs(seed))
    spreads = {'L0_xattn_bq': (0.0, 0.646),
     'L0_xattn_bk': (0.0, 0.1),
     'L0_xattn_bv': (0.0, 0.1),
     'L0_xattn_bo': (0.0, 0.1),
     'L0_ffn_bq': (0.0, 0.367),
     'L0_ffn_bk': (0.0, 2.0),
     'L0_ffn_bv': (0.0, 0.1),
     'L0_ffn_bo': (0.0, 0.1),
     'L0_ffn_b1': (0.0, 0.493),
     'L0_ffn_b2': (0.0, 0.35),
     'L0_ffn_ln1_g': (1.0, 0.2),
     'L0_ffn_ln1_b': (0.0, 0.1),
     'L0_ffn_ln2_g': (1.0, 0.2),
     'L0_ffn_ln2_b': (0.0, 0.27)}
    factors = {}
    for name, (base, spread) in spreads.items():
        noise = np.random.default_rng([zlib.crc32(name.encode()), seed]).standard_normal(out[name].shape)
        drawn = base * np.exp(spread * noise) if base else spread * noise
        out[name] = jnp.asarray(drawn.astype(out[name].dtype))
    for name, factor in factors.items():
        out[name] = (out[name] * factor).astype(out[name].dtype)
    return out
```

```python
import numpy as np
import concourse.bass as bass
from concourse import mybir
from contextlib import ExitStack

fp32 = mybir.dt.float32
fp32r = mybir.dt.float32r
int32 = mybir.dt.int32
uint32 = mybir.dt.uint32
ALU = mybir.AluOpType
ACT = mybir.ActivationFunctionType
AX = mybir.AxisListType


def gated_block_kernel(nc, x, ctx, g_xattn, g_ffn, wq, bq, wk, bk, wv, bv, gqw, gkw, wo, bo,
                       Wq, Bq, Wk, Bk, Wv, Bv, Wo, Bo, router_w, router_b, W1, b1, W2, b2,
                       ln1_g, ln1_b, ln2_g, ln2_b, out):
    B, S, D = x.shape
    H = 16
    DH = D // H
    E, _, F = W1.shape
    P = 128
    TT = S // P
    KD = D // P
    NT = B * TT
    NTOK = B * S
    NF = F // P
    EPS = 1e-5
    SCALE = DH ** -0.5
    G = 4
    HG = H // G
    SLOT = 256
    SA = SLOT // P
    MAXS = NTOK // SLOT + E - 1
    ROW = 2 * D + 1
    NB3 = 3

    qk_dram = nc.dram_tensor("qk_dram", (4, 2, P, S), fp32, kind="Internal").ap()
    m_dram = nc.dram_tensor("m_dram", (2, 32, 4, 32), fp32, kind="Internal").ap()
    x1_dram = nc.dram_tensor("x1_dram", (NTOK, D), fp32, kind="Internal").ap()
    xf_dram = nc.dram_tensor("xf_dram", (NTOK, D), fp32, kind="Internal").ap()
    slots_dram = nc.dram_tensor("slots_dram", (MAXS * SLOT, ROW), fp32, kind="Internal").ap()

    es = ExitStack()
    with es:
        def sb(name, shape, dt=fp32):
            return es.enter_context(nc.sbuf_tensor(name, shape, dt))

        def psum(name, shape):
            return es.enter_context(nc.psum_tensor(name, shape, fp32))

        def sem(name):
            return es.enter_context(nc.semaphore(name))

        w_sb = {n: sb(n + "_sb", [P, KD, D]) for n in ("wq", "wk", "wv", "wo", "Wq", "Wk", "Wv", "Wo")}
        W1_sb = sb("W1_sb", [P, E * KD, F])
        cols = sb("cols", [P, 5, KD])
        gqw_col = sb("gqw_col", [P, TT])
        gqw_row = sb("gqw_row", [P, S])
        gkw_row = sb("gkw_row", [P, S])
        rows_bc = sb("rows_bc", [P, 9, D])
        BO, BO2, BV, G1, B1, RW, G2, B2 = range(8)
        b1_col = sb("b1_col", [P, E * NF])
        rb_col = sb("rb_col", [P, 1])
        gates = sb("gates", [P, 2])
        tg = sb("tg", [P, 2])
        eps_col = sb("eps_col", [P, 1])
        gsum = sb("gsum", [P, 2])
        bG = sb("bG", [P, 2 * KD])
        C1 = sb("C1", [P, KD, S])
        ident = sb("ident", [P, P])
        xin = sb("xin", [P, TT, D])
        cin = sb("cin", [P, TT, D])
        t_a = sb("t_a", [P, TT, D])
        t_x1 = sb("t_x1", [P, TT, D])
        t_res = sb("t_res", [P, TT, D])
        xT = sb("xT", [P, KD, S])
        cT = sb("cT", [P, KD, S])
        oT = sb("oT", [P, KD, S])
        t1 = sb("t1", [P, S])
        xsum = sb("xsum", [P, KD])
        csum = sb("csum", [P, KD])
        g4 = sb("g4", [P, 2 * KD])
        gk = sb("gk", [P, KD])
        gkb = sb("gkb", [P, KD])
        V1 = sb("V1", [P, TT, H, 2 * DH])
        arena = sb("arena", [P, NT * ROW])
        probs = arena[:, 0:8 * 1024].rearrange("p (n q) -> p n q", n=8)
        routed = arena[:, :].rearrange("p (t r) -> p t r", r=ROW)
        mx = sb("mx", [P, 16])
        mneg = sb("mneg", [P, 32], fp32r)
        mT = sb("mT", [P, 2, 32])
        av = sb("av", [P, S])
        rec = sb("rec", [P, S // 32])
        an = sb("an", [P, S // 32, 2, DH])
        stats = sb("stats", [P, TT, 6])
        mv = sb("mv", [P, TT, 2])
        lnv = sb("lnv", [P, TT])
        r0 = sb("r0", [P, TT])
        nw = sb("nw", [P, 3, TT])
        rstd = sb("rstd", [P, TT])
        kb = sb("kb", [P, TT])
        keys = sb("keys", [P, NT])
        slot_row = sb("slot_row", [P, SA, ROW])
        before = sb("before", [P, P])
        ones = sb("ones", [P, P])
        thresholds = sb("thresholds", [P, NTOK // SLOT])
        with ExitStack() as attention:
            HL = attention.enter_context(nc.sbuf_tensor("HL", [P, 2, 2, S], fp32r))
            QS = attention.enter_context(nc.sbuf_tensor("QS", [P, H // 2, S], fp32r))
            KS = attention.enter_context(nc.sbuf_tensor("KS", [P, 2, H // 2, S], fp32r))
        W2_sb = sb("W2_sb", [P, E * NF, D])
        b2_bc = sb("b2_bc", [P, E, D])
        slot_x = sb("slot_x", [P, SA, D])
        slot_xT = sb("slot_xT", [P, KD, SLOT])
        slot_z = sb("slot_z", [P, SA, D])
        hid = V1[:, :, :, :].rearrange("p t h d -> p (t h d)").rearrange("p (f n) -> p f n", f=NF)
        r_int, r_int2 = sb("r_int", [P, NT], int32), sb("r_int2", [P, NT], int32)
        r_f = sb("r_f", [P, 4, NT])
        onehot, upto, place = sb("onehot", [P, E, NT]), sb("upto", [P, E, NT]), sb("place", [P, E, NT])
        counts = sb("counts", [P, 2, E, NT])
        n_over = sb("n_over", [P, E, NTOK // SLOT])
        n_slots, ends, base = sb("n_slots", [P, E]), sb("ends", [P, E]), sb("base", [P, E])
        ends_i = sb("ends_i", [P, E], int32)
        pos_f, pos_i = sb("pos_f", [P, NT]), sb("pos_i", [P, NT], int32)
        out_rows = out.rearrange("b s d -> (b s) d")

        work = [psum(f"work{i}", [P, 512]) for i in range(NB3)]
        sc = [psum(f"sc{i}", [P, 2, 512]) for i in range(2)]
        pv = psum("pv", [P, 512])

        x_loaded, c_loaded, w_loaded, w2_loaded = sem("x_loaded"), sem("c_loaded"), sem("w_loaded"), sem("w2_loaded")
        consts_ready, gates_ready, ones_ready = sem("consts_ready"), sem("gates_ready"), sem("ones_ready")
        id_ready = sem("id_ready")
        bn_done, mv_done, lnv_done, r0_done, newton_done = (sem(n) for n in ("bn_done", "mv_done", "lnv_done", "r0_done", "newton_done"))
        xg_done, xT_done, cT_done, csum_done, gv_full, g4_done, gk_done = (
            sem(n) for n in ("xg_done", "xT_done", "cT_done", "csum_done", "gv_full", "g4_done", "gk_done"))
        work_full = [sem(f"work_full{i}") for i in range(NB3)]
        t1_done, o_done, xb_done, x1_done, src_done, res_done, sT_done = (
            sem(n) for n in ("t1_done", "o_done", "xb_done", "x1_done", "src_done", "res_done", "sT_done"))
        hi_done, lo_done, v_done, qk_loaded, max_done, mneg_done, mT_done = (
            sem(n) for n in ("hi_done", "lo_done", "v_done", "qk_loaded", "max_done", "mneg_done", "mT_done"))
        m_stored, gates_loaded = sem("m_stored"), sem("gates_loaded")
        m_loaded = [sem(f"m_loaded{i}") for i in range(2)]
        qk_stored = [sem(f"qk_stored{i}") for i in range(2)]
        sc_full, exp_done, pv_round, av_done, rec_done, an_done, aT_done = (
            sem(n) for n in ("sc_full", "exp_done", "pv_round", "av_done", "rec_done", "an_done", "aT_done"))
        r_done, xn_done, xf_done, xfb_done, key_done, x1_stored, xf_stored = (
            sem(n) for n in ("r_done", "xn_done", "xf_done", "xfb_done", "key_done", "x1_stored", "xf_stored"))
        keys_ready, route_step, onehot_done, counts_full, ends_ready, pos_ready = (
            sem(n) for n in ("keys_ready", "route_step", "onehot_done", "counts_full", "ends_ready", "pos_ready"))
        tok_loaded, tok_id, scattered, slot_x_free, slot_row_free, slot_x_loaded, slot_row_loaded = (
            sem(n) for n in ("tok_loaded", "tok_id", "scattered", "slot_x_free", "slot_row_free", "slot_x_loaded", "slot_row_loaded"))
        slot_res, slot_out, out_stored, slot_T, slot_xT_done, hid_full, hid_even, hid_odd = (
            sem(n) for n in ("slot_res", "slot_out", "out_stored", "slot_T", "slot_xT_done", "hid_full", "hid_even", "hid_odd"))
        slot_sent, batch_over, slot_mv, slot_lnv, slot_r0, z_step, y_full, y_free = (
            sem(n) for n in ("slot_sent", "batch_over", "slot_mv", "slot_lnv", "slot_r0", "z_step", "y_full", "y_free"))
        W_LOADS, W2_LOADS = 3 + 5 + 8 + 1 + 7 + 16, E + 1 + E + 1
        fill_ready, filled = sem("fill_ready"), sem("filled")

        HEAD_TASKS = ["xT0", "xT1", "cT0", "cT1", "gv", "Q0", "V0", "Q1", "V1", "Y0", "Y1", "sT0", "sT1",
                      "q0", "q1", "k0", "k1", "v0", "v1"]
        TASKS = HEAD_TASKS + [f"A{n}" for n in range(64)] + ["O0", "O1"]
        INDEX = {t: i for i, t in enumerate(TASKS)}
        USES = [len(TASKS[k::NB3]) for k in range(NB3)]

        def bank(task):
            return INDEX[task] % NB3

        def release(task):
            kind = task.rstrip("0123456789")
            n = int(task[len(kind):] or 0)
            return {"xT": (xT_done, 2, n + 1), "cT": (cT_done, 2, n + 1), "gv": (g4_done, 1, 1),
                    "Q": (t1_done, 2, n + 1), "V": (o_done, 2, n + 1), "Y": (x1_done, 2, n + 1),
                    "sT": (sT_done, 2, n + 1), "q": (lo_done, 4, n + 1), "k": (lo_done, 4, n + 3),
                    "v": (v_done, 2, n + 1), "A": (max_done, 64, n + 1), "O": (r_done, 2, n + 1)}[kind]

        def wait_bank_full(eng, b, task):
            k = bank(task)
            eng.wait_ge(work_full[k], b * USES[k] + INDEX[task] // NB3 + 1)

        hid_bank = [sc[0][:, 0, 0:SLOT], sc[0][:, 1, 0:SLOT], sc[1][:, 0, 0:SLOT], sc[1][:, 1, 0:SLOT]]

        def expert_slots(eng):
            first = 0
            for e in range(E):
                end = eng.value_load(ends_i[0:1, e:e + 1], min_val=e + 1, max_val=MAXS - (E - 1 - e))
                yield e, first, end
                first = end

        def tail_sp(sp):
            sp.wait_ge(pv_round, B * 8)
            sp.wait_ge(batch_over, 2 * B)
            sp.wait_ge(xf_stored, B * 16)
            for h, t in ((0, x1_dram), (1, xf_dram)):
                at = D * (1 - h)
                sp.dma_start(routed[:, :, at:at + D], t.rearrange("(t p) d -> p t d", p=P)).then_inc(tok_loaded, 16)
            for e in range(E):
                sp.dma_start(W2_sb[:, e * NF:(e + 1) * NF, :], W2[e, :, :].rearrange("(k p) d -> p k d", p=P)).then_inc(w2_loaded, 16)
            sp.dma_start(b2_bc[:, :, :], b2.partition_broadcast(P)).then_inc(w2_loaded, 16)
            sp.wait_ge(ends_ready, 1)
            sp.wait_ge(scattered, 16 * NT)
            for e, first, end in expert_slots(sp):
                with sp.Fori(first, end) as i:
                    rows = slots_dram[bass.ds(i * SLOT, SLOT), :].rearrange("(a p) r -> p a r", p=P)
                    sp.wait_ge(slot_x_free, i + 1)
                    sp.dma_start(slot_x[:, :, :], rows[:, :, 0:D]).then_inc(slot_x_loaded, 16)
                    sp.wait_ge(slot_row_free, i + 1)
                    sp.dma_start(slot_row[:, :, :], rows).then_inc(slot_row_loaded, 16)

        def tail_pool(pool):
            pool.wait_ge(pv_round, B * 8)
            nc.gpsimd.iota(routed[:, :, 2 * D:ROW].bitcast(int32), [[P, NT], [0, 1]], base=0, channel_multiplier=1).then_inc(tok_id, 1)
            pool.wait_ge(tok_id, 1)
            pool.wait_ge(tok_loaded, 32)
            pool.wait_ge(pos_ready, 1)
            for t in range(NT):
                nc.gpsimd.indirect_dma_start(slots_dram, bass.IndirectOffsetOnAxis(ap=pos_i[:, t:t + 1], axis=0), routed[:, t, :], None).then_inc(scattered, 16)
            pool.wait_ge(w2_loaded, W2_LOADS * 16)
            pool.sem_inc(slot_x_free, 1)
            pool.sem_inc(slot_row_free, 1)
            for e, first, end in expert_slots(pool):
                with pool.Fori(first, end) as i:
                    pool.wait_ge(slot_row_loaded, i * 16 + 16)
                    nc.gpsimd.tensor_tensor(slot_row[:, :, 0:D], slot_row[:, :, 0:D], b2_bc[:, e:e + 1, :].broadcast_to([P, SA, D]), ALU.add).then_inc(slot_res, 1)
                    nc.gpsimd.tensor_tensor(slot_row[:, :, D:2 * D], slot_row[:, :, D:2 * D], rows_bc[:, B2:B2 + 1, :].broadcast_to([P, SA, D]), ALU.add).then_inc(slot_res, 1)
                    pool.wait_ge(slot_out, i * 2 + 2)
                    pool.sem_inc(slot_sent, 1)
                    for a in range(SA):
                        nc.gpsimd.indirect_dma_start(out_rows, bass.IndirectOffsetOnAxis(ap=slot_row[:, a, 2 * D:ROW].bitcast(int32), axis=0), slot_z[:, a, :], None,
                                                     bounds_check=NTOK - 1, oob_is_err=False).then_inc(out_stored, 16)
                    pool.wait_ge(out_stored, i * 32 + 32)
                    pool.sem_inc(slot_row_free, 1)

        def tail_act(act):
            act.wait_ge(w2_loaded, W2_LOADS * 16)
            act.wait_ge(ends_ready, 1)
            for e, first, end in expert_slots(act):
                with act.Fori(first, end) as i:
                    act.wait_ge(slot_T, i + 1)
                    nc.scalar.activation(slot_xT[:, :, :].rearrange("p k n -> p (k n)"), work[2][:, :], ACT.Identity).then_inc(slot_xT_done, 1)
                    for f in range(0, NF, 2):
                        act.wait_ge(hid_full, i * NF + f + 1)
                        nc.scalar.activation(hid[:, f, :], hid_bank[f % 4], ACT.Relu, bias=b1_col[:, e * NF + f:e * NF + f + 1]).then_inc(hid_even, 1)
                    act.wait_ge(slot_mv, i * SA + SA)
                    nc.scalar.activation(lnv[:, 0:SA], mv[:, 0:SA, 1], ACT.Ln, bias=eps_col[:, :]).then_inc(slot_lnv, 1)
                    act.wait_ge(slot_lnv, i + 1)
                    nc.scalar.activation(r0[:, 0:SA], lnv[:, 0:SA], ACT.Exp, scale=-0.5).then_inc(slot_r0, 1)

        def tail_dve(dve):
            dve.wait_ge(keys_ready, B)
            dve.wait_ge(bn_done, B * 3 * (TT + 1))
            step = [0]

            def link(ins):
                step[0] += 1
                ins.then_inc(route_step, 1)
                dve.wait_ge(route_step, step[0])

            link(nc.vector.tensor_copy(r_int[:, :], keys[:, :]))
            link(nc.vector.tensor_copy(r_f[:, 0, :], r_int[:, :]))
            link(nc.vector.tensor_tensor(r_f[:, 1, :], r_f[:, 0, :], keys[:, :], ALU.is_gt))
            link(nc.vector.tensor_tensor(r_f[:, 2, :], r_f[:, 0, :], r_f[:, 1, :], ALU.subtract))
            link(nc.vector.tensor_copy(r_int[:, :], r_f[:, 2, :]))
            link(nc.vector.tensor_scalar(r_int2[:, :], r_int[:, :], E - 1, None, ALU.bitwise_and))
            link(nc.vector.tensor_copy(r_f[:, 3, :], r_int2[:, :]))
            for e in range(E):
                nc.vector.tensor_scalar(onehot[:, e, :], r_f[:, 3, :], float(e), None, ALU.is_equal).then_inc(onehot_done, 1)
            dve.wait_ge(counts_full, 1)
            link(nc.vector.tensor_copy(counts[:, :, :, :].rearrange("p a e t -> p (a e t)"), pv[:, 0:2 * E * NT]))
            for e in range(E):
                link(nc.vector.tensor_tensor_scan(upto[:, e, :], ones[:, 0:NT], counts[:, 1, e, :], 0.0, ALU.mult, ALU.add))
            for e in range(E):
                link(nc.vector.tensor_scalar(n_over[:, e, :], thresholds[:, :], upto[:, e, NT - 1:NT], None, ALU.is_lt))
            link(nc.vector.reduce_sum(n_slots[:, :], n_over[:, :, :], AX.X))
            link(nc.vector.tensor_scalar(n_slots[:, :], n_slots[:, :], 1.0, None, ALU.max))
            link(nc.vector.tensor_tensor_scan(ends[:, :], ones[:, 0:E], n_slots[:, :], 0.0, ALU.mult, ALU.add))
            nc.vector.tensor_copy(ends_i[:, :], ends[:, :]).then_inc(ends_ready, 1)
            link(nc.vector.tensor_tensor(base[:, :], ends[:, :], n_slots[:, :], ALU.subtract))
            link(nc.vector.tensor_scalar(base[:, :], base[:, :], float(SLOT), None, ALU.mult))
            link(nc.vector.tensor_tensor(place[:, :, :], upto[:, :, :], counts[:, 1, :, :], ALU.subtract))
            link(nc.vector.tensor_tensor(place[:, :, :], place[:, :, :], counts[:, 0, :, :], ALU.add))
            link(nc.vector.tensor_tensor(place[:, :, :], place[:, :, :], base[:, :].unsqueeze(2).broadcast_to([P, E, NT]), ALU.add))
            link(nc.vector.tensor_tensor(place[:, :, :], place[:, :, :], onehot[:, :, :], ALU.mult))
            link(nc.vector.reduce_sum(pos_f[:, :], place[:, :, :].rearrange("p e t -> p t e"), AX.X))
            nc.vector.tensor_copy(pos_i[:, :], pos_f[:, :]).then_inc(pos_ready, 1)

            dve.wait_ge(w2_loaded, W2_LOADS * 16)
            dve.wait_ge(ends_ready, 1)
            dve.sem_inc(y_free, 1)
            for e, first, end in expert_slots(dve):
                with dve.Fori(first, end) as i:
                    for f in range(1, NF, 2):
                        dve.wait_ge(hid_full, i * NF + f + 1)
                        nc.vector.tensor_scalar(hid[:, f, :], hid_bank[f % 4], b1_col[:, e * NF + f:e * NF + f + 1], 0.0, ALU.add, ALU.max).then_inc(hid_odd, 1)
                    dve.wait_ge(slot_res, i * 2 + 2)
                    dve.wait_ge(y_full, i + 1)
                    nc.vector.tensor_tensor(slot_z[:, 0, :], work[0][:, 0:D], slot_row[:, 0, 0:D], ALU.add).then_inc(z_step, 1)
                    nc.vector.tensor_tensor(slot_z[:, 1, :], work[1][:, 0:D], slot_row[:, 1, 0:D], ALU.add).then_inc(y_free, 1)
                    dve.wait_ge(z_step, i * 12 + 1)
                    dve.wait_ge(y_free, i + 2)
                    for a in range(SA):
                        nc.vector.bn_stats(stats[:, a, :], slot_z[:, a, :]).then_inc(z_step, 1)
                    dve.wait_ge(z_step, i * 12 + 3)
                    dve.sem_inc(z_step, 1)
                    for a in range(SA):
                        nc.vector.bn_aggr(mv[:, a, :], stats[:, a, :]).then_inc(slot_mv, 1)
                    dve.wait_ge(slot_r0, i + 1)
                    nc.vector.tensor_tensor(nw[:, 0, 0:SA], r0[:, 0:SA], r0[:, 0:SA], ALU.mult).then_inc(z_step, 1)
                    dve.wait_ge(z_step, i * 12 + 5)
                    nc.vector.scalar_tensor_tensor(nw[:, 1, 0:SA], mv[:, 0:SA, 1], EPS, nw[:, 0, 0:SA], ALU.add, ALU.mult).then_inc(z_step, 1)
                    dve.wait_ge(z_step, i * 12 + 6)
                    nc.vector.tensor_scalar(nw[:, 2, 0:SA], nw[:, 1, 0:SA], -0.5, 1.5, ALU.mult, ALU.add).then_inc(z_step, 1)
                    dve.wait_ge(z_step, i * 12 + 7)
                    nc.vector.tensor_tensor(rstd[:, 0:SA], r0[:, 0:SA], nw[:, 2, 0:SA], ALU.mult).then_inc(z_step, 1)
                    dve.wait_ge(z_step, i * 12 + 8)
                    for a in range(SA):
                        nc.vector.tensor_scalar(slot_z[:, a, :], slot_z[:, a, :], mv[:, a, 0:1], rstd[:, a:a + 1], ALU.subtract, ALU.mult).then_inc(z_step, 1)
                    for a in range(SA):
                        dve.wait_ge(z_step, i * 12 + 9 + a)
                        nc.vector.tensor_tensor(slot_z[:, a, :], slot_z[:, a, :], rows_bc[:, G2, :], ALU.mult).then_inc(z_step, 1)
                    for a in range(SA):
                        dve.wait_ge(z_step, i * 12 + 11 + a)
                        nc.vector.tensor_tensor(slot_z[:, a, :], slot_z[:, a, :], slot_row[:, a, D:2 * D], ALU.add).then_inc(slot_out, 1)

        def tail_pe(pe):
            pe.wait_ge(onehot_done, E)
            oh = onehot[:, :, :].rearrange("p e t -> p (e t)")
            nc.tensor.matmul(pv[:, 0:E * NT], before[:, :], oh, start=True, stop=True)
            nc.tensor.matmul(pv[:, E * NT:2 * E * NT], ones[:, :], oh, start=True, stop=True).then_inc(counts_full, 1)
            pe.wait_ge(w2_loaded, W2_LOADS * 16)
            pe.wait_ge(ends_ready, 1)
            pe.sem_inc(hid_even, 2)
            pe.sem_inc(hid_odd, 2)
            for e, first, end in expert_slots(pe):
                with pe.Fori(first, end) as i:
                    pe.wait_ge(slot_x_loaded, i * 16 + 16)
                    for k in range(KD):
                        for a in range(SA):
                            last = nc.tensor.transpose(work[2][:, k * SLOT + a * P:k * SLOT + (a + 1) * P], slot_x[:, a, k * P:(k + 1) * P], ident[:, :])
                    last.then_inc(slot_T, 1)
                    pe.wait_ge(slot_xT_done, i + 1)
                    pe.sem_inc(slot_x_free, 1)

                    def up(f):
                        s = (hid_even, hid_odd)[f % 2]
                        pe.wait_ge(s, i * (NF // 2) + f // 2 + 1)
                        for k in range(KD):
                            last = nc.tensor.matmul(hid_bank[f % 4], W1_sb[:, e * KD + k, f * P:(f + 1) * P], slot_xT[:, k, :], start=(k == 0), stop=(k == KD - 1))
                        last.then_inc(hid_full, 1)

                    def down(f):
                        s = (hid_even, hid_odd)[f % 2]
                        pe.wait_ge(s, i * (NF // 2) + f // 2 + 3)
                        if f == 0:
                            pe.wait_ge(y_free, i + 1)
                        for a in range(SA):
                            last = nc.tensor.matmul(work[a][:, 0:D], hid[:, f, a * P:(a + 1) * P], W2_sb[:, e * NF + f, :], start=(f == 0), stop=(f == NF - 1))
                        if f == NF - 1:
                            last.then_inc(y_full, 1)

                    for f in range(NF + 2):
                        if f < NF:
                            up(f)
                        if f >= 2:
                            down(f - 2)
            pe.wait_ge(slot_sent, end)
            pe.wait_ge(slot_x_free, end + 1)
            pe.wait_ge(slot_row_free, end + 1)

        block = es.enter_context(nc.Block())

        def pair_of(g, hh):
            return 2 * g + hh // 2, hh % 2

        @block.sync
        def _(sp):
            def load_weight(n, ap):
                sp.dma_start(w_sb[n][:, :, :], ap.rearrange("(k p) n -> p k n", p=P)).then_inc(w_loaded, 16)

            def load_batch(b):
                sp.dma_start(xin[:, :, :], x[b, :, :].rearrange("(t p) d -> p t d", p=P)).then_inc(x_loaded, 16)
                sp.dma_start(cin[:, :, :], ctx[b, :, :].rearrange("(t p) d -> p t d", p=P)).then_inc(c_loaded, 16)

            sp.dma_start(gates[:, 0:1], g_xattn.partition_broadcast(P)).then_inc(gates_loaded, 16)
            sp.dma_start(gates[:, 1:2], g_ffn.partition_broadcast(P)).then_inc(gates_loaded, 16)
            sp.dma_start(gqw_col[:, :], gqw.rearrange("(t p) o -> p (t o)", p=P), allow_slow_non_contiguous=True).then_inc(w_loaded, 16)
            sp.dma_start(gqw_row[:, :], gqw.rearrange("s o -> (s o)").partition_broadcast(P)).then_inc(w_loaded, 16)
            sp.dma_start(gkw_row[:, :], gkw.rearrange("s o -> (s o)").partition_broadcast(P)).then_inc(w_loaded, 16)
            for i, v in enumerate((bq, bk, bv, Bq, Bk)):
                sp.dma_start(cols[:, i, :], v.rearrange("(k p) -> p k", p=P), allow_slow_non_contiguous=True).then_inc(w_loaded, 16)
            for i, v in enumerate((bo, Bo, Bv, ln1_g, ln1_b, router_w.rearrange("d o -> (d o)"), ln2_g, ln2_b)):
                sp.dma_start(rows_bc[:, i, :], v.partition_broadcast(P)).then_inc(w_loaded, 16)
            sp.dma_start(rb_col[:, :], router_b.partition_broadcast(P)).then_inc(w_loaded, 16)
            for n, ap in (("wq", wq), ("wk", wk), ("wv", wv), ("wo", wo), ("Wq", Wq), ("Wk", Wk), ("Wv", Wv)):
                load_weight(n, ap)
            for t in range(2):
                for hh in range(HG):
                    for gg in range(2):
                        pair, c = pair_of(2 * t + gg, hh)
                        h = 8 * c + pair
                        r = 32 * hh + 16 * gg
                        sp.dma_start(w_sb["Wo"][r:r + DH, t, :], Wo[h * DH:(h + 1) * DH, :]).then_inc(w_loaded, 16)
            for e in range(E):
                sp.dma_start(W1_sb[:, e * KD:(e + 1) * KD, :], W1[e, :, :].rearrange("(k p) f -> p k f", p=P)).then_inc(w2_loaded, 16)
            sp.dma_start(b1_col[:, :], b1.rearrange("e (f p) -> p (e f)", p=P), allow_slow_non_contiguous=True).then_inc(w2_loaded, 16)
            sp.wait_ge(fill_ready, 2)
            for i in range(MAXS):
                sp.dma_start(slots_dram[i * SLOT:(i + 1) * SLOT, :].rearrange("(a p) r -> p a r", p=P),
                             slot_row[:, :, :]).then_inc(filled, 16)
            with sp.Fori(0, B) as b:
                load_batch(b)
                sp.wait_ge(x1_done, b * 2 + 2)
                sp.dma_start(x1_dram[bass.ds(b * S, S), :].rearrange("(t p) d -> p t d", p=P), t_x1[:, :, :]).then_inc(x1_stored, 16)
                for j in range(4):
                    sp.wait_ge(lo_done, b * 4 + j + 1)
                    sp.dma_start(qk_dram[j, :, :, :].rearrange("h p n -> p h n"), HL[:, j % 2, :, :].bitcast(fp32)).then_inc(qk_stored[j % 2], 16)
                for j in range(2):
                    sp.wait_ge(qk_stored[j], b * 32 + 32)
                for c in range(2):
                    for i, (qpart, kpart) in enumerate(((0, 0), (1, 0), (0, 1))):
                        at = 48 * c + 16 * i
                        sp.dma_start(QS[at:at + DH, :, :].bitcast(fp32), qk_dram[c, qpart, :, :].rearrange("(r d) n -> d r n", d=DH)).then_inc(qk_loaded, 16)
                        sp.dma_start(KS[at:at + DH, c, :, :].bitcast(fp32), qk_dram[2 + c, kpart, :, :].rearrange("(r d) n -> d r n", d=DH)).then_inc(qk_loaded, 16)
                for g in range(G):
                    sp.wait_ge(mT_done, b * G + g + 1)
                    sp.dma_start(m_dram[g % 2, :, :, :].rearrange("y a i -> a y i"), mT[:, g % 2, :]).then_inc(m_stored, 16)
                    sp.wait_ge(m_stored, b * 16 * G + 16 * (g + 1))
                    for u in range(2):
                        sp.dma_start(QS[96:100, 2 * g + u, :].bitcast(fp32),
                                     m_dram[g % 2, :, :, :].rearrange("(h u c k) a i -> u c h (k a i)", h=2, u=2, c=2)[u]).then_inc(m_loaded[g % 2], 16)
                sp.wait_ge(xf_done, b * TT + TT)
                sp.dma_start(xf_dram[bass.ds(b * S, S), :].rearrange("(t p) d -> p t d", p=P), t_a[:, :, :]).then_inc(xf_stored, 16)
                sp.wait_ge(xf_stored, b * 16 + 16)
                sp.wait_ge(x1_stored, b * 16 + 16)
                sp.wait_ge(key_done, b * TT + TT)
                sp.sem_inc(batch_over, 1)
            tail_sp(sp)

        @block.gpsimd
        def _(pool):
            nc.gpsimd.memset(ident[:, :], 0.0).then_inc(id_ready, 1)
            pool.wait_ge(id_ready, 1)
            nc.gpsimd.affine_select(out=ident[:, :], in_=ident[:, :], compare_op=ALU.not_equal, fill=1.0,
                                    base=0, pattern=[[-1, P]], channel_multiplier=1).then_inc(id_ready, 1)
            nc.gpsimd.memset(slot_row[:, :, 0:2 * D], 0.0).then_inc(fill_ready, 1)
            nc.gpsimd.iota(slot_row[:, :, 2 * D:ROW].bitcast(int32), [[0, SA], [0, 1]], base=2 * NTOK, channel_multiplier=1).then_inc(fill_ready, 1)
            nc.gpsimd.memset(ones[:, :], 1.0).then_inc(id_ready, 1)
            nc.gpsimd.iota(thresholds[:, :], [[SLOT, NTOK // SLOT]], base=0, channel_multiplier=0, allow_small_or_imprecise_dtypes=True).then_inc(id_ready, 1)
            pool.wait_ge(id_ready, 4)
            nc.gpsimd.affine_select(out=before[:, :], in_=ones[:, :], compare_op=ALU.is_gt, fill=0.0,
                                    base=0, pattern=[[1, P]], channel_multiplier=-1).then_inc(id_ready, 1)
            pool.wait_ge(consts_ready, 12)
            with pool.Fori(0, B) as b:
                pool.wait_ge(x_loaded, b * 16 + 16)
                nc.gpsimd.tensor_tensor(t_res[:, :, :], xin[:, :, :], rows_bc[:, BO:BO + 1, :].broadcast_to([P, TT, D]), ALU.add).then_inc(xb_done, 1)
                pool.wait_ge(src_done, b * TT + TT)
                pool.wait_ge(x1_done, b * 2 + 2)
                nc.gpsimd.tensor_tensor(t_res[:, :, :], t_a[:, :, :], rows_bc[:, BO2:BO2 + 1, :].broadcast_to([P, TT, D]), ALU.add).then_inc(res_done, 1)
                for t in range(TT):
                    pool.wait_ge(xn_done, b * TT + t + 1)
                    nc.gpsimd.tensor_tensor(t_a[:, t, :], t_res[:, t, :], rows_bc[:, G1, :], ALU.mult).then_inc(xfb_done, 1)
                    pool.wait_ge(xfb_done, b * TT + t + 1)
                    nc.gpsimd.tensor_tensor(t_a[:, t, :], t_a[:, t, :], rows_bc[:, B1, :], ALU.add).then_inc(xf_done, 1)
                pool.wait_ge(key_done, b * TT + TT)
                pool.sem_inc(batch_over, 1)
            tail_pool(pool)

        @block.scalar
        def _(act):
            act.wait_ge(gates_loaded, 32)
            nc.scalar.activation(tg[:, :], gates[:, :], ACT.Tanh).then_inc(gates_ready, 1)

            def rsqrt_start(b, l):
                act.wait_ge(mv_done, b * 3 * TT + (l + 1) * TT)
                nc.scalar.activation(lnv[:, :], mv[:, :, 1], ACT.Ln, bias=eps_col[:, :]).then_inc(lnv_done, 1)
                act.wait_ge(lnv_done, b * 3 + l + 1)
                nc.scalar.activation(r0[:, :], lnv[:, :], ACT.Exp, scale=-0.5).then_inc(r0_done, 1)

            act.wait_ge(consts_ready, 12)
            act.wait_ge(filled, 16 * MAXS)
            with act.Fori(0, B) as b:
                rsqrt_start(b, 0)
                for c in range(KD):
                    wait_bank_full(act, b, f"xT{c}")
                    nc.scalar.activation(xT[:, c, :], work[bank(f"xT{c}")][:, :], ACT.Identity, accum_out=xsum[:, c:c + 1]).then_inc(xT_done, 1)
                for c in range(KD):
                    wait_bank_full(act, b, f"cT{c}")
                    nc.scalar.activation(cT[:, c, :], work[bank(f"cT{c}")][:, :], ACT.Identity).then_inc(cT_done, 1)
                rsqrt_start(b, 1)
                for c in range(KD):
                    wait_bank_full(act, b, f"sT{c}")
                    nc.scalar.activation(xT[:, c, :], work[bank(f"sT{c}")][:, :], ACT.Identity).then_inc(sT_done, 1)
                for j, task in enumerate(("q0", "q1", "k0", "k1")):
                    wait_bank_full(act, b, task)
                    if j >= 2:
                        act.wait_ge(qk_stored[j % 2], b * 32 + 16)
                    nc.scalar.activation(HL[:, j % 2, 0, :], work[bank(task)][:, :], ACT.Identity,
                                         bias=cols[:, 3 + j // 2, j % 2:j % 2 + 1]).then_inc(hi_done, 1)
                for n in range(32):
                    act.wait_ge(sc_full, b * 32 + n + 1)
                    if n >= 8:
                        act.wait_ge(pv_round, b * 8 + n // 4 - 1)
                    nc.scalar.activation(probs[:, n % 8, :], sc[n % 2][:, :, :].rearrange("p a q -> p (a q)"), ACT.Exp, scale=SCALE).then_inc(exp_done, 1)
                rsqrt_start(b, 2)
            tail_act(act)

        @block.vector
        def _(dve):
            nc.vector.memset(eps_col[:, :], EPS).then_inc(ones_ready, 1)
            nc.vector.memset(V1[:, :, :, DH:2 * DH], 1.0).then_inc(ones_ready, 1)
            nc.vector.memset(QS[:, :, :].bitcast(fp32), 0.0).then_inc(ones_ready, 1)
            nc.vector.memset(KS[:, :, :, :].bitcast(fp32), 0.0).then_inc(ones_ready, 1)
            dve.wait_ge(ones_ready, 4)
            nc.vector.memset(KS[96:98, 0, :, :].bitcast(fp32), 1.0).then_inc(ones_ready, 1)
            nc.vector.memset(KS[96:100, 1, :, :].bitcast(fp32), 1.0).then_inc(ones_ready, 1)
            dve.wait_ge(ones_ready, 6)
            nc.vector.memset(KS[96:98, 1, :, :].bitcast(fp32), 0.0).then_inc(ones_ready, 1)
            dve.wait_ge(ones_ready, 7)
            dve.wait_ge(w_loaded, W_LOADS * 16)
            dve.wait_ge(gates_ready, 1)
            nc.vector.tensor_scalar(rows_bc[:, BO, :], rows_bc[:, BO, :], tg[:, 0:1], None, ALU.mult).then_inc(consts_ready, 1)
            nc.vector.tensor_scalar(rows_bc[:, G2, :], rows_bc[:, G2, :], tg[:, 1:2], None, ALU.mult).then_inc(consts_ready, 1)
            nc.vector.tensor_scalar(rows_bc[:, B2, :], rows_bc[:, B2, :], tg[:, 1:2], None, ALU.mult).then_inc(consts_ready, 1)
            nc.vector.reduce_sum(gsum[:, 0:1], gqw_row[:, :], AX.X).then_inc(consts_ready, 1)
            nc.vector.reduce_sum(gsum[:, 1:2], gkw_row[:, :], AX.X).then_inc(consts_ready, 1)
            for c in range(KD):
                nc.vector.tensor_scalar(C1[:, c, :], gqw_row[:, :], cols[:, 0, c:c + 1], None, ALU.mult).then_inc(consts_ready, 1)
            dve.wait_ge(consts_ready, 7)
            for i in range(2):
                nc.vector.tensor_scalar(bG[:, KD * i:KD * (i + 1)], cols[:, i, :], gsum[:, i:i + 1], None, ALU.mult).then_inc(consts_ready, 1)
            dve.wait_ge(consts_ready, 9)
            for i in range(3):
                nc.vector.memset(t1[:, i:i + 1], 0.0).then_inc(consts_ready, 1)
            dve.wait_ge(consts_ready, 12)

            def layernorm_stats(b, l, src):
                for t in range(TT):
                    nc.vector.bn_stats(stats[:, t, :], src[:, t, :]).then_inc(bn_done, 1)
                dve.wait_ge(bn_done, b * 3 * (TT + 1) + l * (TT + 1) + TT)
                dve.sem_inc(bn_done, 1)
                for t in range(TT):
                    nc.vector.bn_aggr(mv[:, t, :], stats[:, t, :]).then_inc(mv_done, 1)
                dve.wait_ge(r0_done, b * 3 + l + 1)
                at = b * 12 + l * 4
                nc.vector.tensor_tensor(nw[:, 0, :], r0[:, :], r0[:, :], ALU.mult).then_inc(newton_done, 1)
                dve.wait_ge(newton_done, at + 1)
                nc.vector.scalar_tensor_tensor(nw[:, 1, :], mv[:, :, 1], EPS, nw[:, 0, :], ALU.add, ALU.mult).then_inc(newton_done, 1)
                dve.wait_ge(newton_done, at + 2)
                nc.vector.tensor_scalar(nw[:, 2, :], nw[:, 1, :], -0.5, 1.5, ALU.mult, ALU.add).then_inc(newton_done, 1)
                dve.wait_ge(newton_done, at + 3)
                nc.vector.tensor_tensor(rstd[:, :], r0[:, :], nw[:, 2, :], ALU.mult).then_inc(newton_done, 1)
                dve.wait_ge(newton_done, at + 4)

            with dve.Fori(0, B) as b:
                dve.wait_ge(x_loaded, b * 16 + 16)
                layernorm_stats(b, 0, xin)
                nc.vector.tensor_tensor(nw[:, 0, :], rstd[:, :], gqw_col[:, :], ALU.mult).then_inc(xg_done, 1)
                dve.wait_ge(xg_done, b * (TT + 1) + 1)
                for t in range(TT):
                    nc.vector.tensor_scalar(t_a[:, t, :], xin[:, t, :], mv[:, t, 0:1], nw[:, 0, t:t + 1], ALU.subtract, ALU.mult).then_inc(xg_done, 1)
                for c in range(KD):
                    dve.wait_ge(cT_done, b * KD + c + 1)
                    nc.vector.tensor_tensor_reduce(out=t1[:, :], in0=cT[:, c, :], in1=gkw_row[:, :], scale=1.0, scalar=0.0,
                                                   op0=ALU.mult, op1=ALU.add, accum_out=csum[:, c:c + 1]).then_inc(csum_done, 1)
                    dve.wait_ge(csum_done, b * KD + c + 1)
                wait_bank_full(dve, b, "gv")
                nc.vector.tensor_tensor(g4[:, :], work[bank("gv")][:, 0:2 * KD], bG[:, :], ALU.add).then_inc(g4_done, 1)
                dve.wait_ge(g4_done, b + 1)
                nc.vector.tensor_tensor(gk[:, :], g4[:, 0:KD], g4[:, KD:2 * KD], ALU.mult).then_inc(gk_done, 1)
                dve.wait_ge(gk_done, b * 2 + 1)
                nc.vector.tensor_tensor(gkb[:, :], gk[:, :], cols[:, 2, :], ALU.mult).then_inc(gk_done, 1)
                dve.wait_ge(gk_done, b * 2 + 2)
                for c in range(KD):
                    wait_bank_full(dve, b, f"Q{c}")
                    nc.vector.scalar_tensor_tensor(t1[:, :], work[bank(f"Q{c}")][:, :], gkb[:, c:c + 1], C1[:, c, :], ALU.add, ALU.add).then_inc(t1_done, 1)
                    dve.wait_ge(t1_done, b * KD + c + 1)
                    wait_bank_full(dve, b, f"V{c}")
                    nc.vector.scalar_tensor_tensor(oT[:, c, :], work[bank(f"V{c}")][:, :], gk[:, c:c + 1], t1[:, :], ALU.mult, ALU.add).then_inc(o_done, 1)
                    dve.wait_ge(o_done, b * KD + c + 1)
                dve.wait_ge(xb_done, b + 1)
                for j in range(2):
                    wait_bank_full(dve, b, f"Y{j}")
                    nc.vector.scalar_tensor_tensor(t_x1[:, 2 * j:2 * j + 2, :].rearrange("p t d -> p (t d)"), work[bank(f"Y{j}")][:, :], tg[:, 0:1],
                                                   t_res[:, 2 * j:2 * j + 2, :].rearrange("p t d -> p (t d)"), ALU.mult, ALU.add).then_inc(x1_done, 1)
                dve.wait_ge(x1_done, b * 2 + 2)
                layernorm_stats(b, 1, t_x1)
                for t in range(TT):
                    nc.vector.tensor_scalar(t_a[:, t, :], t_x1[:, t, :], mv[:, t, 0:1], rstd[:, t:t + 1], ALU.subtract, ALU.mult).then_inc(src_done, 1)
                for j, task in enumerate(("q0", "q1", "k0", "k1")):
                    dve.wait_ge(hi_done, b * 4 + j + 1)
                    nc.vector.scalar_tensor_tensor(HL[:, j % 2, 1, :], work[bank(task)][:, :], cols[:, 3 + j // 2, j % 2:j % 2 + 1],
                                                   HL[:, j % 2, 0, :].bitcast(fp32), ALU.add, ALU.subtract).then_inc(lo_done, 1)
                for j in range(2):
                    wait_bank_full(dve, b, f"v{j}")
                    nc.vector.tensor_tensor(V1[:, 2 * j:2 * j + 2, :, 0:DH], work[bank(f"v{j}")][:, :].rearrange("p (t h d) -> p t h d", t=2, h=H),
                                            rows_bc[:, BV:BV + 1, :].rearrange("p o (h d) -> p o h d", h=H).broadcast_to([P, 2, H, DH]), ALU.add).then_inc(v_done, 1)

                def group_max(g, first, last):
                    for i in range(first, last):
                        n = 16 * g + i
                        wait_bank_full(dve, b, f"A{n}")
                        nc.vector.reduce_max(mx[:, i:i + 1], work[bank(f"A{n}")][:, :], AX.X).then_inc(max_done, 1)

                def group_neg(g):
                    dve.wait_ge(max_done, b * 64 + 16 * (g + 1))
                    nc.vector.tensor_scalar(mneg[:, 0:16], mx[:, :], -1.0, None, ALU.mult).then_inc(mneg_done, 1)
                    dve.wait_ge(mneg_done, b * 2 * G + 2 * g + 1)
                    nc.vector.scalar_tensor_tensor(mneg[:, 16:32], mx[:, :], -1.0, mneg[:, 0:16].bitcast(fp32), ALU.mult, ALU.subtract).then_inc(mneg_done, 1)
                    dve.wait_ge(mneg_done, b * 2 * G + 2 * g + 2)
                    if g >= 2:
                        dve.wait_ge(m_stored, b * 16 * G + 16 * (g - 1))
                    nc.vector.transpose(mT[:, g % 2, :], mneg[:, :].bitcast(fp32)).then_inc(mT_done, 1)

                def group_out(g):
                    gg = g % 2
                    dve.wait_ge(pv_round, b * 8 + 2 * g + 2)
                    nc.vector.transpose(av[:, :], pv[:, :]).then_inc(av_done, 1)
                    dve.wait_ge(av_done, b * G + g + 1)
                    av_v = av[:, :].rearrange("p (n d) -> p n d", d=32)
                    nc.vector.reciprocal(rec[:, :], av_v[:, :, DH]).then_inc(rec_done, 1)
                    dve.wait_ge(rec_done, b * G + g + 1)
                    nc.vector.tensor_tensor(an[:, :, gg, :], av_v[:, :, 0:DH], rec[:, :].unsqueeze(2).broadcast_to([P, S // 32, DH]), ALU.mult).then_inc(an_done, 1)
                    dve.wait_ge(an_done, b * G + g + 1)
                    if gg == 1:
                        nc.vector.transpose(cT[:, g // 2, :], an[:, :, :, :].rearrange("p n g d -> p (n g d)")).then_inc(aT_done, 1)
                        dve.wait_ge(aT_done, b * 2 + g // 2 + 1)

                for g in range(2):
                    group_max(g, 0, 16)
                    group_neg(g)
                for g in range(G):
                    if g + 2 < G:
                        group_max(g + 2, 0, 8)
                    if g:
                        group_out(g - 1)
                    if g + 2 < G:
                        group_max(g + 2, 8, 16)
                        group_neg(g + 2)
                group_out(G - 1)
                dve.wait_ge(res_done, b + 1)
                for j in range(2):
                    wait_bank_full(dve, b, f"O{j}")
                    r = t_res[:, 2 * j:2 * j + 2, :].rearrange("p t d -> p (t d)")
                    nc.vector.tensor_tensor(r, work[bank(f"O{j}")][:, :], r, ALU.add).then_inc(r_done, 1)
                dve.wait_ge(r_done, b * 2 + 2)
                layernorm_stats(b, 2, t_res)
                for t in range(TT):
                    nc.vector.tensor_scalar(t_res[:, t, :], t_res[:, t, :], mv[:, t, 0:1], rstd[:, t:t + 1], ALU.subtract, ALU.mult).then_inc(xn_done, 1)
                for t in range(TT):
                    dve.wait_ge(xf_done, b * TT + t + 1)
                    nc.vector.tensor_tensor_reduce(out=t1[:, 0:D], in0=t_a[:, t, :], in1=rows_bc[:, RW, :], scale=1.0, scalar=0.0,
                                                   op0=ALU.mult, op1=ALU.add, accum_out=kb[:, t:t + 1]).then_inc(key_done, 1)
                    dve.wait_ge(key_done, b * TT + t + 1)
                nc.vector.tensor_scalar(keys[:, bass.ds(b * TT, TT)], kb[:, :], rb_col[:, :], None, ALU.add).then_inc(keys_ready, 1)
                dve.wait_ge(keys_ready, b + 1)
            tail_dve(dve)

        @block.tensor
        def _(pe):
            def wait_bank_free(b, task):
                i = INDEX[task]
                if i >= NB3:
                    s, per, k = release(TASKS[i - NB3])
                    pe.wait_ge(s, b * per + k)

            def transposes(b, task, src, c):
                wait_bank_free(b, task)
                for t in range(TT):
                    last = nc.tensor.transpose(work[bank(task)][:, t * P:(t + 1) * P], src[:, t, c * P:(c + 1) * P], ident[:, :])
                last.then_inc(work_full[bank(task)], 1)

            def project_T(b, task, w, c, src):
                wait_bank_free(b, task)
                for k in range(KD):
                    last = nc.tensor.matmul(work[bank(task)][:, :], w[:, k, c * P:(c + 1) * P], src[:, k, :], start=(k == 0), stop=(k == KD - 1))
                last.then_inc(work_full[bank(task)], 1)

            def project(b, task, j, w, src):
                wait_bank_free(b, task)
                for tt in range(2):
                    t = 2 * j + tt
                    for k in range(KD):
                        last = nc.tensor.matmul(work[bank(task)][:, tt * D:(tt + 1) * D], src[:, k, t * P:(t + 1) * P], w[:, k, :], start=(k == 0), stop=(k == KD - 1))
                last.then_inc(work_full[bank(task)], 1)

            pe.wait_ge(id_ready, 5)
            pe.wait_ge(consts_ready, 12)
            with pe.Fori(0, B) as b:
                pe.wait_ge(xg_done, b * (TT + 1) + TT + 1)
                for c in range(KD):
                    transposes(b, f"xT{c}", t_a, c)
                pe.wait_ge(c_loaded, b * 16 + 16)
                for c in range(KD):
                    transposes(b, f"cT{c}", cin, c)
                wait_bank_free(b, "gv")
                pe.wait_ge(xT_done, b * KD + KD)
                pe.wait_ge(csum_done, b * KD + KD)
                for i, (w, s) in enumerate((("wq", xsum), ("wk", csum))):
                    for c in range(KD):
                        for k in range(KD):
                            last = nc.tensor.matmul(work[bank("gv")][:, i * KD + c:i * KD + c + 1], w_sb[w][:, k, c * P:(c + 1) * P], s[:, k:k + 1], start=(k == 0), stop=(k == KD - 1))
                last.then_inc(work_full[bank("gv")], 1)
                for c in range(KD):
                    project_T(b, f"Q{c}", w_sb["wq"], c, xT)
                    project_T(b, f"V{c}", w_sb["wv"], c, cT)
                pe.wait_ge(o_done, b * 2 + 2)
                for j in range(2):
                    project(b, f"Y{j}", j, w_sb["wo"], oT)
                pe.wait_ge(src_done, b * TT + TT)
                for c in range(KD):
                    transposes(b, f"sT{c}", t_a, c)
                pe.wait_ge(sT_done, b * KD + KD)
                for c in range(2):
                    project_T(b, f"q{c}", w_sb["Wq"], c, xT)
                for c in range(2):
                    project_T(b, f"k{c}", w_sb["Wk"], c, xT)
                for j in range(2):
                    project(b, f"v{j}", j, w_sb["Wv"], xT)

                def scores_for_max(n):
                    g, hh, chunk = n // 16, n // 4 % 4, n % 4
                    pair, c = pair_of(g, hh)
                    task = f"A{n}"
                    wait_bank_free(b, task)
                    nc.tensor.matmul(work[bank(task)][:, :], QS[0:96, pair, chunk * P:(chunk + 1) * P], KS[0:96, c, pair, :], start=True, stop=True)\
                        .then_inc(work_full[bank(task)], 1)

                def weighted_values(r):
                    g = r // 2
                    pe.wait_ge(exp_done, b * 32 + 4 * (r + 1))
                    if r % 2 == 0 and r:
                        pe.wait_ge(av_done, b * G + g)
                    for a in range(2):
                        kc = 2 * (r % 2) + a
                        for hh in range(HG):
                            pair, c = pair_of(g, hh)
                            last = nc.tensor.matmul(pv[32 * hh:32 * hh + 32, :], V1[:, kc, 8 * c + pair, :],
                                                    probs[:, (4 * r + hh) % 8, a * 512:(a + 1) * 512], start=(kc == 0), stop=(kc == TT - 1))
                    last.then_inc(pv_round, 1)

                pe.wait_ge(qk_loaded, b * 12 * 16 + 12 * 16)
                for n in range(32):
                    scores_for_max(n)
                pe.wait_ge(v_done, b * 2 + 2)
                for n in range(32):
                    r, hh = n // 4, n % 4
                    g = r // 2
                    pair, c = pair_of(g, hh)
                    if n % 8 == 0:
                        pe.wait_ge(m_loaded[g % 2], b * 64 + 32 * (g // 2 + 1))
                    if n >= 2:
                        pe.wait_ge(exp_done, b * 32 + n - 1)
                    for a in range(2):
                        kc = 2 * (r % 2) + a
                        last = nc.tensor.matmul(sc[n % 2][:, a, :], KS[0:100, c, pair, kc * P:(kc + 1) * P], QS[0:100, pair, :], start=True, stop=True)
                    last.then_inc(sc_full, 1)
                    if n < 16:
                        scores_for_max(32 + 2 * n)
                        scores_for_max(33 + 2 * n)
                    if hh == 3 and r:
                        weighted_values(r - 1)
                weighted_values(7)
                pe.wait_ge(aT_done, b * 2 + 2)
                for j in range(2):
                    project(b, f"O{j}", j, w_sb["Wo"], cT)
                pe.wait_ge(r_done, b * 2 + 2)
            tail_pe(pe)


_INS = ["x", "ctx_1024", "g_xattn", "g_ffn",
        "L0_xattn_wq", "L0_xattn_bq", "L0_xattn_wk", "L0_xattn_bk", "L0_xattn_wv", "L0_xattn_bv",
        "L0_xattn_gqw", "L0_xattn_gkw", "L0_xattn_wo", "L0_xattn_bo",
        "L0_ffn_Wq", "L0_ffn_bq", "L0_ffn_Wk", "L0_ffn_bk", "L0_ffn_Wv", "L0_ffn_bv", "L0_ffn_Wo", "L0_ffn_bo",
        "L0_ffn_router_w", "L0_ffn_router_b", "L0_ffn_W1", "L0_ffn_b1", "L0_ffn_W2", "L0_ffn_b2",
        "L0_ffn_ln1_g", "L0_ffn_ln1_b", "L0_ffn_ln2_g", "L0_ffn_ln2_b"]


def kernel(**inputs):
    import concourse.bacc as bacc
    from concourse.bass_utils import run_bass_kernel_spmd

    nc = bacc.Bacc("TRN2", target_bir_lowering=False, num_devices=1)
    arrays, args = {}, []
    for name in _INS:
        a = np.ascontiguousarray(inputs[name])
        arrays[f"in_{name}"] = a
        args.append(nc.dram_tensor(f"in_{name}", a.shape, mybir.dt.from_np(a.dtype), kind="ExternalInput").ap())
    out = nc.dram_tensor("out_dram", (4, 512, 256), fp32, kind="ExternalOutput").ap()
    gated_block_kernel(nc, *args, out)
    r = run_bass_kernel_spmd(nc, [arrays], core_ids=[0])
    return r.results[0]["out_dram"]
```

```python
import numpy as np
import concourse.bass as bass
from concourse import mybir
from contextlib import ExitStack

fp32 = mybir.dt.float32
fp32r = mybir.dt.float32r
int32 = mybir.dt.int32
uint32 = mybir.dt.uint32
ALU = mybir.AluOpType
ACT = mybir.ActivationFunctionType
AX = mybir.AxisListType


def gated_block_kernel(nc, x, ctx, g_xattn, g_ffn, wq, bq, wk, bk, wv, bv, gqw, gkw, wo, bo,
                       Wq, Bq, Wk, Bk, Wv, Bv, Wo, Bo, router_w, router_b, W1, b1, W2, b2,
                       ln1_g, ln1_b, ln2_g, ln2_b, out):
    B, S, D = x.shape
    H = 16
    DH = D // H
    E, _, F = W1.shape
    P = 128
    TT = S // P
    KD = D // P
    NT = B * TT
    NTOK = B * S
    NF = F // P
    EPS = 1e-5
    SCALE = DH ** -0.5
    G = 4
    HG = H // G
    SLOT = 256
    SA = SLOT // P
    MAXS = NTOK // SLOT + E - 1
    ROW = 2 * D + 1
    NB3 = 3

    qk_dram = nc.dram_tensor("qk_dram", (4, 2, P, S), fp32, kind="Internal").ap()
    m_dram = nc.dram_tensor("m_dram", (2, 32, 4, 32), fp32, kind="Internal").ap()
    x1_dram = nc.dram_tensor("x1_dram", (NTOK, D), fp32, kind="Internal").ap()
    res_dram = nc.dram_tensor("res_dram", (NTOK, D), fp32, kind="Internal").ap()
    xf_dram = nc.dram_tensor("xf_dram", (NTOK, D), fp32, kind="Internal").ap()
    slots_dram = nc.dram_tensor("slots_dram", (MAXS * SLOT, ROW), fp32, kind="Internal").ap()

    es = ExitStack()
    with es:
        def sb(name, shape, dt=fp32):
            return es.enter_context(nc.sbuf_tensor(name, shape, dt))

        def psum(name, shape):
            return es.enter_context(nc.psum_tensor(name, shape, fp32))

        def sem(name):
            return es.enter_context(nc.semaphore(name))

        w_sb = {n: sb(n + "_sb", [P, KD, D]) for n in ("wq", "wk", "wv", "wo", "Wq", "Wk", "Wv", "Wo")}
        W1_sb = sb("W1_sb", [P, E * KD, F])
        cols = sb("cols", [P, 5, KD])
        gqw_col = sb("gqw_col", [P, TT])
        gkw_row = sb("gkw_row", [P, S])
        rows_bc = sb("rows_bc", [P, 9, D])
        BO, BO2, BV, G1, B1, RW, G2, B2, GRW = range(9)
        b1_col = sb("b1_col", [P, E * NF])
        rb_col = sb("rb_col", [P, 1])
        gates = sb("gates", [P, 2])
        tg = sb("tg", [P, 2])
        mhalf = sb("mhalf", [P, TT])
        gsum = sb("gsum", [P, 4])
        bG = sb("bG", [P, 2 * KD])
        C1 = sb("C1", [P, KD, S])
        ident = sb("ident", [P, P])
        before = sb("before", [P, P])
        ones = sb("ones", [P, P])
        thresholds = sb("thresholds", [P, NTOK // SLOT])
        pad_row = sb("pad_row", [P, ROW])
        xin = sb("xin", [P, TT, D])
        cin = sb("cin", [P, TT, D])
        t_a = sb("t_a", [P, TT, D])
        t_r = sb("t_r", [P, TT, D])
        xT = sb("xT", [P, KD, S])
        cT = sb("cT", [P, KD, S])
        oT = sb("oT", [P, KD, S])
        srcT = sb("srcT", [P, KD, S])
        aT = sb("aT", [P, KD, S])
        t1 = sb("t1", [P, S])
        xsum = sb("xsum", [P, KD])
        csum = sb("csum", [P, KD])
        g4 = sb("g4", [P, 2 * KD])
        gk = sb("gk", [P, KD])
        gkb = sb("gkb", [P, KD])
        V1 = sb("V1", [P, TT, H, 2 * DH])
        hid = V1[:, :, :, :].rearrange("p t h d -> p (t h d)").rearrange("p (f n) -> p f n", f=NF)
        arena = sb("arena", [P, NT * ROW])
        probs = arena[:, 0:8 * 1024].rearrange("p (n q) -> p n q", n=8)
        routed = arena[:, :].rearrange("p (t r) -> p t r", r=ROW)
        mx = sb("mx", [P, 16])
        mneg = sb("mneg", [P, 32], fp32r)
        mT = sb("mT", [P, 2, 32])
        av = sb("av", [P, S])
        rec = sb("rec", [P, S // 32])
        an = sb("an", [P, S // 32, 2, DH])
        stats = sb("stats", [P, TT, 6])
        mv = [sb(f"mv{l}", [P, TT, 2]) for l in range(3)]
        var_eps = sb("var_eps", [P, TT])
        rstd = [sb(f"rstd{l}", [P, TT]) for l in range(3)]
        rg = sb("rg", [P, TT])
        kb = sb("kb", [P, TT])
        dots, means, rstds = sb("dots", [P, NT]), sb("means", [P, NT]), sb("rstds", [P, NT])
        keys = sb("keys", [P, NT])
        with ExitStack() as attention:
            HL = attention.enter_context(nc.sbuf_tensor("HL", [P, 2, 2, S], fp32r))
            QS = attention.enter_context(nc.sbuf_tensor("QS", [P, H // 2, S], fp32r))
            KS = attention.enter_context(nc.sbuf_tensor("KS", [P, 2, H // 2, S], fp32r))
        W2_sb = sb("W2_sb", [P, E * NF, D])
        b2_bc = sb("b2_bc", [P, E, D])
        slot_x = sb("slot_x", [P, SA, D])
        slot_xT = sb("slot_xT", [P, KD, SLOT])
        slot_z = sb("slot_z", [P, SA, D])
        slot_row = sb("slot_row", [P, SA, ROW])
        r_int, r_int2 = sb("r_int", [P, NT], int32), sb("r_int2", [P, NT], int32)
        r_f = sb("r_f", [P, 4, NT])
        onehot, upto, place = sb("onehot", [P, E, NT]), sb("upto", [P, E, NT]), sb("place", [P, E, NT])
        counts = sb("counts", [P, 2, E, NT])
        n_over = sb("n_over", [P, E, NTOK // SLOT])
        n_slots, ends, base = sb("n_slots", [P, E]), sb("ends", [P, E]), sb("base", [P, E])
        ends_i = sb("ends_i", [P, E], int32)
        pos_f, pos_i = sb("pos_f", [P, NT]), sb("pos_i", [P, NT], int32)
        out_rows = out.rearrange("b s d -> (b s) d")

        amax = [psum(f"amax{i}", [P, 512]) for i in range(2)]
        side = psum("side", [P, 512])
        sc = [psum(f"sc{i}", [P, 2, 512]) for i in range(2)]
        pv = psum("pv", [P, 512])

        SEMS = {}

        def sems(names):
            return [SEMS.setdefault(n, sem(n)) for n in names.split()]

        x_loaded, c_loaded, w_loaded, W_loaded, gates_loaded, filled = sems("x_loaded c_loaded w_loaded W_loaded gates_loaded filled")
        pool_ready, stack_ready, ks_ready, consts_ready, gates_ready = sems("pool_ready stack_ready ks_ready consts_ready gates_ready")
        bn_done, mv_done, ve_done, rstd_done = sems("bn_done mv_done ve_done rstd_done")
        rg_done, xg_done, csum_done, g4_done, gk_done, t1_done, o_done, xb_done, x1_done, src_done, res_done = sems(
            "rg_done xg_done csum_done g4_done gk_done t1_done o_done xb_done x1_done src_done res_done")
        xT_full, cT_full, gv_full, Q_full, V_full, Y_full, sT_full, qk_full, v_full, O_full, A_full = sems(
            "xT_full cT_full gv_full Q_full V_full Y_full sT_full qk_full v_full O_full A_full")
        xT_done, cT_done, sT_done, hi_done, lo_done, v_done, max_done, mneg_done, mT_done = sems(
            "xT_done cT_done sT_done hi_done lo_done v_done max_done mneg_done mT_done")
        m_stored, x1_stored, res_stored, xf_stored, r_loaded, tok_loaded = sems("m_stored x1_stored res_stored xf_stored r_loaded tok_loaded")
        m_loaded, qk_stored, stack_loaded = sems("m_loaded0 m_loaded1"), sems("qk_stored0 qk_stored1"), sems("stack0 stack1 stack2 stack3")
        sc_full, exp_done, pv_round, av_done, rec_done, an_done, aT_done = sems("sc_full exp_done pv_round av_done rec_done an_done aT_done")
        r_done, dot_done, xn_done, xfm_done, xf_done, keys_ready = sems("r_done dot_done xn_done xfm_done xf_done keys_ready")
        w2_loaded, route_step, onehot_done, counts_full, ends_ready, pos_ready, tok_id, scattered = sems(
            "w2_loaded route_step onehot_done counts_full ends_ready pos_ready tok_id scattered")
        slot_x_free, slot_row_free, slot_x_loaded, slot_row_loaded, slot_res, slot_out, out_stored, slot_T, slot_xT_done = sems(
            "slot_x_free slot_row_free slot_x_loaded slot_row_loaded slot_res slot_out out_stored slot_T slot_xT_done")
        hid_full, hid_even, hid_odd, slot_sent, slot_mv, slot_ve, slot_rstd, z_step, y_full, y_free = sems(
            "hid_full hid_even hid_odd slot_sent slot_mv slot_ve slot_rstd z_step y_full y_free")
        sp_passed, pool_passed = sems("sp_passed pool_passed")
        CONSTS = 12
        POOL_CONSTS = 6
        W2_LOADS = 2 * (E + 1)

        def pair_of(g, hh):
            return 2 * g + hh // 2, hh % 2

        STEPS = range(8, 40)
        SIDE = {8: ("sT", 0, 1), 9: ("sT", 1, 1), 10: ("q", 0, 1), 11: ("q", 1, 1), 12: ("k", 0, 1), 13: ("k", 1, 1),
                14: ("cT", 0, 2), 15: ("cT", 1, 2), 17: ("xT", 0, 2), 18: ("xT", 1, 2), 20: ("gv", 0, 2),
                22: ("Q", 0, 2), 23: ("V", 0, 2), 25: ("Q", 1, 2), 26: ("V", 1, 2), 29: ("Y", 0, 2), 30: ("Y", 1, 2),
                35: ("v", 0, 1), 36: ("v", 1, 1), 38: ("O", 0, 0), 39: ("O", 1, 0)}
        FIRST_PART = [("cT", 0), ("cT", 1), ("xT", 0), ("xT", 1), ("gv", 0), ("Q", 0), ("V", 0), ("Q", 1), ("V", 1), ("Y", 0), ("Y", 1)]
        SECOND_PART = [("sT", 0), ("sT", 1), ("q", 0), ("q", 1), ("k", 0), ("k", 1)]
        LEAD = [t + (0,) for t in FIRST_PART + SECOND_PART]
        LEAD_SIDE = dict(zip(range(-11, 0), [t + (1,) for t in FIRST_PART]))
        LEAD_SIDE.update({1: ("v", 0, 0), 2: ("v", 1, 0)})
        LAST_MAX = 20

        def wait(eng, s, value):
            if isinstance(value, int) and value <= 0:
                return
            eng.wait_ge(s, value)

        def release(task, n, b):
            return {"xT": (xT_done, b * 2 + n + 1), "cT": (cT_done, b * 2 + n + 1), "gv": (g4_done, b + 1),
                    "Q": (t1_done, b * 2 + n + 1), "V": (o_done, b * 2 + n + 1), "Y": (x1_done, b * 2 + n + 1),
                    "sT": (sT_done, b * 2 + n + 1), "q": (lo_done, b * 4 + n + 1), "k": (lo_done, b * 4 + n + 3),
                    "v": (v_done, b * 2 + n + 1), "O": (r_done, b * 2 + n + 1)}[task]

        def runs(task, after, part):
            return after <= {"all": 2, "next": 1, "last": 0}[part]

        def steps_of(part):
            return STEPS if part != "last" else range(8, 32)

        def sp_program(sp):
            def load_weight(n, ap, s):
                sp.dma_start(w_sb[n][:, :, :], ap.rearrange("(k p) n -> p k n", p=P)).then_inc(s, 16)

            def store_qk(b, j):
                if j == 0:
                    for g in range(G):
                        wait(sp, stack_loaded[g], b * 192)
                        if not isinstance(b, int):
                            sp.sem_inc(sp_passed, 1)
                sp.wait_ge(lo_done, b * 4 + j + 1)
                sp.dma_start(qk_dram[j, :, :, :].rearrange("h p n -> p h n"), HL[:, j % 2, :, :].bitcast(fp32)).then_inc(qk_stored[j % 2], 16)

            def load_stack(b, g):
                if g == 0:
                    for i in range(2):
                        sp.wait_ge(qk_stored[i], b * 32 + 32)
                    sp.sem_inc(sp_passed, 1)
                wait(sp, sc_full, (b - 1) * 32 + 8 * (g + 1))
                for c in range(2):
                    for i, (qpart, kpart) in enumerate(((0, 0), (1, 0), (0, 1))):
                        at = 48 * c + 16 * i
                        sp.dma_start(QS[at:at + DH, 2 * g:2 * g + 2, :].bitcast(fp32), qk_dram[c, qpart, 32 * g:32 * g + 32, :].rearrange("(r d) n -> d r n", d=DH))\
                            .then_inc(stack_loaded[g], 16)
                        sp.dma_start(KS[at:at + DH, c, 2 * g:2 * g + 2, :].bitcast(fp32), qk_dram[2 + c, kpart, 32 * g:32 * g + 32, :].rearrange("(r d) n -> d r n", d=DH))\
                            .then_inc(stack_loaded[g], 16)

            def move_maxima(b, g):
                sp.wait_ge(mT_done, b * G + g + 1)
                sp.dma_start(m_dram[g % 2, :, :, :].rearrange("y a i -> a y i"), mT[:, g % 2, :]).then_inc(m_stored, 16)
                sp.wait_ge(m_stored, b * 16 * G + 16 * (g + 1))
                for u in range(2):
                    sp.dma_start(QS[96:100, 2 * g + u, :].bitcast(fp32),
                                 m_dram[g % 2, :, :, :].rearrange("(h u c k) a i -> u c h (k a i)", h=2, u=2, c=2)[u]).then_inc(m_loaded[g % 2], 16)

            sp.dma_start(gqw_col[:, :], gqw.rearrange("(t p) o -> p (t o)", p=P), allow_slow_non_contiguous=True).then_inc(w_loaded, 16)
            sp.dma_start(gates[:, 0:1], g_xattn.partition_broadcast(P)).then_inc(gates_loaded, 16)
            sp.dma_start(gates[:, 1:2], g_ffn.partition_broadcast(P)).then_inc(gates_loaded, 16)
            sp.dma_start(t1[:, :], gqw.rearrange("s o -> (s o)").partition_broadcast(P)).then_inc(w_loaded, 16)
            sp.dma_start(gkw_row[:, :], gkw.rearrange("s o -> (s o)").partition_broadcast(P)).then_inc(w_loaded, 16)
            for i, v in enumerate((bq, bk, bv, Bq, Bk)):
                sp.dma_start(cols[:, i, :], v.rearrange("(k p) -> p k", p=P), allow_slow_non_contiguous=True).then_inc(w_loaded, 16)
            for i, v in enumerate((bo, Bo, Bv, ln1_g, ln1_b, router_w.rearrange("d o -> (d o)"), ln2_g, ln2_b)):
                sp.dma_start(rows_bc[:, i, :], v.partition_broadcast(P)).then_inc(w_loaded, 16)
            sp.dma_start(rb_col[:, :], router_b.partition_broadcast(P)).then_inc(w_loaded, 16)
            for n, ap in (("wq", wq), ("wk", wk), ("wv", wv), ("wo", wo)):
                load_weight(n, ap, w_loaded)
            for n, ap in (("Wq", Wq), ("Wk", Wk), ("Wv", Wv)):
                load_weight(n, ap, W_loaded)
            for t in range(2):
                for hh in range(HG):
                    for gg in range(2):
                        pair, c = pair_of(2 * t + gg, hh)
                        h = 8 * c + pair
                        r = 32 * hh + 16 * gg
                        sp.dma_start(w_sb["Wo"][r:r + DH, t, :], Wo[h * DH:(h + 1) * DH, :]).then_inc(W_loaded, 16)
            for j in range(4):
                store_qk(0, j)
            sp.wait_ge(stack_ready, 2)
            for g in range(G):
                load_stack(0, g)
            sp.wait_ge(pool_ready, POOL_CONSTS)
            for i in range(MAXS * SA):
                sp.dma_start(slots_dram[i * P:(i + 1) * P, :], pad_row[:, :]).then_inc(filled, 16)
            for e in range(E):
                sp.dma_start(W1_sb[:, e * KD:(e + 1) * KD, :], W1[e, :, :].rearrange("(k p) f -> p k f", p=P)).then_inc(w2_loaded, 16)
            sp.dma_start(b1_col[:, :], b1.rearrange("e (f p) -> p (e f)", p=P), allow_slow_non_contiguous=True).then_inc(w2_loaded, 16)
            for g in range(2):
                move_maxima(0, g)

            def turn(b, part):
                for n in steps_of(part):
                    if n % 8 == 4:
                        g = (n + 4) // 8
                        if g < G:
                            move_maxima(b, g)
                        elif part != "last":
                            move_maxima(b + 1, g - G)
                    if part != "last":
                        if n in SIDE and SIDE[n][0] in "qk":
                            store_qk(b + 1, SIDE[n][1] + 2 * (SIDE[n][0] == "k"))
                        if n in (16, 20, 26, 34):
                            load_stack(b + 1, {16: 0, 20: 1, 26: 2, 34: 3}[n])

            with sp.Fori(0, B - 2) as b:
                turn(b, "all")
            turn(B - 2, "next")
            turn(B - 1, "last")
            tail_sp(sp)

        def pool_program(pool):
            pool.dma_start(xin[:, :, :], x[0, :, :].rearrange("(t p) d -> p t d", p=P)).then_inc(x_loaded, 16)
            pool.dma_start(cin[:, :, :], ctx[0, :, :].rearrange("(t p) d -> p t d", p=P)).then_inc(c_loaded, 16)
            nc.gpsimd.memset(ident[:, :], 0.0).then_inc(pool_ready, 1)
            nc.gpsimd.memset(mhalf[:, :], -0.5).then_inc(pool_ready, 1)
            pool.wait_ge(pool_ready, 2)
            nc.gpsimd.affine_select(out=ident[:, :], in_=ident[:, :], compare_op=ALU.not_equal, fill=1.0,
                                    base=0, pattern=[[-1, P]], channel_multiplier=1).then_inc(pool_ready, 1)

            def rsqrt(idx, l):
                pool.wait_ge(mv_done, idx * TT + TT)
                pool.sem_inc(pool_passed, 1)
                nc.gpsimd.tensor_scalar(var_eps[:, :], mv[l][:, :, 1], EPS, None, ALU.add).then_inc(ve_done, 1)
                pool.wait_ge(ve_done, idx + 1)
                nc.gpsimd.tensor_tensor(rstd[l][:, :], var_eps[:, :], mhalf[:, :], ALU.pow).then_inc(rstd_done, 1)
                pool.wait_ge(rstd_done, idx + 1)
                pool.sem_inc(pool_passed, 1)

            def first_part(b, idx):
                rsqrt(idx, 0)
                wait(pool, res_stored, b * 16)
                nc.gpsimd.tensor_tensor(rg[:, :], rstd[0][:, :], gqw_col[:, :], ALU.mult).then_inc(rg_done, 1)
                pool.wait_ge(rg_done, b + 1)
                pool.sem_inc(pool_passed, 1)
                for t in range(TT):
                    nc.gpsimd.tensor_scalar(t_a[:, t, :], xin[:, t, :], mv[0][:, t, 0:1], rg[:, t:t + 1], ALU.subtract, ALU.mult).then_inc(xg_done, 1)
                pool.wait_ge(xg_done, b * TT + TT)
                nc.gpsimd.tensor_tensor(xin[:, :, :], xin[:, :, :], rows_bc[:, BO:BO + 1, :].broadcast_to([P, TT, D]), ALU.add).then_inc(xb_done, 1)
                rsqrt(idx + 1, 1)
                pool.dma_start(token_rows(x1_dram, b), xin[:, :, :]).then_inc(x1_stored, 16)
                for t in range(TT):
                    nc.gpsimd.tensor_scalar(t_a[:, t, :], xin[:, t, :], mv[1][:, t, 0:1], rstd[1][:, t:t + 1], ALU.subtract, ALU.mult).then_inc(src_done, 1)

            def token_rows(dram, b):
                return dram[b * S:(b + 1) * S, :].rearrange("(t p) d -> p t d", p=P) if isinstance(b, int) else \
                    dram[bass.ds(b * S, S), :].rearrange("(t p) d -> p t d", p=P)

            def residual(b):
                pool.wait_ge(sT_full, b * 2 + 2)
                nc.gpsimd.tensor_tensor(t_a[:, :, :], t_a[:, :, :], rows_bc[:, BO2:BO2 + 1, :].broadcast_to([P, TT, D]), ALU.add).then_inc(res_done, 1)
                pool.wait_ge(res_done, b + 1)
                pool.sem_inc(pool_passed, 1)
                pool.dma_start(token_rows(res_dram, b), t_a[:, :, :]).then_inc(res_stored, 16)

            def load_residual(b):
                pool.wait_ge(res_stored, b * 16 + 16)
                pool.sem_inc(pool_passed, 1)
                pool.dma_start(t_r[:, :, :], token_rows(res_dram, b)).then_inc(r_loaded, 16)

            def load_next(b):
                pool.wait_ge(x1_stored, b * 16)
                pool.wait_ge(src_done, b * TT)
                pool.sem_inc(pool_passed, 1)
                pool.dma_start(xin[:, :, :], x[b, :, :].rearrange("(t p) d -> p t d", p=P)).then_inc(x_loaded, 16)
                pool.wait_ge(cT_full, b * 2)
                pool.sem_inc(pool_passed, 1)
                pool.dma_start(cin[:, :, :], ctx[b, :, :].rearrange("(t p) d -> p t d", p=P)).then_inc(c_loaded, 16)

            def ffn_input(b, idx, more):
                rsqrt(idx, 2)
                nc.gpsimd.tensor_copy(rstds[:, bass.ds(b * TT, TT)], rstd[2][:, :]).then_inc(keys_ready, 1)
                pool.wait_ge(dot_done, b * (TT + 2) + TT + 2)
                pool.sem_inc(pool_passed, 1)
                for t in range(TT):
                    nc.gpsimd.tensor_scalar(t_r[:, t, :], t_r[:, t, :], mv[2][:, t, 0:1], rstd[2][:, t:t + 1], ALU.subtract, ALU.mult).then_inc(xn_done, 1)
                pool.wait_ge(xn_done, b * TT + TT)
                nc.gpsimd.tensor_tensor(t_r[:, :, :], t_r[:, :, :], rows_bc[:, G1:G1 + 1, :].broadcast_to([P, TT, D]), ALU.mult).then_inc(xfm_done, 1)
                pool.wait_ge(xfm_done, b + 1)
                nc.gpsimd.tensor_tensor(t_r[:, :, :], t_r[:, :, :], rows_bc[:, B1:B1 + 1, :].broadcast_to([P, TT, D]), ALU.add).then_inc(xf_done, 1)
                pool.wait_ge(xf_done, b + 1)
                pool.sem_inc(pool_passed, 1)
                pool.dma_start(token_rows(xf_dram, b), t_r[:, :, :]).then_inc(xf_stored, 16)
                if more:
                    pool.wait_ge(xf_stored, b * 16 + 16)
                    load_residual(b + 1)

            nc.gpsimd.memset(pad_row[:, 0:2 * D], 0.0).then_inc(pool_ready, 1)
            nc.gpsimd.iota(pad_row[:, 2 * D:ROW].bitcast(int32), [[0, 1]], base=2 * NTOK, channel_multiplier=1).then_inc(pool_ready, 1)
            nc.gpsimd.memset(ones[:, :], 1.0).then_inc(pool_ready, 1)
            nc.gpsimd.memset(KS[0:100, 0, :, :].bitcast(fp32), 0.0).then_inc(stack_ready, 1)
            pool.wait_ge(stack_ready, 1)
            nc.gpsimd.memset(KS[96:98, 0, :, :].bitcast(fp32), 1.0).then_inc(stack_ready, 1)
            pool.wait_ge(stack_ready, 2)
            pool.wait_ge(pool_ready, POOL_CONSTS)
            pool.wait_ge(consts_ready, CONSTS)
            first_part(0, 0)
            load_next(1)
            residual(0)
            load_residual(0)
            nc.gpsimd.iota(thresholds[:, :], [[SLOT, NTOK // SLOT]], base=0, channel_multiplier=0, allow_small_or_imprecise_dtypes=True).then_inc(tok_id, 1)
            pool.wait_ge(pool_ready, POOL_CONSTS)
            nc.gpsimd.affine_select(out=before[:, :], in_=ones[:, :], compare_op=ALU.is_gt, fill=0.0,
                                    base=0, pattern=[[1, P]], channel_multiplier=-1).then_inc(tok_id, 1)
            first_part(1, 2)

            def turn(b, part):
                if part == "all":
                    load_next(b + 2)
                if part != "last":
                    residual(b + 1)
                if part == "all":
                    first_part(b + 2, ln_index(b, 0))
                ffn_input(b, ln_index(b, 2), part != "last")

            with pool.Fori(0, B - 2) as b:
                turn(b, "all")
            turn(B - 2, "next")
            turn(B - 1, "last")
            tail_pool(pool)

        def ln_index(b, l):
            if isinstance(b, int):
                return 4 + 3 * min(b, B - 2) + max(b - (B - 2), 0) + (l if b < B - 2 else 0)
            return b * 3 + 4 + l

        def act_program(act):
            act.wait_ge(gates_loaded, 32)
            nc.scalar.activation(tg[:, :], gates[:, :], ACT.Tanh).then_inc(gates_ready, 1)
            act.sem_inc(exp_done, 2)

            def side_work(task, i, b):
                if task == "xT":
                    act.wait_ge(xT_full, b * 2 + i + 1)
                    nc.scalar.activation(xT[:, i, :], side[:, :], ACT.Identity, accum_out=xsum[:, i:i + 1]).then_inc(xT_done, 1)
                elif task == "cT":
                    act.wait_ge(cT_full, b * 2 + i + 1)
                    nc.scalar.activation(cT[:, i, :], side[:, :], ACT.Identity).then_inc(cT_done, 1)
                elif task == "sT":
                    act.wait_ge(sT_full, b * 2 + i + 1)
                    nc.scalar.activation(srcT[:, i, :], side[:, :], ACT.Identity).then_inc(sT_done, 1)
                elif task in "qk":
                    j = i + 2 * (task == "k")
                    act.wait_ge(qk_full, b * 4 + j + 1)
                    wait(act, qk_stored[j % 2], b * 32 + 16 * (j // 2))
                    nc.scalar.activation(HL[:, j % 2, 0, :], side[:, :], ACT.Identity, bias=cols[:, 3 + j // 2, i:i + 1]).then_inc(hi_done, 1)

            def probabilities(b, n):
                act.wait_ge(sc_full, b * 32 + n + 1)
                act.wait_ge(pv_round, b * 8 + n // 4 + 1)
                nc.scalar.activation(probs[:, n % 8, :], sc[n % 2][:, :, :].rearrange("p a q -> p (a q)"), ACT.Exp, scale=SCALE).then_inc(exp_done, 1)

            for task in LEAD:
                side_work(*task)
            for n in range(-12, 8):
                if n >= 0:
                    probabilities(0, n)
                if n in LEAD_SIDE:
                    side_work(*LEAD_SIDE[n])

            def turn(b, part):
                for n in steps_of(part):
                    probabilities(b, n)
                    if n in SIDE and runs(*SIDE[n][::2], part):
                        side_work(SIDE[n][0], SIDE[n][1], b + SIDE[n][2])

            with act.Fori(0, B - 2) as b:
                turn(b, "all")
            turn(B - 2, "next")
            turn(B - 1, "last")
            tail_act(act)

        def dve_program(dve):
            dve.sem_inc(pv_round, 2)
            nc.vector.memset(KS[0:48, 1, :, :].bitcast(fp32), 0.0).then_inc(ks_ready, 1)
            nc.vector.memset(KS[96:100, 1, :, :].bitcast(fp32), 1.0).then_inc(ks_ready, 1)
            nc.vector.memset(V1[:, :, :, DH:2 * DH], 1.0).then_inc(ks_ready, 1)
            dve.wait_ge(ks_ready, 3)
            nc.vector.memset(KS[96:98, 1, :, :].bitcast(fp32), 0.0).then_inc(ks_ready, 1)

            def stats_of(idx, l, src):
                for t in range(TT):
                    nc.vector.bn_stats(stats[:, t, :], src[:, t, :]).then_inc(bn_done, 1)
                dve.wait_ge(bn_done, idx * (TT + 1) + TT)
                dve.sem_inc(bn_done, 1)
                for t in range(TT):
                    nc.vector.bn_aggr(mv[l][:, t, :], stats[:, t, :]).then_inc(mv_done, 1)

            def side_work(task, i, b):
                if task == "cT":
                    dve.wait_ge(cT_done, b * 2 + i + 1)
                    nc.vector.tensor_tensor_reduce(out=t1[:, :], in0=cT[:, i, :], in1=gkw_row[:, :], scale=1.0, scalar=0.0,
                                                   op0=ALU.mult, op1=ALU.add, accum_out=csum[:, i:i + 1]).then_inc(csum_done, 1)
                    dve.wait_ge(csum_done, b * 2 + i + 1)
                elif task == "gv":
                    dve.wait_ge(gv_full, b + 1)
                    nc.vector.tensor_tensor(g4[:, :], side[:, 0:2 * KD], bG[:, :], ALU.add).then_inc(g4_done, 1)
                    dve.wait_ge(g4_done, b + 1)
                    nc.vector.tensor_tensor(gk[:, :], g4[:, 0:KD], g4[:, KD:2 * KD], ALU.mult).then_inc(gk_done, 1)
                    dve.wait_ge(gk_done, b * 2 + 1)
                    nc.vector.tensor_tensor(gkb[:, :], gk[:, :], cols[:, 2, :], ALU.mult).then_inc(gk_done, 1)
                    dve.wait_ge(gk_done, b * 2 + 2)
                elif task == "Q":
                    dve.wait_ge(Q_full, b * 2 + i + 1)
                    nc.vector.scalar_tensor_tensor(t1[:, :], side[:, :], gkb[:, i:i + 1], C1[:, i, :], ALU.add, ALU.add).then_inc(t1_done, 1)
                    dve.wait_ge(t1_done, b * 2 + i + 1)
                elif task == "V":
                    dve.wait_ge(V_full, b * 2 + i + 1)
                    nc.vector.scalar_tensor_tensor(oT[:, i, :], side[:, :], gk[:, i:i + 1], t1[:, :], ALU.mult, ALU.add).then_inc(o_done, 1)
                    dve.wait_ge(o_done, b * 2 + i + 1)
                elif task == "Y":
                    dve.wait_ge(Y_full, b * 2 + i + 1)
                    dve.wait_ge(xb_done, b + 1)
                    r = xin[:, 2 * i:2 * i + 2, :].rearrange("p t d -> p (t d)")
                    nc.vector.scalar_tensor_tensor(r, side[:, :], tg[:, 0:1], r, ALU.mult, ALU.add).then_inc(x1_done, 1)
                elif task in "qk":
                    j = i + 2 * (task == "k")
                    dve.wait_ge(hi_done, b * 4 + j + 1)
                    nc.vector.scalar_tensor_tensor(HL[:, j % 2, 1, :], side[:, :], cols[:, 3 + j // 2, i:i + 1],
                                                   HL[:, j % 2, 0, :].bitcast(fp32), ALU.add, ALU.subtract).then_inc(lo_done, 1)
                elif task == "v":
                    dve.wait_ge(v_full, b * 2 + i + 1)
                    nc.vector.tensor_tensor(V1[:, 2 * i:2 * i + 2, :, 0:DH], side[:, :].rearrange("p (t h d) -> p t h d", t=2, h=H),
                                            rows_bc[:, BV:BV + 1, :].rearrange("p o (h d) -> p o h d", h=H).broadcast_to([P, 2, H, DH]), ALU.add).then_inc(v_done, 1)
                elif task == "O":
                    dve.wait_ge(O_full, b * 2 + i + 1)
                    dve.wait_ge(r_loaded, b * 16 + 16)
                    r = t_r[:, 2 * i:2 * i + 2, :].rearrange("p t d -> p (t d)")
                    nc.vector.tensor_tensor(r, side[:, :], r, ALU.add).then_inc(r_done, 1)

            def x1_stats(b, idx):
                dve.wait_ge(x1_done, b * 2 + 2)
                stats_of(idx, 1, xin)

            def r_stats(b, idx):
                dve.wait_ge(r_done, b * 2 + 2)
                stats_of(idx, 2, t_r)
                for t in range(TT):
                    nc.vector.tensor_tensor_reduce(out=t1[:, 0:D], in0=t_r[:, t, :], in1=rows_bc[:, GRW, :], scale=1.0, scalar=0.0,
                                                   op0=ALU.mult, op1=ALU.add, accum_out=kb[:, t:t + 1]).then_inc(dot_done, 1)
                    dve.wait_ge(dot_done, b * (TT + 2) + t + 1)
                dve.wait_ge(mv_done, idx * TT + TT)
                nc.vector.tensor_copy(dots[:, bass.ds(b * TT, TT)], kb[:, :]).then_inc(dot_done, 1)
                nc.vector.tensor_copy(means[:, bass.ds(b * TT, TT)], mv[2][:, :, 0]).then_inc(dot_done, 1)

            def row_maxima(b, n):
                for m in (2 * n + 24, 2 * n + 25):
                    dve.wait_ge(A_full, b * 64 + m + 1)
                    nc.vector.reduce_max(mx[:, m % 16:m % 16 + 1], amax[m % 2][:, :], AX.X).then_inc(max_done, 1)
                if n % 8 == 3:
                    k = (n + 13) // 8
                    dve.wait_ge(max_done, b * 64 + 16 * k)
                    nc.vector.tensor_scalar(mneg[:, 0:16], mx[:, :], -1.0, None, ALU.mult).then_inc(mneg_done, 1)
                    dve.wait_ge(mneg_done, b * 2 * G + 2 * k - 1)
                    nc.vector.scalar_tensor_tensor(mneg[:, 16:32], mx[:, :], -1.0, mneg[:, 0:16].bitcast(fp32), ALU.mult, ALU.subtract).then_inc(mneg_done, 1)
                    dve.wait_ge(mneg_done, b * 2 * G + 2 * k)
                    wait(dve, m_stored, b * 16 * G + 16 * (k - 2))
                    nc.vector.transpose(mT[:, (k - 1) % 2, :], mneg[:, :].bitcast(fp32)).then_inc(mT_done, 1)

            def group_out(b, g):
                gg = g % 2
                dve.wait_ge(pv_round, b * 8 + 2 * g + 2 + 2)
                nc.vector.transpose(av[:, :], pv[:, :]).then_inc(av_done, 1)
                dve.wait_ge(av_done, b * G + g + 1)
                av_v = av[:, :].rearrange("p (n d) -> p n d", d=32)
                nc.vector.reciprocal(rec[:, :], av_v[:, :, DH]).then_inc(rec_done, 1)
                dve.wait_ge(rec_done, b * G + g + 1)
                nc.vector.tensor_tensor(an[:, :, gg, :], av_v[:, :, 0:DH], rec[:, :].unsqueeze(2).broadcast_to([P, S // 32, DH]), ALU.mult).then_inc(an_done, 1)
                dve.wait_ge(an_done, b * G + g + 1)
                if gg == 1:
                    nc.vector.transpose(aT[:, g // 2, :], an[:, :, :, :].rearrange("p n g d -> p (n g d)")).then_inc(aT_done, 1)
                    dve.wait_ge(aT_done, b * 2 + g // 2 + 1)

            dve.wait_ge(x_loaded, 16)
            stats_of(0, 0, xin)
            dve.wait_ge(w_loaded, W_LOADS * 16)
            dve.wait_ge(gates_ready, 1)
            for row, g in ((BO, 0), (G2, 1), (B2, 1)):
                nc.vector.tensor_scalar(rows_bc[:, row, :], rows_bc[:, row, :], tg[:, g:g + 1], None, ALU.mult).then_inc(consts_ready, 1)
            nc.vector.reduce_sum(gsum[:, 0:1], t1[:, :], AX.X).then_inc(consts_ready, 1)
            nc.vector.reduce_sum(gsum[:, 1:2], gkw_row[:, :], AX.X).then_inc(consts_ready, 1)
            for c in range(KD):
                nc.vector.tensor_scalar(C1[:, c, :], t1[:, :], cols[:, 0, c:c + 1], None, ALU.mult).then_inc(consts_ready, 1)
            nc.vector.tensor_tensor(rows_bc[:, GRW, :], rows_bc[:, G1, :], rows_bc[:, RW, :], ALU.mult).then_inc(consts_ready, 1)
            dve.wait_ge(consts_ready, 8)
            for i in range(2):
                nc.vector.tensor_scalar(bG[:, KD * i:KD * (i + 1)], cols[:, i, :], gsum[:, i:i + 1], None, ALU.mult).then_inc(consts_ready, 1)
            nc.vector.reduce_sum(gsum[:, 2:3], rows_bc[:, GRW, :], AX.X).then_inc(consts_ready, 1)
            nc.vector.tensor_tensor_reduce(out=t1[:, 0:D], in0=rows_bc[:, B1, :], in1=rows_bc[:, RW, :], scale=1.0, scalar=rb_col[:, 0:1],
                                           op0=ALU.mult, op1=ALU.add, accum_out=gsum[:, 3:4]).then_inc(consts_ready, 1)
            dve.wait_ge(consts_ready, CONSTS)

            for task in LEAD:
                side_work(*task)
                if task == ("Y", 1, 0):
                    x1_stats(0, 1)
            dve.wait_ge(x_loaded, 32)
            stats_of(2, 0, xin)
            for n in range(-12, 8):
                row_maxima(0, n)
                if n in LEAD_SIDE:
                    side_work(*LEAD_SIDE[n])
                    if LEAD_SIDE[n] == ("Y", 1, 1):
                        x1_stats(1, 3)

            def turn(b, part):
                for n in steps_of(part):
                    if part != "last" or n < LAST_MAX:
                        row_maxima(b, n)
                    if n in SIDE and runs(*SIDE[n][::2], part):
                        side_work(SIDE[n][0], SIDE[n][1], b + SIDE[n][2])
                    if part == "all" and n == 10:
                        dve.wait_ge(x_loaded, b * 16 + 48)
                        stats_of(ln_index(b, 0), 0, xin)
                    if part == "all" and n == 30:
                        x1_stats(b + 2, ln_index(b, 1))
                    if n % 8 == 4 and n > 8:
                        group_out(b, (n - 12) // 8)
                if part == "last":
                    group_out(b, G - 1)
                    side_work("O", 0, b)
                    side_work("O", 1, b)
                r_stats(b, ln_index(b, 2))

            with dve.Fori(0, B - 2) as b:
                turn(b, "all")
            turn(B - 2, "next")
            turn(B - 1, "last")
            tail_dve(dve)

        def pe_program(pe):
            before_side = [None]

            def transposes(src, c, full):
                for t in range(TT):
                    last = nc.tensor.transpose(side[:, t * P:(t + 1) * P], src[:, t, c * P:(c + 1) * P], ident[:, :])
                last.then_inc(full, 1)

            def features_out(w, c, src, full):
                for k in range(KD):
                    last = nc.tensor.matmul(side[:, :], w[:, k, c * P:(c + 1) * P], src[:, k, :], start=(k == 0), stop=(k == KD - 1))
                last.then_inc(full, 1)

            def tokens_out(w, j, src, full):
                for tt in range(2):
                    t = 2 * j + tt
                    for k in range(KD):
                        last = nc.tensor.matmul(side[:, tt * D:(tt + 1) * D], src[:, k, t * P:(t + 1) * P], w[:, k, :], start=(k == 0), stop=(k == KD - 1))
                last.then_inc(full, 1)

            def side_work(task, i, b):
                if before_side[0]:
                    wait(pe, *before_side[0])
                before_side[0] = release(task, i, b)
                if task == "xT":
                    pe.wait_ge(xg_done, b * TT + TT)
                    transposes(t_a, i, xT_full)
                elif task == "cT":
                    pe.wait_ge(c_loaded, b * 16 + 16)
                    transposes(cin, i, cT_full)
                elif task == "gv":
                    pe.wait_ge(xT_done, b * 2 + 2)
                    pe.wait_ge(csum_done, b * 2 + 2)
                    for a, (w, s) in enumerate((("wq", xsum), ("wk", csum))):
                        for c in range(KD):
                            for k in range(KD):
                                last = nc.tensor.matmul(side[:, a * KD + c:a * KD + c + 1], w_sb[w][:, k, c * P:(c + 1) * P], s[:, k:k + 1], start=(k == 0), stop=(k == KD - 1))
                    last.then_inc(gv_full, 1)
                elif task == "Q":
                    features_out(w_sb["wq"], i, xT, Q_full)
                elif task == "V":
                    features_out(w_sb["wv"], i, cT, V_full)
                elif task == "Y":
                    pe.wait_ge(o_done, b * 2 + 2)
                    tokens_out(w_sb["wo"], i, oT, Y_full)
                elif task == "sT":
                    pe.wait_ge(src_done, b * TT + TT)
                    transposes(t_a, i, sT_full)
                elif task in "qk":
                    pe.wait_ge(sT_done, b * 2 + 2)
                    features_out(w_sb["W" + task], i, srcT, qk_full)
                elif task == "v":
                    tokens_out(w_sb["Wv"], i, srcT, v_full)
                elif task == "O":
                    pe.wait_ge(aT_done, b * 2 + 2)
                    tokens_out(w_sb["Wo"], i, aT, O_full)

            def scores_for_maxima(b, n):
                for m in (2 * n + 24, 2 * n + 25):
                    g, hh, chunk = m // 16 % G, m // 4 % 4, m % 4
                    pair, c = pair_of(g, hh)
                    if m % 16 == 0:
                        pe.wait_ge(stack_loaded[g], (b + m // 64) * 192 + 192)
                    wait(pe, max_done, b * 64 + m - 1)
                    nc.tensor.matmul(amax[m % 2][:, :], QS[0:96, pair, chunk * P:(chunk + 1) * P], KS[0:96, c, pair, :], start=True, stop=True).then_inc(A_full, 1)

            def scores(b, n):
                g, r = n // 8 % G, n // 4
                pair, c = pair_of(g, n % 4)
                if n % 8 == 0:
                    pe.wait_ge(m_loaded[g % 2], (b + n // 32) * 64 + 32 * (g // 2 + 1))
                pe.wait_ge(exp_done, b * 32 + n + 1)
                for a in range(2):
                    kc = 2 * (r % 2) + a
                    last = nc.tensor.matmul(sc[n % 2][:, a, :], KS[0:100, c, pair, kc * P:(kc + 1) * P], QS[0:100, pair, :], start=True, stop=True)
                last.then_inc(sc_full, 1)

            def weighted_values(b, r):
                g = r // 2 % G
                pe.wait_ge(exp_done, b * 32 + 4 * (r + 1) + 2)
                if r % 2 == 0:
                    if r % 8 == 0:
                        pe.wait_ge(v_done, (b + r // 8) * 2 + 2)
                    wait(pe, av_done, b * G + r // 2)
                for a in range(2):
                    kc = 2 * (r % 2) + a
                    for hh in range(HG):
                        pair, c = pair_of(g, hh)
                        last = nc.tensor.matmul(pv[32 * hh:32 * hh + 32, :], V1[:, kc, 8 * c + pair, :],
                                                probs[:, (4 * r + hh) % 8, a * 512:(a + 1) * 512], start=(kc == 0), stop=(kc == TT - 1))
                last.then_inc(pv_round, 1)

            def step(b, n):
                scores(b, n)
                if n % 4 == 3 and not (isinstance(b, int) and b == 0 and n == 3):
                    weighted_values(b, n // 4 - 1)

            pe.wait_ge(pool_ready, 3)
            pe.wait_ge(consts_ready, CONSTS)
            for task in LEAD:
                if task == ("sT", 0, 0):
                    pe.wait_ge(W_loaded, W_LOADS2 * 16)
                side_work(*task)
            pe.wait_ge(stack_ready, 2)
            pe.wait_ge(ks_ready, 4)
            for n in range(-12, 8):
                if n >= 0:
                    step(0, n)
                scores_for_maxima(0, n)
                if n in LEAD_SIDE:
                    side_work(*LEAD_SIDE[n])
            wait(pe, *before_side[0])

            def turn(b, part):
                for n in steps_of(part):
                    step(b, n)
                    if part != "last" or n < LAST_MAX:
                        scores_for_maxima(b, n)
                    if n in SIDE and runs(*SIDE[n][::2], part):
                        side_work(SIDE[n][0], SIDE[n][1], b + SIDE[n][2])
                if part == "last":
                    weighted_values(b, 7)
                    side_work("O", 0, b)
                    side_work("O", 1, b)
                wait(pe, *before_side[0])
                before_side[0] = None

            before_side[0] = None
            with pe.Fori(0, B - 2) as b:
                turn(b, "all")
            turn(B - 2, "next")
            turn(B - 1, "last")
            tail_pe(pe)

        W_LOADS, W_LOADS2 = 1 + 2 + 5 + 8 + 1 + 4, 3 + 16

        hid_bank = [sc[0][:, 0, 0:SLOT], sc[0][:, 1, 0:SLOT], sc[1][:, 0, 0:SLOT], sc[1][:, 1, 0:SLOT]]

        def expert_slots(eng):
            first = 0
            for e in range(E):
                end = eng.value_load(ends_i[0:1, e:e + 1], min_val=e + 1, max_val=MAXS - (E - 1 - e))
                yield e, first, end
                first = end

        def tail_sp(sp):
            sp.wait_ge(pv_round, B * 8 + 2)
            sp.wait_ge(x1_stored, B * 16)
            sp.wait_ge(xf_stored, B * 16)
            for h, t in ((0, x1_dram), (1, xf_dram)):
                at = D * (1 - h)
                sp.dma_start(routed[:, :, at:at + D], t.rearrange("(t p) d -> p t d", p=P)).then_inc(tok_loaded, 16)
            for e in range(E):
                sp.dma_start(W2_sb[:, e * NF:(e + 1) * NF, :], W2[e, :, :].rearrange("(k p) d -> p k d", p=P)).then_inc(w2_loaded, 16)
            sp.dma_start(b2_bc[:, :, :], b2.partition_broadcast(P)).then_inc(w2_loaded, 16)
            sp.wait_ge(ends_ready, 1)
            sp.wait_ge(scattered, 16 * NT)
            for e, first, end in expert_slots(sp):
                with sp.Fori(first, end) as i:
                    rows = slots_dram[bass.ds(i * SLOT, SLOT), :].rearrange("(a p) r -> p a r", p=P)
                    sp.wait_ge(slot_x_free, i + 1)
                    sp.dma_start(slot_x[:, :, :], rows[:, :, 0:D]).then_inc(slot_x_loaded, 16)
                    sp.wait_ge(slot_row_free, i + 1)
                    sp.dma_start(slot_row[:, :, :], rows).then_inc(slot_row_loaded, 16)

        def tail_pool(pool):
            pool.wait_ge(pv_round, B * 8 + 2)
            nc.gpsimd.iota(routed[:, :, 2 * D:ROW].bitcast(int32), [[P, NT], [0, 1]], base=0, channel_multiplier=1).then_inc(tok_id, 1)
            pool.wait_ge(tok_id, 3)
            pool.wait_ge(filled, MAXS * SA * 16)
            pool.wait_ge(tok_loaded, 32)
            pool.wait_ge(pos_ready, 1)
            for t in range(NT):
                nc.gpsimd.indirect_dma_start(slots_dram, bass.IndirectOffsetOnAxis(ap=pos_i[:, t:t + 1], axis=0), routed[:, t, :], None).then_inc(scattered, 16)
            pool.wait_ge(w2_loaded, W2_LOADS * 16)
            pool.sem_inc(slot_x_free, 1)
            pool.sem_inc(slot_row_free, 1)
            for e, first, end in expert_slots(pool):
                with pool.Fori(first, end) as i:
                    pool.wait_ge(slot_row_loaded, i * 16 + 16)
                    nc.gpsimd.tensor_tensor(slot_row[:, :, 0:D], slot_row[:, :, 0:D], b2_bc[:, e:e + 1, :].broadcast_to([P, SA, D]), ALU.add).then_inc(slot_res, 1)
                    nc.gpsimd.tensor_tensor(slot_row[:, :, D:2 * D], slot_row[:, :, D:2 * D], rows_bc[:, B2:B2 + 1, :].broadcast_to([P, SA, D]), ALU.add).then_inc(slot_res, 1)
                    pool.wait_ge(slot_mv, i * SA + SA)
                    pool.sem_inc(pool_passed, 1)
                    nc.gpsimd.tensor_scalar(var_eps[:, 0:SA], mv[0][:, 0:SA, 1], EPS, None, ALU.add).then_inc(slot_ve, 1)
                    pool.wait_ge(slot_ve, i + 1)
                    nc.gpsimd.tensor_tensor(rstd[0][:, 0:SA], var_eps[:, 0:SA], mhalf[:, 0:SA], ALU.pow).then_inc(slot_rstd, 1)
                    pool.wait_ge(slot_out, i * 2 + 2)
                    pool.sem_inc(slot_sent, 1)
                    for a in range(SA):
                        nc.gpsimd.indirect_dma_start(out_rows, bass.IndirectOffsetOnAxis(ap=slot_row[:, a, 2 * D:ROW].bitcast(int32), axis=0), slot_z[:, a, :], None,
                                                     bounds_check=NTOK - 1, oob_is_err=False).then_inc(out_stored, 16)
                    pool.wait_ge(out_stored, i * 32 + 32)
                    pool.sem_inc(slot_row_free, 1)

        def tail_act(act):
            act.wait_ge(w2_loaded, W2_LOADS * 16)
            act.wait_ge(ends_ready, 1)
            for e, first, end in expert_slots(act):
                with act.Fori(first, end) as i:
                    act.wait_ge(slot_T, i + 1)
                    nc.scalar.activation(slot_xT[:, :, :].rearrange("p k n -> p (k n)"), side[:, :], ACT.Identity).then_inc(slot_xT_done, 1)
                    for f in range(0, NF, 2):
                        act.wait_ge(hid_full, i * NF + f + 1)
                        nc.scalar.activation(hid[:, f, :], hid_bank[f % 4], ACT.Relu, bias=b1_col[:, e * NF + f:e * NF + f + 1]).then_inc(hid_even, 1)

        def tail_dve(dve):
            dve.wait_ge(keys_ready, B)
            dve.wait_ge(dot_done, B * (TT + 2))
            dve.wait_ge(bn_done, B * 3 * (TT + 1))
            step = [0]

            def link(ins):
                step[0] += 1
                ins.then_inc(route_step, 1)
                dve.wait_ge(route_step, step[0])

            link(nc.vector.scalar_tensor_tensor(keys[:, :], means[:, :], gsum[:, 2:3], dots[:, :], ALU.mult, ALU.subtract))
            link(nc.vector.scalar_tensor_tensor(keys[:, :], keys[:, :], -1.0, rstds[:, :], ALU.mult, ALU.mult))
            link(nc.vector.tensor_scalar(keys[:, :], keys[:, :], gsum[:, 3:4], None, ALU.add))
            link(nc.vector.tensor_copy(r_int[:, :], keys[:, :]))
            link(nc.vector.tensor_copy(r_f[:, 0, :], r_int[:, :]))
            link(nc.vector.tensor_tensor(r_f[:, 1, :], r_f[:, 0, :], keys[:, :], ALU.is_gt))
            link(nc.vector.tensor_tensor(r_f[:, 2, :], r_f[:, 0, :], r_f[:, 1, :], ALU.subtract))
            link(nc.vector.tensor_copy(r_int[:, :], r_f[:, 2, :]))
            link(nc.vector.tensor_scalar(r_int2[:, :], r_int[:, :], E - 1, None, ALU.bitwise_and))
            link(nc.vector.tensor_copy(r_f[:, 3, :], r_int2[:, :]))
            for e in range(E):
                nc.vector.tensor_scalar(onehot[:, e, :], r_f[:, 3, :], float(e), None, ALU.is_equal).then_inc(onehot_done, 1)
            dve.wait_ge(counts_full, 1)
            link(nc.vector.tensor_copy(counts[:, :, :, :].rearrange("p a e t -> p (a e t)"), pv[:, 0:2 * E * NT]))
            for e in range(E):
                link(nc.vector.tensor_tensor_scan(upto[:, e, :], ones[:, 0:NT], counts[:, 1, e, :], 0.0, ALU.mult, ALU.add))
            for e in range(E):
                link(nc.vector.tensor_scalar(n_over[:, e, :], thresholds[:, :], upto[:, e, NT - 1:NT], None, ALU.is_lt))
            link(nc.vector.reduce_sum(n_slots[:, :], n_over[:, :, :], AX.X))
            link(nc.vector.tensor_scalar(n_slots[:, :], n_slots[:, :], 1.0, None, ALU.max))
            link(nc.vector.tensor_tensor_scan(ends[:, :], ones[:, 0:E], n_slots[:, :], 0.0, ALU.mult, ALU.add))
            nc.vector.tensor_copy(ends_i[:, :], ends[:, :]).then_inc(ends_ready, 1)
            link(nc.vector.tensor_tensor(base[:, :], ends[:, :], n_slots[:, :], ALU.subtract))
            link(nc.vector.tensor_scalar(base[:, :], base[:, :], float(SLOT), None, ALU.mult))
            link(nc.vector.tensor_tensor(place[:, :, :], upto[:, :, :], counts[:, 1, :, :], ALU.subtract))
            link(nc.vector.tensor_tensor(place[:, :, :], place[:, :, :], counts[:, 0, :, :], ALU.add))
            link(nc.vector.tensor_tensor(place[:, :, :], place[:, :, :], base[:, :].unsqueeze(2).broadcast_to([P, E, NT]), ALU.add))
            link(nc.vector.tensor_tensor(place[:, :, :], place[:, :, :], onehot[:, :, :], ALU.mult))
            link(nc.vector.reduce_sum(pos_f[:, :], place[:, :, :].rearrange("p e t -> p t e"), AX.X))
            nc.vector.tensor_copy(pos_i[:, :], pos_f[:, :]).then_inc(pos_ready, 1)

            dve.wait_ge(w2_loaded, W2_LOADS * 16)
            dve.wait_ge(ends_ready, 1)
            dve.sem_inc(y_free, 1)
            for e, first, end in expert_slots(dve):
                with dve.Fori(first, end) as i:
                    for f in range(1, NF, 2):
                        dve.wait_ge(hid_full, i * NF + f + 1)
                        nc.vector.tensor_scalar(hid[:, f, :], hid_bank[f % 4], b1_col[:, e * NF + f:e * NF + f + 1], 0.0, ALU.add, ALU.max).then_inc(hid_odd, 1)
                    dve.wait_ge(slot_res, i * 2 + 2)
                    dve.wait_ge(y_full, i + 1)
                    nc.vector.tensor_tensor(slot_z[:, 0, :], amax[0][:, 0:D], slot_row[:, 0, 0:D], ALU.add).then_inc(z_step, 1)
                    nc.vector.tensor_tensor(slot_z[:, 1, :], amax[1][:, 0:D], slot_row[:, 1, 0:D], ALU.add).then_inc(y_free, 1)
                    dve.wait_ge(z_step, i * 8 + 1)
                    dve.wait_ge(y_free, i + 2)
                    for a in range(SA):
                        nc.vector.bn_stats(stats[:, a, :], slot_z[:, a, :]).then_inc(z_step, 1)
                    dve.wait_ge(z_step, i * 8 + 3)
                    dve.sem_inc(z_step, 1)
                    for a in range(SA):
                        nc.vector.bn_aggr(mv[0][:, a, :], stats[:, a, :]).then_inc(slot_mv, 1)
                    dve.wait_ge(slot_rstd, i + 1)
                    for a in range(SA):
                        nc.vector.tensor_scalar(slot_z[:, a, :], slot_z[:, a, :], mv[0][:, a, 0:1], rstd[0][:, a:a + 1], ALU.subtract, ALU.mult).then_inc(z_step, 1)
                    for a in range(SA):
                        dve.wait_ge(z_step, i * 8 + 5 + a)
                        nc.vector.tensor_tensor(slot_z[:, a, :], slot_z[:, a, :], rows_bc[:, G2, :], ALU.mult).then_inc(z_step, 1)
                    for a in range(SA):
                        dve.wait_ge(z_step, i * 8 + 7 + a)
                        nc.vector.tensor_tensor(slot_z[:, a, :], slot_z[:, a, :], slot_row[:, a, D:2 * D], ALU.add).then_inc(slot_out, 1)

        def tail_pe(pe):
            pe.wait_ge(tok_id, 2)
            pe.wait_ge(onehot_done, E)
            oh = onehot[:, :, :].rearrange("p e t -> p (e t)")
            nc.tensor.matmul(pv[:, 0:E * NT], before[:, :], oh, start=True, stop=True)
            nc.tensor.matmul(pv[:, E * NT:2 * E * NT], ones[:, :], oh, start=True, stop=True).then_inc(counts_full, 1)
            pe.wait_ge(w2_loaded, W2_LOADS * 16)
            pe.wait_ge(ends_ready, 1)
            pe.sem_inc(hid_even, 2)
            pe.sem_inc(hid_odd, 2)
            for e, first, end in expert_slots(pe):
                with pe.Fori(first, end) as i:
                    pe.wait_ge(slot_x_loaded, i * 16 + 16)
                    for k in range(KD):
                        for a in range(SA):
                            last = nc.tensor.transpose(side[:, k * SLOT + a * P:k * SLOT + (a + 1) * P], slot_x[:, a, k * P:(k + 1) * P], ident[:, :])
                    last.then_inc(slot_T, 1)
                    pe.wait_ge(slot_xT_done, i + 1)
                    pe.sem_inc(slot_x_free, 1)

                    def up(f):
                        s = (hid_even, hid_odd)[f % 2]
                        pe.wait_ge(s, i * (NF // 2) + f // 2 + 1)
                        for k in range(KD):
                            last = nc.tensor.matmul(hid_bank[f % 4], W1_sb[:, e * KD + k, f * P:(f + 1) * P], slot_xT[:, k, :], start=(k == 0), stop=(k == KD - 1))
                        last.then_inc(hid_full, 1)

                    def down(f):
                        s = (hid_even, hid_odd)[f % 2]
                        pe.wait_ge(s, i * (NF // 2) + f // 2 + 3)
                        if f == 0:
                            pe.wait_ge(y_free, i + 1)
                        for a in range(SA):
                            last = nc.tensor.matmul(amax[a][:, 0:D], hid[:, f, a * P:(a + 1) * P], W2_sb[:, e * NF + f, :], start=(f == 0), stop=(f == NF - 1))
                        if f == NF - 1:
                            last.then_inc(y_full, 1)

                    for f in range(NF + 2):
                        if f < NF:
                            up(f)
                        if f >= 2:
                            down(f - 2)
            pe.wait_ge(slot_sent, end)
            pe.wait_ge(slot_x_free, end + 1)
            pe.wait_ge(slot_row_free, end + 1)


        block = es.enter_context(nc.Block())

        @block.sync
        def _(sp):
            sp_program(sp)

        @block.gpsimd
        def _(pool):
            pool_program(pool)

        @block.scalar
        def _(act):
            act_program(act)

        @block.vector
        def _(dve):
            dve_program(dve)

        @block.tensor
        def _(pe):
            pe_program(pe)


_INS = ["x", "ctx_1024", "g_xattn", "g_ffn",
        "L0_xattn_wq", "L0_xattn_bq", "L0_xattn_wk", "L0_xattn_bk", "L0_xattn_wv", "L0_xattn_bv",
        "L0_xattn_gqw", "L0_xattn_gkw", "L0_xattn_wo", "L0_xattn_bo",
        "L0_ffn_Wq", "L0_ffn_bq", "L0_ffn_Wk", "L0_ffn_bk", "L0_ffn_Wv", "L0_ffn_bv", "L0_ffn_Wo", "L0_ffn_bo",
        "L0_ffn_router_w", "L0_ffn_router_b", "L0_ffn_W1", "L0_ffn_b1", "L0_ffn_W2", "L0_ffn_b2",
        "L0_ffn_ln1_g", "L0_ffn_ln1_b", "L0_ffn_ln2_g", "L0_ffn_ln2_b"]


def kernel(**inputs):
    import concourse.bacc as bacc
    from concourse.bass_utils import run_bass_kernel_spmd

    nc = bacc.Bacc("TRN2", target_bir_lowering=False, num_devices=1)
    arrays, args = {}, []
    for name in _INS:
        a = np.ascontiguousarray(inputs[name])
        arrays[f"in_{name}"] = a
        args.append(nc.dram_tensor(f"in_{name}", a.shape, mybir.dt.from_np(a.dtype), kind="ExternalInput").ap())
    out = nc.dram_tensor("out_dram", (4, 512, 256), fp32, kind="ExternalOutput").ap()
    gated_block_kernel(nc, *args, out)
    r = run_bass_kernel_spmd(nc, [arrays], core_ids=[0])
    return r.results[0]["out_dram"]
```

```python
import numpy as np
import concourse.bass as bass
from concourse import mybir
from contextlib import ExitStack

fp32 = mybir.dt.float32
fp32r = mybir.dt.float32r
int32 = mybir.dt.int32
uint32 = mybir.dt.uint32
ALU = mybir.AluOpType
ACT = mybir.ActivationFunctionType
AX = mybir.AxisListType


def gated_block_kernel(nc, x, ctx, g_xattn, g_ffn, wq, bq, wk, bk, wv, bv, gqw, gkw, wo, bo,
                       Wq, Bq, Wk, Bk, Wv, Bv, Wo, Bo, router_w, router_b, W1, b1, W2, b2,
                       ln1_g, ln1_b, ln2_g, ln2_b, out):
    B, S, D = x.shape
    H = 16
    DH = D // H
    E, _, F = W1.shape
    P = 128
    TT = S // P
    KD = D // P
    NT = B * TT
    NTOK = B * S
    NF = F // P
    EPS = 1e-5
    SCALE = DH ** -0.5
    G = 4
    HG = H // G
    SLOT = 256
    SA = SLOT // P
    MAXS = NTOK // SLOT + E - 1
    COLS = (MAXS + 1) * SA
    PAD = 2 * NTOK

    qk_dram = nc.dram_tensor("qk_dram", (4, 2, P, S), fp32, kind="Internal").ap()
    m_dram = nc.dram_tensor("m_dram", (2, 32, 4, 32), fp32, kind="Internal").ap()
    x1_dram = nc.dram_tensor("x1_dram", (NTOK, D), fp32, kind="Internal").ap()
    res_dram = nc.dram_tensor("res_dram", (NTOK, D), fp32, kind="Internal").ap()
    xf_dram = nc.dram_tensor("xf_dram", (NTOK, D), fp32, kind="Internal").ap()

    es = ExitStack()
    with es:
        def sb(name, shape, dt=fp32):
            return es.enter_context(nc.sbuf_tensor(name, shape, dt))

        def psum(name, shape):
            return es.enter_context(nc.psum_tensor(name, shape, fp32))

        def sem(name):
            return es.enter_context(nc.semaphore(name))

        cols = sb("cols", [P, 5, KD])
        gqw_col = sb("gqw_col", [P, TT])
        gkw_row = sb("gkw_row", [P, S])
        rows_bc = sb("rows_bc", [P, 9, D])
        BO, BO2, BV, G1, B1, RW, G2, B2, GRW = range(9)
        b1_col = sb("b1_col", [P, E * NF])
        rb_col = sb("rb_col", [P, 1])
        gates = sb("gates", [P, 2])
        tg = sb("tg", [P, 2])
        mhalf = sb("mhalf", [P, TT])
        gsum = sb("gsum", [P, 4])
        bG = sb("bG", [P, 2 * KD])
        ident = sb("ident", [P, P])
        t_a = sb("t_a", [P, TT, D])
        t_r = sb("t_r", [P, TT, D])
        aT = sb("aT", [P, KD, S])
        t1 = sb("t1", [P, S])
        xsum = sb("xsum", [P, KD])
        csum = sb("csum", [P, KD])
        g4 = sb("g4", [P, 2 * KD])
        gk = sb("gk", [P, KD])
        gkb = sb("gkb", [P, KD])
        mx = sb("mx", [P, 16])
        mneg = sb("mneg", [P, 32], fp32r)
        mT = sb("mT", [P, 2, 32])
        av = sb("av", [P, S])
        rec = sb("rec", [P, S // 32])
        an = sb("an", [P, S // 32, 2, DH])
        stats = sb("stats", [P, TT, 6])
        mv = [sb(f"mv{l}", [P, TT, 2]) for l in range(3)]
        var_eps = sb("var_eps", [P, TT])
        rstd = [sb(f"rstd{l}", [P, TT]) for l in range(3)]
        rg = sb("rg", [P, TT])
        kb = sb("kb", [P, TT])
        dots, means, rstds = sb("dots", [P, NT]), sb("means", [P, NT]), sb("rstds", [P, NT])
        keys = sb("keys", [P, NT])
        b2_bc = sb("b2_bc", [P, E, D])
        with ExitStack() as attention:
            def att(name, shape, dt=fp32):
                return attention.enter_context(nc.sbuf_tensor(name, shape, dt))

            W1_sb = att("W1_sb", [P, E * KD, F])
            xc = att("xc", [P, 2 * TT, D])
            xcT = att("xcT", [P, 2 * KD, S])
            oC = att("oC", [P, 2 * KD, S])
            w_first = att("w_first", [P, 4 * KD, D])
            probs = att("probs", [P, 8, 1024])
            w_second = att("w_second", [P, 4 * KD, D])
            V1 = att("V1", [P, TT, H, 2 * DH])
            srcT = att("srcT", [P, KD, S])
            HL = att("HL", [P, 2, 2, S], fp32r)
            QS = att("QS", [P, H // 2, S], fp32r)
            KS = att("KS", [P, 2, H // 2, S], fp32r)
        w_sb = {n: w_first[:, KD * i:KD * (i + 1), :] for i, n in enumerate(("wq", "wk", "wv", "wo"))}
        w_sb.update({n: w_second[:, KD * i:KD * (i + 1), :] for i, n in enumerate(("Wq", "Wk", "Wv", "Wo"))})
        C1 = oC[:, KD:2 * KD, :]
        xin, cin = xc[:, 0:TT, :], xc[:, TT:2 * TT, :]
        xT, cT = xcT[:, 0:KD, :], xcT[:, KD:2 * KD, :]
        oT = oC[:, 0:KD, :]
        W2_sb = [xc, xcT[:, :, :].rearrange("p k (h d) -> p (k h) d", d=D), oC[:, :, :].rearrange("p k (h d) -> p (k h) d", d=D), w_first]
        hid = t_a[:, :, :].rearrange("p t d -> p (t d)").rearrange("p (r f n) -> p r f n", r=2, f=2)
        W1_lo = sb("W1_lo", [P, E * KD, F], fp32r)
        W2_lo = sb("W2_lo", [P, E * NF, D], fp32r)
        W1_hi = sb("W1_hi", [P, E * KD, F], fp32r)
        hid_lo, hid_hi = sb("hid_lo", [P, NF, SLOT], fp32r), sb("hid_hi", [P, NF, SLOT], fp32r)
        lo_hot = hid_hi[:, :, :].rearrange("p f n -> p (f n)").rearrange("p (t n) -> p t n", n=P)
        slot_xT = sb("slot_xT", [P, 2, KD, SLOT], fp32r)
        W2_hi = sb("W2_hi", [P, E * NF, D], fp32r)
        before = sb("before", [P, P])
        ones = sb("ones", [P, P])
        thresholds = sb("thresholds", [P, NTOK // SLOT])
        lo_is, hi_is = sb("lo_is", [P, P]), sb("hi_is", [P, COLS])
        token_id = sb("token_id", [P, NT])
        slot_x = sb("slot_x", [P, SA, D])
        slot_z = sb("slot_z", [P, SA, D])
        slot_xb = sb("slot_xb", [P, SA, D])
        slot_x1 = sb("slot_x1", [P, SA, D])
        hi_hot = sb("hi_hot", [P, 2, NT, COLS], fp32r)
        lo_f, hi_f = sb("lo_f", [P, NT]), sb("hi_f", [P, NT])
        ids_f, load_f = sb("ids_f", [P, COLS]), sb("load_f", [P, COLS])
        ids, load_ids = sb("ids", [P, COLS], int32), sb("load_ids", [P, COLS], int32)
        ids_now, load_now, load_next_ids = sb("ids_now", [P, SA], int32), sb("load_now", [P, SA], int32), sb("load_next_ids", [P, SA], int32)
        r_int, r_int2 = sb("r_int", [P, NT], int32), sb("r_int2", [P, NT], int32)
        r_f = sb("r_f", [P, 4, NT])
        onehot, upto, place = sb("onehot", [P, E, NT]), sb("upto", [P, E, NT]), sb("place", [P, E, NT])
        counts = sb("counts", [P, 2, E, NT])
        n_over = sb("n_over", [P, E, NTOK // SLOT])
        n_slots, ends, base = sb("n_slots", [P, E]), sb("ends", [P, E]), sb("base", [P, E])
        ends_i = sb("ends_i", [P, E], int32)
        pos_f, pos_i = sb("pos_f", [P, NT]), sb("pos_i", [P, NT], int32)
        out_rows = out.rearrange("b s d -> (b s) d")

        amax, sc, side, pv = [[psum(f"{n}{i}", [P, 512]) for i in range(2)] for n in ("amax", "sc", "side", "pv")]

        SEMS = {}

        def sems(names):
            return [SEMS.setdefault(n, sem(n)) for n in names.split()]

        x_loaded, c_loaded, w_loaded, W_loaded, gates_loaded = sems("x_loaded c_loaded w_loaded W_loaded gates_loaded")
        pool_ready, stack_ready, ks_ready, consts_ready, gates_ready = sems("pool_ready stack_ready ks_ready consts_ready gates_ready")
        bn_done, mv_done, ve_done, rstd_done = sems("bn_done mv_done ve_done rstd_done")
        rg_done, xg_done, csum_done, g4_done, gk_done, t1_done, o_done, xb_done, x1_done, src_done, res_done = sems(
            "rg_done xg_done csum_done g4_done gk_done t1_done o_done xb_done x1_done src_done res_done")
        xT_full, cT_full, gv_full, Q_full, V_full, Y_full, sT_full, qk_full, v_full, O_full, A_full = sems(
            "xT_full cT_full gv_full Q_full V_full Y_full sT_full qk_full v_full O_full A_full")
        xT_done, cT_done, sT_done, hi_done, lo_done, v_done, max_done, mneg_done, mT_done = sems(
            "xT_done cT_done sT_done hi_done lo_done v_done max_done mneg_done mT_done")
        m_stored, x1_stored, res_stored, xf_stored, r_loaded = sems("m_stored x1_stored res_stored xf_stored r_loaded")
        m_loaded, qk_stored, stack_loaded = sems("m_loaded0 m_loaded1"), sems("qk_stored0 qk_stored1"), sems("stack0 stack1 stack2 stack3")
        sc_full, exp_done, pv_round, av_done, rec_done, an_done, aT_done = sems("sc_full exp_done pv_round av_done rec_done an_done aT_done")
        r_done, dot_done, xn_done, xfm_done, xf_done, keys_ready = sems("r_done dot_done xn_done xfm_done xf_done keys_ready")
        w2_loaded, route_step, onehot_done, counts_full, ends_ready, tok_id = sems(
            "w2_loaded route_step onehot_done counts_full ends_ready tok_id")
        slot_x_loaded, slot_x1_loaded, slot_ids, slot_free, xb_ready, x1_ready, slot_out, out_stored, slot_T, slot_xh, slot_xT_done = sems(
            "slot_x_loaded slot_x1_loaded slot_ids slot_free xb_ready x1_ready slot_out out_stored slot_T slot_xh slot_xT_done")
        hot_done, ids_full, ids_ready = sems("hot_done ids_full ids_ready")
        hid_full, hid_done, hid_high, hid_split, slot_mv, slot_ve, slot_rstd, z_step, y_full, y_free, w_high, w_split_dve, w_split_pool, x0_ready = sems(
            "hid_full hid_done hid_high hid_split slot_mv slot_ve slot_rstd z_step y_full y_free w_high w_split_dve w_split_pool x0_ready")
        sp_passed, pool_passed = sems("sp_passed pool_passed")
        W_LOADS, W_LOADS2 = 2 + 5 + 8 + 1 + 4, 3 + 16
        CONSTS = 12
        POOL_CONSTS = 4
        W2_LOADS = 2 * (E + 1)

        def pair_of(g, hh):
            return 2 * g + hh // 2, hh % 2

        FIRST = 12
        STEPS = range(FIRST, FIRST + 32)
        SIDE = {12: ("k", 0, 1), 13: ("k", 1, 1), 16: ("cT", 0, 2), 17: ("cT", 1, 2), 19: ("xT", 0, 2), 20: ("xT", 1, 2), 22: ("gv", 0, 2),
                24: ("Q", 0, 2), 25: ("V", 0, 2), 26: ("Q", 1, 2), 27: ("V", 1, 2), 29: ("Y", 0, 2), 30: ("Y", 1, 2),
                34: ("v", 0, 1), 35: ("v", 1, 1), 38: ("O", 0, 0), 39: ("O", 1, 0),
                40: ("sT", 0, 2), 41: ("sT", 1, 2), 42: ("q", 0, 2), 43: ("q", 1, 2)}
        FIRST_PART = [("cT", 0), ("cT", 1), ("xT", 0), ("xT", 1), ("gv", 0), ("Q", 0), ("V", 0), ("Q", 1), ("V", 1), ("Y", 0), ("Y", 1)]
        SECOND_PART = [("sT", 0), ("sT", 1), ("q", 0), ("q", 1), ("k", 0), ("k", 1)]
        LEAD = [t + (0,) for t in FIRST_PART + SECOND_PART]
        LEAD_SIDE = dict(zip(range(-11, 0), [t + (1,) for t in FIRST_PART]))
        LEAD_SIDE.update({1: ("v", 0, 0), 2: ("v", 1, 0), 8: ("sT", 0, 1), 9: ("sT", 1, 1), 10: ("q", 0, 1), 11: ("q", 1, 1)})
        LAST_MAX = 20

        def side_bank(task, i):
            return 1 if task in ("gv", "V") else 0 if task == "Q" else i

        def wait(eng, s, value):
            if isinstance(value, int) and value <= 0:
                return
            eng.wait_ge(s, value)

        def release(task, n, b):
            return {"xT": (xT_done, b * 2 + n + 1), "cT": (cT_done, b * 2 + n + 1), "gv": (g4_done, b + 1),
                    "Q": (t1_done, b * 2 + n + 1), "V": (o_done, b * 2 + n + 1), "Y": (x1_done, b * 2 + n + 1),
                    "sT": (sT_done, b * 2 + n + 1), "q": (lo_done, b * 4 + n + 1), "k": (lo_done, b * 4 + n + 3),
                    "v": (v_done, b * 2 + n + 1), "O": (r_done, b * 2 + n + 1)}[task]

        def runs(task, after, part):
            return after <= {"all": 2, "next": 1, "last": 0}[part]

        def steps_of(part):
            return STEPS if part != "last" else range(FIRST, 32)

        def sp_program(sp):
            def load_weight(n, ap, s):
                sp.dma_start(w_sb[n][:, :, :], ap.rearrange("(k p) n -> p k n", p=P)).then_inc(s, 16)

            def load_batch(b):
                wait(sp, x1_stored, b * 16)
                if not isinstance(b, int):
                    sp.sem_inc(sp_passed, 1)
                wait(sp, src_done, b * TT)
                if not isinstance(b, int):
                    sp.sem_inc(sp_passed, 1)
                sp.dma_start(xin[:, :, :], x[b, :, :].rearrange("(t p) d -> p t d", p=P)).then_inc(x_loaded, 16)
                wait(sp, cT_full, b * 2)
                if not isinstance(b, int):
                    sp.sem_inc(sp_passed, 1)
                sp.dma_start(cin[:, :, :], ctx[b, :, :].rearrange("(t p) d -> p t d", p=P)).then_inc(c_loaded, 16)

            def store_qk(b, j):
                if j == 0:
                    for g in range(G):
                        wait(sp, stack_loaded[g], b * 192)
                        if not isinstance(b, int):
                            sp.sem_inc(sp_passed, 1)
                sp.wait_ge(lo_done, b * 4 + j + 1)
                sp.dma_start(qk_dram[j, :, :, :].rearrange("h p n -> p h n"), HL[:, j % 2, :, :].bitcast(fp32)).then_inc(qk_stored[j % 2], 16)

            def load_stack(b, g, sides="qk"):
                if g == 0:
                    for i in range(2):
                        sp.wait_ge(qk_stored[i], b * 32 + 16 * (1 if sides == "q" else 2))
                    sp.sem_inc(sp_passed, 1)
                wait(sp, sc_full, (b - 1) * 64 + 16 * (g + 1))
                for c in range(2):
                    for i, (qpart, kpart) in enumerate(((0, 0), (1, 0), (0, 1))):
                        at = 48 * c + 16 * i
                        if "q" in sides:
                            sp.dma_start(QS[at:at + DH, 2 * g:2 * g + 2, :].bitcast(fp32), qk_dram[c, qpart, 32 * g:32 * g + 32, :].rearrange("(r d) n -> d r n", d=DH))\
                                .then_inc(stack_loaded[g], 16)
                        if "k" in sides:
                            sp.dma_start(KS[at:at + DH, c, 2 * g:2 * g + 2, :].bitcast(fp32), qk_dram[2 + c, kpart, 32 * g:32 * g + 32, :].rearrange("(r d) n -> d r n", d=DH))\
                                .then_inc(stack_loaded[g], 16)

            def move_maxima(b, g):
                sp.wait_ge(mT_done, b * G + g + 1)
                sp.dma_start(m_dram[g % 2, :, :, :].rearrange("y a i -> a y i"), mT[:, g % 2, :]).then_inc(m_stored, 16)
                sp.wait_ge(m_stored, b * 16 * G + 16 * (g + 1))
                for u in range(2):
                    sp.dma_start(QS[96:100, 2 * g + u, :].bitcast(fp32),
                                 m_dram[g % 2, :, :, :].rearrange("(h u c k) a i -> u c h (k a i)", h=2, u=2, c=2)[u]).then_inc(m_loaded[g % 2], 16)

            load_batch(0)
            sp.dma_start(gqw_col[:, :], gqw.rearrange("(t p) o -> p (t o)", p=P), allow_slow_non_contiguous=True).then_inc(gates_loaded, 16)
            sp.dma_start(gates[:, 0:1], g_xattn.partition_broadcast(P)).then_inc(gates_loaded, 16)
            sp.dma_start(gates[:, 1:2], g_ffn.partition_broadcast(P)).then_inc(gates_loaded, 16)
            sp.dma_start(t1[:, :], gqw.rearrange("s o -> (s o)").partition_broadcast(P)).then_inc(w_loaded, 16)
            sp.dma_start(gkw_row[:, :], gkw.rearrange("s o -> (s o)").partition_broadcast(P)).then_inc(w_loaded, 16)
            for i, v in enumerate((bq, bk, bv, Bq, Bk)):
                sp.dma_start(cols[:, i, :], v.rearrange("(k p) -> p k", p=P), allow_slow_non_contiguous=True).then_inc(w_loaded, 16)
            for i, v in enumerate((bo, Bo, Bv, ln1_g, ln1_b, router_w.rearrange("d o -> (d o)"), ln2_g, ln2_b)):
                sp.dma_start(rows_bc[:, i, :], v.partition_broadcast(P)).then_inc(w_loaded, 16)
            sp.dma_start(rb_col[:, :], router_b.partition_broadcast(P)).then_inc(w_loaded, 16)
            for n, ap in (("wq", wq), ("wk", wk), ("wv", wv), ("wo", wo)):
                load_weight(n, ap, w_loaded)
            for n, ap in (("Wq", Wq), ("Wk", Wk), ("Wv", Wv)):
                load_weight(n, ap, W_loaded)
            for t in range(2):
                for hh in range(HG):
                    for gg in range(2):
                        pair, c = pair_of(2 * t + gg, hh)
                        h = 8 * c + pair
                        r = 32 * hh + 16 * gg
                        sp.dma_start(w_sb["Wo"][r:r + DH, t, :], Wo[h * DH:(h + 1) * DH, :]).then_inc(W_loaded, 16)
            load_batch(1)
            for side_of, js in (("q", (0, 1)), ("k", (2, 3))):
                for j in js:
                    store_qk(0, j)
                sp.wait_ge(stack_ready, 2)
                load_stack(0, 0, side_of)
            for g in range(1, G):
                load_stack(0, g)
            for g in range(2):
                move_maxima(0, g)
            for j in range(2):
                store_qk(1, j)

            def load_expert(e):
                if e == 0:
                    for s, v in ((x1_stored, B * 16), (src_done, B * TT), (cT_full, B * 2), (t1_done, B * 2), (csum_done, B * 2),
                                 (Q_full, B * 2), (V_full, B * 2), (Y_full, B * 2)):
                        sp.wait_ge(s, v)
                    sp.dma_start(b1_col[:, :], b1.rearrange("e (f p) -> p (e f)", p=P), allow_slow_non_contiguous=True).then_inc(w2_loaded, 16)
                    sp.dma_start(b2_bc[:, :, :], b2.partition_broadcast(P)).then_inc(w2_loaded, 16)
                sp.dma_start(W1_sb[:, e * KD:(e + 1) * KD, :], W1[e, :, :].rearrange("(k p) f -> p k f", p=P)).then_inc(w2_loaded, 16)
                sp.dma_start(W2_sb[e][:, :, :], W2[e, :, :].rearrange("(k p) d -> p k d", p=P)).then_inc(w2_loaded, 16)

            def turn(b, part):
                for n in steps_of(part):
                    if part == "all" and n == FIRST:
                        load_batch(b + 2)
                    if (part, n) in (("next", 37), ("last", 13), ("last", 21), ("last", 29)):
                        load_expert((("next", 37), ("last", 13), ("last", 21), ("last", 29)).index((part, n)))
                    if n % 8 == 4:
                        g = (n + 4) // 8
                        if g < G:
                            move_maxima(b, g)
                        elif part != "last":
                            move_maxima(b + 1, g - G)
                    if n in SIDE and SIDE[n][0] in "qk" and runs(*SIDE[n][::2], part):
                        store_qk(b + SIDE[n][2], SIDE[n][1] + 2 * (SIDE[n][0] == "k"))
                    if part != "last":
                        if n in (16, 20, 26, 34):
                            load_stack(b + 1, {16: 0, 20: 1, 26: 2, 34: 3}[n])

            with sp.Fori(0, B - 2) as b:
                turn(b, "all")
            turn(B - 2, "next")
            turn(B - 1, "last")

        def pool_program(pool):
            nc.gpsimd.memset(ident[:, :], 0.0).then_inc(pool_ready, 1)
            nc.gpsimd.memset(mhalf[:, :], -0.5).then_inc(pool_ready, 1)
            pool.wait_ge(pool_ready, 2)
            nc.gpsimd.affine_select(out=ident[:, :], in_=ident[:, :], compare_op=ALU.not_equal, fill=1.0,
                                    base=0, pattern=[[-1, P]], channel_multiplier=1).then_inc(pool_ready, 1)

            def rsqrt(idx, l):
                pool.wait_ge(mv_done, idx * TT + TT)
                pool.sem_inc(pool_passed, 1)
                nc.gpsimd.tensor_scalar(var_eps[:, :], mv[l][:, :, 1], EPS, None, ALU.add).then_inc(ve_done, 1)
                pool.wait_ge(ve_done, idx + 1)
                nc.gpsimd.tensor_tensor(rstd[l][:, :], var_eps[:, :], mhalf[:, :], ALU.pow).then_inc(rstd_done, 1)
                pool.wait_ge(rstd_done, idx + 1)
                pool.sem_inc(pool_passed, 1)

            def first_part(b, idx):
                rsqrt(idx, 0)
                nc.gpsimd.tensor_tensor(rg[:, :], rstd[0][:, :], gqw_col[:, :], ALU.mult).then_inc(rg_done, 1)
                pool.wait_ge(xg_done, b * TT + TT)
                if isinstance(b, int):
                    pool.wait_ge(consts_ready, CONSTS)
                nc.gpsimd.tensor_tensor(xin[:, :, :], xin[:, :, :], rows_bc[:, BO:BO + 1, :].broadcast_to([P, TT, D]), ALU.add).then_inc(xb_done, 1)
                rsqrt(idx + 1, 1)
                pool.dma_start(token_rows(x1_dram, b), xin[:, :, :]).then_inc(x1_stored, 16)

            def token_rows(dram, b):
                return dram[b * S:(b + 1) * S, :].rearrange("(t p) d -> p t d", p=P) if isinstance(b, int) else \
                    dram[bass.ds(b * S, S), :].rearrange("(t p) d -> p t d", p=P)

            def residual(b):
                pool.wait_ge(sT_full, b * 2 + 2)
                nc.gpsimd.tensor_tensor(t_a[:, :, :], t_a[:, :, :], rows_bc[:, BO2:BO2 + 1, :].broadcast_to([P, TT, D]), ALU.add).then_inc(res_done, 1)
                pool.wait_ge(res_done, b + 1)
                pool.sem_inc(pool_passed, 1)
                pool.dma_start(token_rows(res_dram, b), t_a[:, :, :]).then_inc(res_stored, 16)

            def load_residual(b):
                pool.wait_ge(res_stored, b * 16 + 16)
                pool.sem_inc(pool_passed, 1)
                pool.dma_start(t_r[:, :, :], token_rows(res_dram, b)).then_inc(r_loaded, 16)

            def ffn_input(b, idx, more):
                rsqrt(idx, 2)
                nc.gpsimd.tensor_copy(rstds[:, bass.ds(b * TT, TT)], rstd[2][:, :]).then_inc(keys_ready, 1)
                pool.wait_ge(xn_done, b * TT + TT)
                nc.gpsimd.tensor_tensor(t_r[:, :, :], t_r[:, :, :], rows_bc[:, G1:G1 + 1, :].broadcast_to([P, TT, D]), ALU.mult).then_inc(xfm_done, 1)
                pool.wait_ge(xfm_done, b + 1)
                nc.gpsimd.tensor_tensor(t_r[:, :, :], t_r[:, :, :], rows_bc[:, B1:B1 + 1, :].broadcast_to([P, TT, D]), ALU.add).then_inc(xf_done, 1)
                pool.wait_ge(xf_done, b + 1)
                pool.sem_inc(pool_passed, 1)
                pool.dma_start(token_rows(xf_dram, b), t_r[:, :, :]).then_inc(xf_stored, 16)
                if more:
                    pool.wait_ge(xf_stored, b * 16 + 16)
                    load_residual(b + 1)

            nc.gpsimd.memset(KS[0:100, 0, :, :].bitcast(fp32), 0.0).then_inc(stack_ready, 1)
            pool.wait_ge(stack_ready, 1)
            nc.gpsimd.memset(KS[96:98, 0, :, :].bitcast(fp32), 1.0).then_inc(stack_ready, 1)
            pool.wait_ge(stack_ready, 2)
            pool.wait_ge(gates_loaded, 48)
            pool.wait_ge(pool_ready, 3)
            first_part(0, 0)
            residual(0)
            load_residual(0)
            first_part(1, 2)

            def routing_constants():
                pool.wait_ge(pv_round, B * 8 + 2)
                for t, pattern, base_id, per_row in ((thresholds, [[SLOT, NTOK // SLOT]], 0, 0), (lo_is, [[1, P]], 0, 0),
                                                     (hi_is, [[P, COLS]], 0, 0), (token_id, [[P, NT]], -PAD, 1)):
                    nc.gpsimd.iota(t[:, :], pattern, base=base_id, channel_multiplier=per_row, allow_small_or_imprecise_dtypes=True).then_inc(tok_id, 1)
                nc.gpsimd.memset(ones[:, :], 1.0).then_inc(pool_ready, 1)
                pool.wait_ge(pool_ready, POOL_CONSTS)
                nc.gpsimd.affine_select(out=before[:, :], in_=ones[:, :], compare_op=ALU.is_gt, fill=0.0,
                                        base=0, pattern=[[1, P]], channel_multiplier=-1).then_inc(tok_id, 1)
                pool.wait_ge(tok_id, 5)

            def turn(b, part):
                if part != "last":
                    residual(b + 1)
                if part == "all":
                    first_part(b + 2, ln_index(b, 0))
                if part == "last":
                    routing_constants()
                    split_weights(pool, nc.gpsimd, w_split_pool, (2,))
                ffn_input(b, ln_index(b, 2), part != "last")

            with pool.Fori(0, B - 2) as b:
                turn(b, "all")
            turn(B - 2, "next")
            turn(B - 1, "last")
            tail_pool(pool)

        def ln_index(b, l):
            if isinstance(b, int):
                return 4 + 3 * min(b, B - 2) + max(b - (B - 2), 0) + (l if b < B - 2 else 0)
            return b * 3 + 4 + l

        def act_program(act):
            act.wait_ge(gates_loaded, 48)
            nc.scalar.activation(tg[:, :], gates[:, :], ACT.Tanh).then_inc(gates_ready, 1)
            act.sem_inc(exp_done, 2)

            def side_work(task, i, b):
                bank = side[side_bank(task, i)]
                if task == "xT":
                    act.wait_ge(xT_full, b * 2 + i + 1)
                    nc.scalar.activation(xT[:, i, :], bank[:, :], ACT.Identity, accum_out=xsum[:, i:i + 1]).then_inc(xT_done, 1)
                elif task == "cT":
                    act.wait_ge(cT_full, b * 2 + i + 1)
                    nc.scalar.activation(cT[:, i, :], bank[:, :], ACT.Identity).then_inc(cT_done, 1)
                elif task == "sT":
                    act.wait_ge(sT_full, b * 2 + i + 1)
                    nc.scalar.activation(srcT[:, i, :], bank[:, :], ACT.Identity).then_inc(sT_done, 1)
                elif task in "qk":
                    j = i + 2 * (task == "k")
                    act.wait_ge(qk_full, b * 4 + j + 1)
                    wait(act, qk_stored[j % 2], b * 32 + 16 * (j // 2))
                    nc.scalar.activation(HL[:, j % 2, 0, :], bank[:, :], ACT.Identity, bias=cols[:, 3 + j // 2, i:i + 1]).then_inc(hi_done, 1)

            def probabilities(b, n):
                act.wait_ge(pv_round, b * 8 + n // 4 + 1)
                for a in range(2):
                    act.wait_ge(sc_full, b * 64 + 2 * n + a + 1)
                    nc.scalar.activation(probs[:, n % 8, a * 512:(a + 1) * 512], sc[a][:, :], ACT.Exp, scale=SCALE).then_inc(exp_done, 1)

            for task in LEAD:
                side_work(*task)
            for n in range(-12, FIRST):
                if n >= 0:
                    probabilities(0, n)
                if n in LEAD_SIDE:
                    side_work(*LEAD_SIDE[n])

            def turn(b, part):
                for n in steps_of(part):
                    probabilities(b, n)
                    if n in SIDE and runs(*SIDE[n][::2], part):
                        side_work(SIDE[n][0], SIDE[n][1], b + SIDE[n][2])

            with act.Fori(0, B - 2) as b:
                turn(b, "all")
            turn(B - 2, "next")
            turn(B - 1, "last")
            tail_act(act)

        def dve_program(dve):
            dve.sem_inc(pv_round, 2)
            dve.sem_inc(av_done, 2)
            def stats_of(idx, l, src):
                for t in range(TT):
                    nc.vector.bn_stats(stats[:, t, :], src[:, t, :]).then_inc(bn_done, 1)
                dve.wait_ge(bn_done, idx * (TT + 1) + TT)
                dve.sem_inc(bn_done, 1)
                for t in range(TT):
                    nc.vector.bn_aggr(mv[l][:, t, :], stats[:, t, :]).then_inc(mv_done, 1)

            def side_work(task, i, b):
                bank = side[side_bank(task, i)]
                if task == "cT":
                    dve.wait_ge(cT_done, b * 2 + i + 1)
                    nc.vector.tensor_tensor_reduce(out=t1[:, :], in0=cT[:, i, :], in1=gkw_row[:, :], scale=1.0, scalar=0.0,
                                                   op0=ALU.mult, op1=ALU.add, accum_out=csum[:, i:i + 1]).then_inc(csum_done, 1)
                    dve.wait_ge(csum_done, b * 2 + i + 1)
                elif task == "gv":
                    dve.wait_ge(gv_full, b + 1)
                    nc.vector.tensor_tensor(g4[:, :], bank[:, 0:2 * KD], bG[:, :], ALU.add).then_inc(g4_done, 1)
                    dve.wait_ge(g4_done, b + 1)
                    nc.vector.tensor_tensor(gk[:, :], g4[:, 0:KD], g4[:, KD:2 * KD], ALU.mult).then_inc(gk_done, 1)
                    dve.wait_ge(gk_done, b * 2 + 1)
                    nc.vector.tensor_tensor(gkb[:, :], gk[:, :], cols[:, 2, :], ALU.mult).then_inc(gk_done, 1)
                    dve.wait_ge(gk_done, b * 2 + 2)
                elif task == "Q":
                    dve.wait_ge(Q_full, b * 2 + i + 1)
                    nc.vector.scalar_tensor_tensor(t1[:, :], bank[:, :], gkb[:, i:i + 1], C1[:, i, :], ALU.add, ALU.add).then_inc(t1_done, 1)
                    dve.wait_ge(t1_done, b * 2 + i + 1)
                elif task == "V":
                    dve.wait_ge(V_full, b * 2 + i + 1)
                    nc.vector.scalar_tensor_tensor(oT[:, i, :], bank[:, :], gk[:, i:i + 1], t1[:, :], ALU.mult, ALU.add).then_inc(o_done, 1)
                    dve.wait_ge(o_done, b * 2 + i + 1)
                elif task == "Y":
                    dve.wait_ge(Y_full, b * 2 + i + 1)
                    dve.wait_ge(xb_done, b + 1)
                    r = xin[:, 2 * i:2 * i + 2, :].rearrange("p t d -> p (t d)")
                    nc.vector.scalar_tensor_tensor(r, bank[:, :], tg[:, 0:1], r, ALU.mult, ALU.add).then_inc(x1_done, 1)
                elif task in "qk":
                    j = i + 2 * (task == "k")
                    dve.wait_ge(hi_done, b * 4 + j + 1)
                    nc.vector.scalar_tensor_tensor(HL[:, j % 2, 1, :], bank[:, :], cols[:, 3 + j // 2, i:i + 1],
                                                   HL[:, j % 2, 0, :].bitcast(fp32), ALU.add, ALU.subtract).then_inc(lo_done, 1)
                elif task == "v":
                    dve.wait_ge(v_full, b * 2 + i + 1)
                    nc.vector.tensor_tensor(V1[:, 2 * i:2 * i + 2, :, 0:DH], bank[:, :].rearrange("p (t h d) -> p t h d", t=2, h=H),
                                            rows_bc[:, BV:BV + 1, :].rearrange("p o (h d) -> p o h d", h=H).broadcast_to([P, 2, H, DH]), ALU.add).then_inc(v_done, 1)
                elif task == "O":
                    dve.wait_ge(O_full, b * 2 + i + 1)
                    dve.wait_ge(r_loaded, b * 16 + 16)
                    r = t_r[:, 2 * i:2 * i + 2, :].rearrange("p t d -> p (t d)")
                    nc.vector.tensor_tensor(r, bank[:, :], r, ALU.add).then_inc(r_done, 1)

            def scale_x(b):
                dve.wait_ge(rg_done, b + 1)
                wait(dve, res_stored, b * 16)
                for t in range(TT):
                    nc.vector.tensor_scalar(t_a[:, t, :], xin[:, t, :], mv[0][:, t, 0:1], rg[:, t:t + 1], ALU.subtract, ALU.mult).then_inc(xg_done, 1)

            def make_src(b, idx):
                dve.wait_ge(rstd_done, idx + 1)
                for t in range(TT):
                    nc.vector.tensor_scalar(t_a[:, t, :], xin[:, t, :], mv[1][:, t, 0:1], rstd[1][:, t:t + 1], ALU.subtract, ALU.mult).then_inc(src_done, 1)

            def normalise_r(b, idx):
                dve.wait_ge(rstd_done, idx + 1)
                for t in range(TT):
                    nc.vector.tensor_scalar(t_r[:, t, :], t_r[:, t, :], mv[2][:, t, 0:1], rstd[2][:, t:t + 1], ALU.subtract, ALU.mult).then_inc(xn_done, 1)

            def x1_stats(b, idx):
                dve.wait_ge(x1_done, b * 2 + 2)
                stats_of(idx, 1, xin)

            def r_stats(b, idx):
                dve.wait_ge(r_done, b * 2 + 2)
                stats_of(idx, 2, t_r)

            def r_dots(b, idx, tiles):
                for t in tiles:
                    nc.vector.tensor_tensor_reduce(out=t1[:, 0:D], in0=t_r[:, t, :], in1=rows_bc[:, GRW, :], scale=1.0, scalar=0.0,
                                                   op0=ALU.mult, op1=ALU.add, accum_out=kb[:, t:t + 1]).then_inc(dot_done, 1)
                    dve.wait_ge(dot_done, b * (TT + 2) + t + 1)
                if TT - 1 in tiles:
                    dve.wait_ge(mv_done, idx * TT + TT)
                    nc.vector.tensor_copy(dots[:, bass.ds(b * TT, TT)], kb[:, :]).then_inc(dot_done, 1)
                    nc.vector.tensor_copy(means[:, bass.ds(b * TT, TT)], mv[2][:, :, 0]).then_inc(dot_done, 1)

            def row_maxima(b, n):
                for m in (2 * n + 24, 2 * n + 25):
                    dve.wait_ge(A_full, b * 64 + m + 1)
                    nc.vector.reduce_max(mx[:, m % 16:m % 16 + 1], amax[m % 2][:, :], AX.X).then_inc(max_done, 1)
                if n % 8 == 3:
                    k = (n + 13) // 8
                    dve.wait_ge(max_done, b * 64 + 16 * k)
                    nc.vector.tensor_scalar(mneg[:, 0:16], mx[:, :], -1.0, None, ALU.mult).then_inc(mneg_done, 1)
                    dve.wait_ge(mneg_done, b * 2 * G + 2 * k - 1)
                    nc.vector.scalar_tensor_tensor(mneg[:, 16:32], mx[:, :], -1.0, mneg[:, 0:16].bitcast(fp32), ALU.mult, ALU.subtract).then_inc(mneg_done, 1)
                    dve.wait_ge(mneg_done, b * 2 * G + 2 * k)
                    wait(dve, m_stored, b * 16 * G + 16 * (k - 2))
                    nc.vector.transpose(mT[:, (k - 1) % 2, :], mneg[:, :].bitcast(fp32)).then_inc(mT_done, 1)

            def group_out(b, g):
                gg = g % 2
                dve.wait_ge(pv_round, b * 8 + 2 * g + 2 + 2)
                nc.vector.transpose(av[:, :], pv[gg][:, :]).then_inc(av_done, 1)
                dve.wait_ge(av_done, b * G + g + 3)
                av_v = av[:, :].rearrange("p (n d) -> p n d", d=32)
                nc.vector.reciprocal(rec[:, :], av_v[:, :, DH]).then_inc(rec_done, 1)
                dve.wait_ge(rec_done, b * G + g + 1)
                nc.vector.tensor_tensor(an[:, :, gg, :], av_v[:, :, 0:DH], rec[:, :].unsqueeze(2).broadcast_to([P, S // 32, DH]), ALU.mult).then_inc(an_done, 1)
                dve.wait_ge(an_done, b * G + g + 1)
                if gg == 1:
                    nc.vector.transpose(aT[:, g // 2, :], an[:, :, :, :].rearrange("p n g d -> p (n g d)")).then_inc(aT_done, 1)
                    dve.wait_ge(aT_done, b * 2 + g // 2 + 1)

            dve.wait_ge(x_loaded, 16)
            stats_of(0, 0, xin)
            nc.vector.memset(KS[0:48, 1, :, :].bitcast(fp32), 0.0).then_inc(ks_ready, 1)
            scale_x(0)
            nc.vector.memset(KS[96:100, 1, :, :].bitcast(fp32), 1.0).then_inc(ks_ready, 1)
            dve.wait_ge(w_loaded, W_LOADS * 16)
            dve.wait_ge(gates_ready, 1)
            for row, g in ((BO, 0), (G2, 1), (B2, 1)):
                nc.vector.tensor_scalar(rows_bc[:, row, :], rows_bc[:, row, :], tg[:, g:g + 1], None, ALU.mult).then_inc(consts_ready, 1)
            nc.vector.reduce_sum(gsum[:, 0:1], t1[:, :], AX.X).then_inc(consts_ready, 1)
            nc.vector.reduce_sum(gsum[:, 1:2], gkw_row[:, :], AX.X).then_inc(consts_ready, 1)
            for c in range(KD):
                nc.vector.tensor_scalar(C1[:, c, :], t1[:, :], cols[:, 0, c:c + 1], None, ALU.mult).then_inc(consts_ready, 1)
            nc.vector.tensor_tensor(rows_bc[:, GRW, :], rows_bc[:, G1, :], rows_bc[:, RW, :], ALU.mult).then_inc(consts_ready, 1)
            dve.wait_ge(consts_ready, 8)
            for i in range(2):
                nc.vector.tensor_scalar(bG[:, KD * i:KD * (i + 1)], cols[:, i, :], gsum[:, i:i + 1], None, ALU.mult).then_inc(consts_ready, 1)
            nc.vector.reduce_sum(gsum[:, 2:3], rows_bc[:, GRW, :], AX.X).then_inc(consts_ready, 1)
            nc.vector.tensor_tensor_reduce(out=t1[:, 0:D], in0=rows_bc[:, B1, :], in1=rows_bc[:, RW, :], scale=1.0, scalar=rb_col[:, 0:1],
                                           op0=ALU.mult, op1=ALU.add, accum_out=gsum[:, 3:4]).then_inc(consts_ready, 1)
            dve.wait_ge(consts_ready, CONSTS)

            for task in LEAD:
                if task == ("gv", 0, 0):
                    nc.vector.memset(V1[:, :, :, DH:2 * DH], 1.0).then_inc(ks_ready, 1)
                    dve.wait_ge(ks_ready, 3)
                    nc.vector.memset(KS[96:98, 1, :, :].bitcast(fp32), 0.0).then_inc(ks_ready, 1)
                side_work(*task)
                if task == ("Y", 1, 0):
                    x1_stats(0, 1)
                    make_src(0, 1)
            dve.wait_ge(x_loaded, 32)
            stats_of(2, 0, xin)
            scale_x(1)
            for n in range(-12, FIRST):
                row_maxima(0, n)
                if n in LEAD_SIDE:
                    side_work(*LEAD_SIDE[n])
                    if LEAD_SIDE[n] == ("Y", 1, 1):
                        x1_stats(1, 3)
                if n == 2:
                    make_src(1, 3)

            def turn(b, part):
                for n in steps_of(part):
                    if part != "last" or n < LAST_MAX:
                        row_maxima(b, n)
                    if n in SIDE and runs(*SIDE[n][::2], part):
                        side_work(SIDE[n][0], SIDE[n][1], b + SIDE[n][2])
                    if part == "all" and n == 15:
                        dve.wait_ge(x_loaded, b * 16 + 48)
                        stats_of(ln_index(b, 0), 0, xin)
                    if part == "all" and n == 17:
                        scale_x(b + 2)
                    if part == "all" and n == 30:
                        x1_stats(b + 2, ln_index(b, 1))
                    if part == "all" and n == 32:
                        make_src(b + 2, ln_index(b, 1))
                    if n % 8 == 4:
                        group_out(b, (n - 12) // 8)
                    if n == 40:
                        r_stats(b, ln_index(b, 2))
                    if n in (41, 42):
                        r_dots(b, ln_index(b, 2), range(2 * (n - 41), 2 * (n - 40)))
                    if n == 43:
                        normalise_r(b, ln_index(b, 2))
                if part == "last":
                    group_out(b, G - 1)
                    split_weights(dve, nc.vector, w_split_dve, (0, 1))
                    side_work("O", 0, b)
                    side_work("O", 1, b)
                    r_stats(b, ln_index(b, 2))
                    r_dots(b, ln_index(b, 2), range(TT))
                    normalise_r(b, ln_index(b, 2))

            with dve.Fori(0, B - 2) as b:
                turn(b, "all")
            turn(B - 2, "next")
            turn(B - 1, "last")
            tail_dve(dve)

        def pe_program(pe):
            before_side = [None, None]

            def transposes(bank, src, c, full):
                for t in range(TT):
                    last = nc.tensor.transpose(bank[:, t * P:(t + 1) * P], src[:, t, c * P:(c + 1) * P], ident[:, :])
                last.then_inc(full, 1)

            def features_out(bank, w, c, src, full):
                for k in range(KD):
                    last = nc.tensor.matmul(bank[:, :], w[:, k, c * P:(c + 1) * P], src[:, k, :], start=(k == 0), stop=(k == KD - 1))
                last.then_inc(full, 1)

            def tokens_out(bank, w, j, src, full):
                for tt in range(2):
                    t = 2 * j + tt
                    for k in range(KD):
                        last = nc.tensor.matmul(bank[:, tt * D:(tt + 1) * D], src[:, k, t * P:(t + 1) * P], w[:, k, :], start=(k == 0), stop=(k == KD - 1))
                last.then_inc(full, 1)

            def side_work(task, i, b):
                bank = side[side_bank(task, i)]
                if before_side[side_bank(task, i)]:
                    wait(pe, *before_side[side_bank(task, i)])
                before_side[side_bank(task, i)] = release(task, i, b)
                if task == "xT":
                    pe.wait_ge(xg_done, b * TT + TT)
                    transposes(bank, t_a, i, xT_full)
                elif task == "cT":
                    pe.wait_ge(c_loaded, b * 16 + 16)
                    transposes(bank, cin, i, cT_full)
                elif task == "gv":
                    pe.wait_ge(xT_done, b * 2 + 2)
                    pe.wait_ge(csum_done, b * 2 + 2)
                    for a, (w, s) in enumerate((("wq", xsum), ("wk", csum))):
                        for c in range(KD):
                            for k in range(KD):
                                last = nc.tensor.matmul(bank[:, a * KD + c:a * KD + c + 1], w_sb[w][:, k, c * P:(c + 1) * P], s[:, k:k + 1], start=(k == 0), stop=(k == KD - 1))
                    last.then_inc(gv_full, 1)
                elif task == "Q":
                    features_out(bank, w_sb["wq"], i, xT, Q_full)
                elif task == "V":
                    features_out(bank, w_sb["wv"], i, cT, V_full)
                elif task == "Y":
                    pe.wait_ge(o_done, b * 2 + 2)
                    tokens_out(bank, w_sb["wo"], i, oT, Y_full)
                elif task == "sT":
                    pe.wait_ge(src_done, b * TT + TT)
                    transposes(bank, t_a, i, sT_full)
                elif task in "qk":
                    pe.wait_ge(sT_done, b * 2 + 2)
                    features_out(bank, w_sb["W" + task], i, srcT, qk_full)
                elif task == "v":
                    tokens_out(bank, w_sb["Wv"], i, srcT, v_full)
                elif task == "O":
                    pe.wait_ge(aT_done, b * 2 + 2)
                    tokens_out(bank, w_sb["Wo"], i, aT, O_full)

            def scores_for_maxima(b, n):
                for m in (2 * n + 24, 2 * n + 25):
                    g, hh, chunk = m // 16 % G, m // 4 % 4, m % 4
                    pair, c = pair_of(g, hh)
                    if m % 16 == 0:
                        pe.wait_ge(stack_loaded[g], (b + m // 64) * 192 + 192)
                    wait(pe, max_done, b * 64 + m - 1)
                    nc.tensor.matmul(amax[m % 2][:, :], QS[0:96, pair, chunk * P:(chunk + 1) * P], KS[0:96, c, pair, :], start=True, stop=True).then_inc(A_full, 1)

            def scores(b, n):
                g, r = n // 8 % G, n // 4
                pair, c = pair_of(g, n % 4)
                if n % 8 == 0:
                    pe.wait_ge(m_loaded[g % 2], (b + n // 32) * 64 + 32 * (g // 2 + 1))
                for a in range(2):
                    kc = 2 * (r % 2) + a
                    pe.wait_ge(exp_done, b * 64 + 2 * n + a + 1)
                    nc.tensor.matmul(sc[a][:, :], KS[0:100, c, pair, kc * P:(kc + 1) * P], QS[0:100, pair, :], start=True, stop=True).then_inc(sc_full, 1)

            def weighted_values(b, r):
                g = r // 2 % G
                pe.wait_ge(exp_done, b * 64 + 8 * (r + 1) + 2)
                if r % 2 == 0:
                    if r % 8 == 0:
                        pe.wait_ge(v_done, (b + r // 8) * 2 + 2)
                    pe.wait_ge(av_done, b * G + r // 2 + 1)
                for a in range(2):
                    kc = 2 * (r % 2) + a
                    for hh in range(HG):
                        pair, c = pair_of(g, hh)
                        last = nc.tensor.matmul(pv[g % 2][32 * hh:32 * hh + 32, :], V1[:, kc, 8 * c + pair, :],
                                                probs[:, (4 * r + hh) % 8, a * 512:(a + 1) * 512], start=(kc == 0), stop=(kc == TT - 1))
                last.then_inc(pv_round, 1)

            def step(b, n):
                scores(b, n)
                if n % 4 == 3 and not (isinstance(b, int) and b == 0 and n == 3):
                    weighted_values(b, n // 4 - 1)

            pe.wait_ge(pool_ready, 3)
            for task in LEAD:
                if task == ("gv", 0, 0):
                    pe.wait_ge(consts_ready, CONSTS)
                if task == ("sT", 0, 0):
                    pe.wait_ge(W_loaded, W_LOADS2 * 16)
                side_work(*task)
            pe.wait_ge(stack_ready, 2)
            pe.wait_ge(ks_ready, 4)
            for n in range(-12, FIRST):
                if n >= 0:
                    step(0, n)
                scores_for_maxima(0, n)
                if n in LEAD_SIDE:
                    side_work(*LEAD_SIDE[n])

            def turn(b, part):
                for i in range(2):
                    before_side[i] = release("O", i, b - 1) if part == "last" else release("q", i, b + 1)
                for n in steps_of(part):
                    step(b, n)
                    if part != "last" or n < LAST_MAX:
                        scores_for_maxima(b, n)
                    if n in SIDE and runs(*SIDE[n][::2], part):
                        side_work(SIDE[n][0], SIDE[n][1], b + SIDE[n][2])
                if part == "last":
                    weighted_values(b, 7)
                    side_work("O", 0, b)
                    side_work("O", 1, b)

            with pe.Fori(0, B - 2) as b:
                turn(b, "all")
            turn(B - 2, "next")
            turn(B - 1, "last")
            tail_pe(pe)


        hid_bank = [bank[:, 0:SLOT] for bank in (sc[0], sc[1], pv[1], side[1])]
        PARTS = ((0, 0), (1, 0), (0, 1))

        def expert_weights(w):
            e = w // 2
            if w % 2 == 0:
                return [t[:, e * KD:(e + 1) * KD, :] for t in (W1_sb, W1_hi, W1_lo)]
            return [W2_sb[e][:, :, :]] + [t[:, e * NF:(e + 1) * NF, :] for t in (W2_hi, W2_lo)]

        def expert_slots(eng):
            first = 0
            for e in range(E):
                end = eng.value_load(ends_i[0:1, e:e + 1], min_val=e + 1, max_val=MAXS - (E - 1 - e))
                yield e, first, end
                first = end

        def split_weights(eng, ops, done, which):
            for w in which:
                whole, high, low = expert_weights(w)
                eng.wait_ge(w_high, w + 1)
                ops.tensor_tensor(low, whole, high.bitcast(fp32), ALU.subtract).then_inc(done, 1)

        def tail_pool(pool):
            def load_rows(to, dram, at, s):
                for a in range(SA):
                    nc.gpsimd.indirect_dma_start(to[:, a, :], None, dram, bass.IndirectOffsetOnAxis(ap=at[:, a:a + 1], axis=0)).then_inc(s, 16)

            split_weights(pool, nc.gpsimd, w_split_pool, (3, 4))
            pool.wait_ge(x1_stored, B * 16)
            pool.wait_ge(xf_stored, B * 16)
            pool.wait_ge(ids_ready, 2)
            load_rows(slot_x, xf_dram, load_ids, slot_x_loaded)
            nc.gpsimd.iota(ids_now[:, :], [[0, SA]], base=PAD, channel_multiplier=0).then_inc(xb_ready, 1)
            nc.gpsimd.memset(slot_x1[:, :, :], 0.0).then_inc(x1_ready, 1)
            pool.sem_inc(slot_free, 1)

            def finish(n):
                pool.wait_ge(slot_mv, n * SA + SA)
                pool.sem_inc(pool_passed, 1)
                nc.gpsimd.tensor_scalar(var_eps[:, 0:SA], mv[0][:, 0:SA, 1], EPS, None, ALU.add).then_inc(slot_ve, 1)
                pool.wait_ge(slot_ve, n + 1)
                nc.gpsimd.tensor_tensor(rstd[0][:, 0:SA], var_eps[:, 0:SA], mhalf[:, 0:SA], ALU.pow).then_inc(slot_rstd, 1)

            def send(n):
                pool.wait_ge(slot_out, n * SA + SA)
                pool.sem_inc(pool_passed, 1)
                for a in range(SA):
                    nc.gpsimd.indirect_dma_start(out_rows, bass.IndirectOffsetOnAxis(ap=ids_now[:, a:a + 1], axis=0), slot_z[:, a, :], None,
                                                 bounds_check=NTOK - 1, oob_is_err=False).then_inc(out_stored, 16)

            def sent(n):
                pool.wait_ge(out_stored, (n + 1) * 16 * SA)
                pool.sem_inc(slot_free, 1)

            for e, first, end in expert_slots(pool):
                with pool.Fori(first, end) as i:
                    finish(i)
                    pool.wait_ge(y_free, i + 1)
                    pool.sem_inc(pool_passed, 1)
                    pool.wait_ge(slot_x_loaded, (i + 1) * 16 * SA)
                    nc.gpsimd.tensor_tensor(slot_xb[:, :, :], slot_x[:, :, :], b2_bc[:, e:e + 1, :].broadcast_to([P, SA, D]), ALU.add).then_inc(xb_ready, 1)
                    nc.gpsimd.tensor_copy(load_next_ids[:, :], load_ids[:, bass.ds(i * SA + SA, SA)]).then_inc(slot_ids, 1)
                    pool.wait_ge(slot_ids, i * 3 + 1)
                    pool.sem_inc(pool_passed, 1)
                    pool.wait_ge(xb_ready, i + 2)
                    pool.sem_inc(pool_passed, 1)
                    pool.wait_ge(slot_T, i + 1)
                    pool.sem_inc(pool_passed, 1)
                    load_rows(slot_x, xf_dram, load_next_ids, slot_x_loaded)
                    nc.gpsimd.tensor_copy(load_now[:, :], load_ids[:, bass.ds(i * SA, SA)]).then_inc(slot_ids, 1)
                    pool.wait_ge(slot_ids, i * 3 + 2)
                    pool.sem_inc(pool_passed, 1)
                    send(i)
                    load_rows(slot_x1, x1_dram, load_now, slot_x1_loaded)
                    sent(i)
                    nc.gpsimd.tensor_copy(ids_now[:, :], ids[:, bass.ds(i * SA, SA)]).then_inc(slot_ids, 1)
                    pool.wait_ge(slot_ids, i * 3 + 3)
                    pool.sem_inc(pool_passed, 1)
                    pool.wait_ge(slot_x1_loaded, (i + 1) * 16 * SA)
                    nc.gpsimd.tensor_tensor(slot_x1[:, :, :], slot_x1[:, :, :], rows_bc[:, B2:B2 + 1, :].broadcast_to([P, SA, D]), ALU.add).then_inc(x1_ready, 1)
            finish(end)
            send(end)
            sent(end)

        def tail_act(act):
            act.wait_ge(w2_loaded, W2_LOADS * 16)
            act.wait_ge(pv_round, B * 8 + 2)
            for w in range(2 * E):
                whole, high, low = expert_weights(w)
                nc.scalar.activation(high, whole, ACT.Identity).then_inc(w_high, 1)
            act.wait_ge(res_stored, B * 16)
            act.wait_ge(ends_ready, 1)
            act.sem_inc(hid_done, 4)

            def x_high(n):
                act.wait_ge(slot_T, n + 1)
                nc.scalar.activation(slot_xT[:, 0, :, :].rearrange("p k n -> p (k n)"), side[0][:, :], ACT.Identity).then_inc(slot_xh, 1)

            x_high(0)
            for e, first, end in expert_slots(act):
                with act.Fori(first, end) as i:
                    for f in range(NF):
                        q = f // 2
                        act.wait_ge(hid_full, i * NF + f + 1)
                        act.wait_ge(hid_split, i * (NF // 2) + q + 1)
                        nc.scalar.activation(hid[:, q % 2, f % 2, :], hid_bank[f % 4], ACT.Relu, bias=b1_col[:, e * NF + f:e * NF + f + 1]).then_inc(hid_done, 1)
                    x_high(i + 1)

        def tail_dve(dve):
            dve.wait_ge(keys_ready, B)
            dve.wait_ge(dot_done, B * (TT + 2))
            dve.wait_ge(bn_done, B * 3 * (TT + 1))
            step = [0]

            def link(ins):
                step[0] += 1
                ins.then_inc(route_step, 1)
                dve.wait_ge(route_step, step[0])

            link(nc.vector.scalar_tensor_tensor(keys[:, :], means[:, :], gsum[:, 2:3], dots[:, :], ALU.mult, ALU.subtract))
            link(nc.vector.scalar_tensor_tensor(keys[:, :], keys[:, :], -1.0, rstds[:, :], ALU.mult, ALU.mult))
            link(nc.vector.tensor_scalar(keys[:, :], keys[:, :], gsum[:, 3:4], None, ALU.add))
            dve.wait_ge(tok_id, 5)
            link(nc.vector.tensor_copy(r_int[:, :], keys[:, :]))
            link(nc.vector.tensor_copy(r_f[:, 0, :], r_int[:, :]))
            link(nc.vector.tensor_tensor(r_f[:, 1, :], r_f[:, 0, :], keys[:, :], ALU.is_gt))
            link(nc.vector.tensor_tensor(r_f[:, 2, :], r_f[:, 0, :], r_f[:, 1, :], ALU.subtract))
            link(nc.vector.tensor_copy(r_int[:, :], r_f[:, 2, :]))
            link(nc.vector.tensor_scalar(r_int2[:, :], r_int[:, :], E - 1, None, ALU.bitwise_and))
            link(nc.vector.tensor_copy(r_f[:, 3, :], r_int2[:, :]))
            for e in range(E):
                nc.vector.tensor_scalar(onehot[:, e, :], r_f[:, 3, :], float(e), None, ALU.is_equal).then_inc(onehot_done, 1)
            dve.wait_ge(counts_full, 1)
            link(nc.vector.tensor_copy(counts[:, :, :, :].rearrange("p a e t -> p (a e t)"), pv[0][:, 0:2 * E * NT]))
            for e in range(E):
                link(nc.vector.tensor_tensor_scan(upto[:, e, :], ones[:, 0:NT], counts[:, 1, e, :], 0.0, ALU.mult, ALU.add))
            for e in range(E):
                link(nc.vector.tensor_scalar(n_over[:, e, :], thresholds[:, :], upto[:, e, NT - 1:NT], None, ALU.is_lt))
            link(nc.vector.reduce_sum(n_slots[:, :], n_over[:, :, :], AX.X))
            link(nc.vector.tensor_scalar(n_slots[:, :], n_slots[:, :], 1.0, None, ALU.max))
            link(nc.vector.tensor_tensor_scan(ends[:, :], ones[:, 0:E], n_slots[:, :], 0.0, ALU.mult, ALU.add))
            nc.vector.tensor_copy(ends_i[:, :], ends[:, :]).then_inc(ends_ready, 1)
            link(nc.vector.tensor_tensor(base[:, :], ends[:, :], n_slots[:, :], ALU.subtract))
            link(nc.vector.tensor_scalar(base[:, :], base[:, :], float(SLOT), None, ALU.mult))
            link(nc.vector.tensor_tensor(place[:, :, :], upto[:, :, :], counts[:, 1, :, :], ALU.subtract))
            link(nc.vector.tensor_tensor(place[:, :, :], place[:, :, :], counts[:, 0, :, :], ALU.add))
            link(nc.vector.tensor_tensor(place[:, :, :], place[:, :, :], base[:, :].unsqueeze(2).broadcast_to([P, E, NT]), ALU.add))
            link(nc.vector.tensor_tensor(place[:, :, :], place[:, :, :], onehot[:, :, :], ALU.mult))
            link(nc.vector.reduce_sum(pos_f[:, :], place[:, :, :].rearrange("p e t -> p t e"), AX.X))
            link(nc.vector.tensor_copy(pos_i[:, :], pos_f[:, :]))
            link(nc.vector.tensor_scalar(r_int[:, :], pos_i[:, :], P - 1, None, ALU.bitwise_and))
            link(nc.vector.tensor_copy(lo_f[:, :], r_int[:, :]))
            link(nc.vector.tensor_tensor(hi_f[:, :], pos_f[:, :], lo_f[:, :], ALU.subtract))
            link(nc.vector.tensor_tensor(hi_hot[:, 0, :, :], hi_is[:, :].unsqueeze(1).broadcast_to([P, NT, COLS]), hi_f[:, :].unsqueeze(2).broadcast_to([P, NT, COLS]), ALU.is_equal))
            nc.vector.tensor_tensor(hi_hot[:, 1, :, :], hi_hot[:, 0, :, :].bitcast(fp32), token_id[:, :].unsqueeze(2).broadcast_to([P, NT, COLS]), ALU.mult).then_inc(hot_done, 1)
            nc.vector.tensor_tensor(lo_hot[:, :, :], lo_is[:, :].unsqueeze(1).broadcast_to([P, NT, P]), lo_f[:, :].unsqueeze(2).broadcast_to([P, NT, P]), ALU.is_equal).then_inc(hot_done, 1)
            split_weights(dve, nc.vector, w_split_dve, (5, 6, 7))
            dve.wait_ge(ids_full, 1)
            link(nc.vector.tensor_scalar(ids_f[:, :], pv[0][:, 0:COLS], float(PAD), None, ALU.add))
            link(nc.vector.tensor_scalar(load_f[:, :], ids_f[:, :], float(NTOK - 1), None, ALU.min))
            nc.vector.tensor_copy(load_ids[:, :], load_f[:, :]).then_inc(ids_ready, 1)
            nc.vector.tensor_copy(ids[:, :], ids_f[:, :]).then_inc(ids_ready, 1)

            dve.wait_ge(w2_loaded, W2_LOADS * 16)
            dve.wait_ge(ends_ready, 1)
            dve.sem_inc(hid_split, 2)

            def x_low(n):
                dve.wait_ge(slot_xh, n + 1)
                nc.vector.tensor_tensor(slot_xT[:, 1, :, :].rearrange("p k n -> p (k n)"), side[0][:, :], slot_xT[:, 0, :, :].bitcast(fp32).rearrange("p k n -> p (k n)"), ALU.subtract).then_inc(slot_xT_done, 1)

            def split_hidden(i, q):
                dve.wait_ge(hid_done, i * NF + 2 * q + 2 + 4)
                high, low = [h[:, 2 * q:2 * q + 2, :] for h in (hid_hi, hid_lo)]
                nc.vector.tensor_copy(high, hid[:, q % 2, :, :]).then_inc(hid_high, 1)
                dve.wait_ge(hid_high, i * (NF // 2) + q + 1)
                nc.vector.tensor_tensor(low, hid[:, q % 2, :, :], high.bitcast(fp32), ALU.subtract).then_inc(hid_split, 1)

            def residual_stats(n):
                dve.wait_ge(xb_ready, n + 1)
                dve.wait_ge(slot_free, n + 1)
                dve.wait_ge(y_full, n + 1)
                nc.vector.tensor_tensor(slot_z[:, 0, :], amax[0][:, 0:D], slot_xb[:, 0, :], ALU.add).then_inc(z_step, 1)
                nc.vector.tensor_tensor(slot_z[:, 1, :], amax[1][:, 0:D], slot_xb[:, 1, :], ALU.add).then_inc(y_free, 1)
                dve.wait_ge(z_step, n * 8 + 1)
                dve.wait_ge(y_free, n + 1)
                for a in range(SA):
                    nc.vector.bn_stats(stats[:, a, :], slot_z[:, a, :]).then_inc(z_step, 1)
                dve.wait_ge(z_step, n * 8 + 3)
                dve.sem_inc(z_step, 1)
                for a in range(SA):
                    nc.vector.bn_aggr(mv[0][:, a, :], stats[:, a, :]).then_inc(slot_mv, 1)

            def layernorm(n):
                dve.wait_ge(slot_rstd, n + 1)
                for a in range(SA):
                    nc.vector.tensor_scalar(slot_z[:, a, :], slot_z[:, a, :], mv[0][:, a, 0:1], rstd[0][:, a:a + 1], ALU.subtract, ALU.mult).then_inc(z_step, 1)
                for a in range(SA):
                    dve.wait_ge(z_step, n * 8 + 5 + a)
                    nc.vector.tensor_tensor(slot_z[:, a, :], slot_z[:, a, :], rows_bc[:, G2, :], ALU.mult).then_inc(z_step, 1)
                dve.wait_ge(x1_ready, n + 1)
                for a in range(SA):
                    dve.wait_ge(z_step, n * 8 + 7 + a)
                    nc.vector.tensor_tensor(slot_z[:, a, :], slot_z[:, a, :], slot_x1[:, a, :], ALU.add).then_inc(slot_out, 1)

            nc.vector.memset(slot_xb[:, :, :], 0.0).then_inc(x0_ready, 1)
            dve.wait_ge(x0_ready, 1)
            x_low(0)
            for e, first, end in expert_slots(dve):
                with dve.Fori(first, end) as i:
                    residual_stats(i)
                    split_hidden(i, 0)
                    split_hidden(i, 1)
                    layernorm(i)
                    split_hidden(i, 2)
                    split_hidden(i, 3)
                    x_low(i + 1)
            residual_stats(end)
            layernorm(end)

        def tail_pe(pe):
            pe.wait_ge(tok_id, 5)
            pe.wait_ge(onehot_done, E)
            oh = onehot[:, :, :].rearrange("p e t -> p (e t)")
            nc.tensor.matmul(pv[0][:, 0:E * NT], before[:, :], oh, start=True, stop=True)
            nc.tensor.matmul(pv[0][:, E * NT:2 * E * NT], ones[:, :], oh, start=True, stop=True).then_inc(counts_full, 1)
            pe.wait_ge(hot_done, 2)
            pe.wait_ge(route_step, 8)
            for t in range(NT):
                last = nc.tensor.matmul(pv[0][:, 0:COLS], lo_hot[:, t, :], hi_hot[:, 1, t, :], start=(t == 0), stop=(t == NT - 1))
            last.then_inc(ids_full, 1)
            pe.wait_ge(w2_loaded, W2_LOADS * 16)
            pe.wait_ge(ends_ready, 1)
            pe.sem_inc(y_full, 1)

            def transpose_x(n):
                pe.wait_ge(slot_x_loaded, (n + 1) * 16 * SA)
                for k in range(KD):
                    for a in range(SA):
                        last = nc.tensor.transpose(side[0][:, k * SLOT + a * P:k * SLOT + (a + 1) * P], slot_x[:, a, k * P:(k + 1) * P], ident[:, :])
                last.then_inc(slot_T, 1)

            def up(e, i, f):
                pe.wait_ge(hid_done, i * NF + f + 1)
                steps = [(k, part) for k in range(KD) for part in PARTS]
                for k, (xp, wp) in steps:
                    w = (W1_hi, W1_lo)[wp]
                    last = nc.tensor.matmul(hid_bank[f % 4], w[:, e * KD + k, f * P:(f + 1) * P], slot_xT[:, xp, k, :], start=((k, (xp, wp)) == steps[0]), stop=((k, (xp, wp)) == steps[-1]))
                last.then_inc(hid_full, 1)

            def down(e, i, f):
                pe.wait_ge(hid_split, i * (NF // 2) + f // 2 + 3)
                if f == 0:
                    pe.wait_ge(y_free, i + 1)
                for a in range(SA):
                    for xp, wp in PARTS:
                        w = (W2_hi, W2_lo)[wp][:, e * NF + f, :]
                        last = nc.tensor.matmul(amax[a][:, 0:D], (hid_hi, hid_lo)[xp][:, f, a * P:(a + 1) * P], w, start=(f == 0 and (xp, wp) == PARTS[0]), stop=(f == NF - 1 and (xp, wp) == PARTS[-1]))
                if f == NF - 1:
                    last.then_inc(y_full, 1)

            transpose_x(0)
            for e, first, end in expert_slots(pe):
                for done, w in ((w_split_dve, (2, 2, 3, 5)[e]), (w_split_pool, (0, 2, 3, 3)[e])):
                    wait(pe, done, w)
                with pe.Fori(first, end) as i:
                    pe.wait_ge(slot_xT_done, i + 1)
                    for f in range(NF):
                        up(e, i, f)
                        if f >= 4:
                            down(e, i, f - 4)
                    transpose_x(i + 1)
                    for f in range(NF - 4, NF):
                        down(e, i, f)
            pe.wait_ge(slot_free, end + 2)
            pe.wait_ge(slot_x_loaded, (end + 1) * 16 * SA)


        block = es.enter_context(nc.Block())

        @block.sync
        def _(sp):
            sp_program(sp)

        @block.gpsimd
        def _(pool):
            pool_program(pool)

        @block.scalar
        def _(act):
            act_program(act)

        @block.vector
        def _(dve):
            dve_program(dve)

        @block.tensor
        def _(pe):
            pe_program(pe)


_INS = ["x", "ctx_1024", "g_xattn", "g_ffn",
        "L0_xattn_wq", "L0_xattn_bq", "L0_xattn_wk", "L0_xattn_bk", "L0_xattn_wv", "L0_xattn_bv",
        "L0_xattn_gqw", "L0_xattn_gkw", "L0_xattn_wo", "L0_xattn_bo",
        "L0_ffn_Wq", "L0_ffn_bq", "L0_ffn_Wk", "L0_ffn_bk", "L0_ffn_Wv", "L0_ffn_bv", "L0_ffn_Wo", "L0_ffn_bo",
        "L0_ffn_router_w", "L0_ffn_router_b", "L0_ffn_W1", "L0_ffn_b1", "L0_ffn_W2", "L0_ffn_b2",
        "L0_ffn_ln1_g", "L0_ffn_ln1_b", "L0_ffn_ln2_g", "L0_ffn_ln2_b"]


def kernel(**inputs):
    import concourse.bacc as bacc
    from concourse.bass_utils import run_bass_kernel_spmd

    nc = bacc.Bacc("TRN2", target_bir_lowering=False, num_devices=1)
    arrays, args = {}, []
    for name in _INS:
        a = np.ascontiguousarray(inputs[name])
        arrays[f"in_{name}"] = a
        args.append(nc.dram_tensor(f"in_{name}", a.shape, mybir.dt.from_np(a.dtype), kind="ExternalInput").ap())
    out = nc.dram_tensor("out_dram", (4, 512, 256), fp32, kind="ExternalOutput").ap()
    gated_block_kernel(nc, *args, out)
    r = run_bass_kernel_spmd(nc, [arrays], core_ids=[0])
    return r.results[0]["out_dram"]
```
